# Optimizing a Trainium2 kernel written in Bass

```python
import numpy as np
import jax
import jax.numpy as jnp

def _softmax(x, axis=-1):
    return jax.nn.softmax(x, axis=axis)

def _gelu(x):
    return jax.nn.gelu(x, approximate=True)

def _silu(x):
    return jax.nn.silu(x)

def _sigmoid(x):
    return jax.nn.sigmoid(x)

def _layernorm(x, axis=-1, eps=1e-05):
    m = jnp.mean(x, axis=axis, keepdims=True)
    v = jnp.var(x, axis=axis, keepdims=True)
    return (x - m) / jnp.sqrt(v + eps)

def _scatter_add(tgt, idx, src, axis=0):
    return tgt.at[idx].add(src)

def _segment_sum(src, seg, n):
    return jax.ops.segment_sum(src, seg, n)
kernel_name = 'mk_flamingo_gated_d1_seqx_r4_a8939d'

def setup_inputs(seed: int=0):
    np.random.seed(seed)
    _w = jnp.asarray

    def _rec_inputs():
        import jax
        import jax.numpy as jnp
        _rk = jax.random.key(seed)
        x = 7.22e-05 + 1 * jax.random.normal(jax.random.fold_in(_rk, 1), (16, 128, 256), jnp.float32)
        _lenS = 128 - jax.random.randint(jax.random.fold_in(_rk, 7), (16,), 0, max(1, 128 // 4) + 1, jnp.int32)
        _lenS2 = 128 - jax.random.randint(jax.random.fold_in(_rk, 8), (16,), 0, max(1, 128 // 4) + 1, jnp.int32)
        _ctx_768P = jax.random.normal(jax.random.fold_in(_rk, 11), (16, 16, 192), jnp.float32)
        _ctx_768c = jax.random.dirichlet(jax.random.fold_in(_rk, 511), 0.3 * jnp.ones((16,), jnp.float32), (16, 128))
        _ctx_768t = jnp.einsum('bsk,bkd->bsd', _ctx_768c, _ctx_768P)
        _ctx_768t = _ctx_768t * jax.lax.rsqrt(jnp.mean(jnp.square(_ctx_768t)) + 1e-12) * 0.953939
        ctx_768 = 2.09791e-05 + 1.00001 * (_ctx_768t + 0.3 * jax.random.normal(jax.random.fold_in(_rk, 611), (16, 128, 192), jnp.float32))
        _validS = jnp.arange(128)[None, :] < _lenS[:, None]
        _validS2 = jnp.arange(128)[None, :] < _lenS2[:, None]
        _causal = jnp.tril(jnp.ones((128, 128), dtype=bool))
        mask_BxS_bk0 = jnp.logical_not(jnp.broadcast_to(_validS[:, :], (16, 128)))
        _g = jax.random.normal(jax.random.fold_in(_rk, 9001), (2, 1), jnp.float32)
        _g = jnp.sign(_g) * jnp.maximum(jnp.abs(_g), 1.0) + (_g == 0) * 1.0
        g_xattn = _g[0]
        g_ffn = _g[1]
        return (x, ctx_768, mask_BxS_bk0, g_xattn, g_ffn)
    x, ctx_768, mask_BxS_bk0, g_xattn, g_ffn = _rec_inputs()

    def _L0_xattn_setup():
        import jax, jax.numpy as jnp
        import numpy as np
        NUM_HEADS = 16
        key = jax.random.key(seed)
        k1, k2, k3, k4, k5 = jax.random.split(key, 5)
        B, N, C = (4, 512, 256)
        N2, Cy = (256, 192)
        x = jax.random.normal(k1, (B, N, C), dtype=jnp.float32)
        y = jax.random.normal(k2, (B, N2, Cy), dtype=jnp.float32)
        pad_mask = jax.random.randint(k3, (B, N), 0, 2).astype(jnp.bool_)
        Wq = jax.random.normal(k4, (C, C), dtype=jnp.float32) * C ** (-0.5)
        Wkv = jax.random.normal(k5, (2 * C, Cy), dtype=jnp.float32) * Cy ** (-0.5)
        return {'x': x, 'y': y, 'pad_mask': pad_mask, 'Wq': Wq, 'Wkv': Wkv}
    _L0_xattn_all = _L0_xattn_setup()
    _L0_xattn_in = {k: v for k, v in _L0_xattn_all.items() if k in ('Wq', 'Wkv')}
    del _L0_xattn_all

    def _L0_ffn_setup():
        import jax, jax.numpy as jnp
        import numpy as np
        E = 8
        TOPK = 2
        H = 256
        I = 256
        ISH = I * 2
        B, S = (2, 256)
        key = jax.random.key(seed)
        ks = jax.random.split(key, 7)
        s = 0.02
        return {'hidden_states': jax.random.normal(ks[0], (B, S, H), jnp.float32), 'w_router': jax.random.normal(ks[1], (H, E), jnp.float32) * s, 'fc1_w': jax.random.normal(ks[2], (E, H, 2 * I), jnp.float32) * s, 'fc2_w': jax.random.normal(ks[3], (E, I, H), jnp.float32) * s, 'gate_w': jax.random.normal(ks[4], (H, ISH), jnp.float32) * s, 'up_w': jax.random.normal(ks[5], (H, ISH), jnp.float32) * s, 'down_w': jax.random.normal(ks[6], (ISH, H), jnp.float32) * s}
    _L0_ffn_all = _L0_ffn_setup()
    _L0_ffn_in = {k: v for k, v in _L0_ffn_all.items() if k in ('w_router', 'fc1_w', 'fc2_w', 'gate_w', 'up_w', 'down_w')}
    del _L0_ffn_all
    return {'x': x, 'ctx_768': ctx_768, 'mask_BxS_bk0': mask_BxS_bk0, 'g_xattn': g_xattn, 'g_ffn': g_ffn, 'L0_xattn_Wq': _L0_xattn_in['Wq'], 'L0_xattn_Wkv': _L0_xattn_in['Wkv'], 'L0_ffn_w_router': _L0_ffn_in['w_router'], 'L0_ffn_fc1_w': _L0_ffn_in['fc1_w'], 'L0_ffn_fc2_w': _L0_ffn_in['fc2_w'], 'L0_ffn_gate_w': _L0_ffn_in['gate_w'], 'L0_ffn_up_w': _L0_ffn_in['up_w'], 'L0_ffn_down_w': _L0_ffn_in['down_w']}

def reference(x, ctx_768, mask_BxS_bk0, g_xattn, g_ffn, L0_xattn_Wq, L0_xattn_Wkv, L0_ffn_w_router, L0_ffn_fc1_w, L0_ffn_fc2_w, L0_ffn_gate_w, L0_ffn_up_w, L0_ffn_down_w):
    import jax
    import jax.numpy as jnp

    def _L0_xattn_ref(x, y, pad_mask, Wq, Wkv):
        import jax, jax.numpy as jnp
        import numpy as np
        NUM_HEADS = 16
        B, N, C = x.shape
        N2 = y.shape[1]
        H = NUM_HEADS
        d = C // H
        scale = d ** (-0.5)
        q = (x @ Wq.T).reshape(B, N, H, d).transpose(0, 2, 1, 3)
        kv = (y @ Wkv.T).reshape(B, N2, 2, H, d).transpose(2, 0, 3, 1, 4)
        k, v = (kv[0], kv[1])
        attn = jnp.einsum('bhnd,bhmd->bhnm', q * scale, k)
        attn = jnp.where(pad_mask[:, None, :, None], attn, jnp.float32(-1000000000.0))
        attn = jax.nn.softmax(attn, axis=-1)
        out = jnp.einsum('bhnm,bhmd->bhnd', attn, v)
        return out.transpose(0, 2, 1, 3).reshape(B, N, C)

    def _L0_ffn_ref(hidden_states, w_router, fc1_w, fc2_w, gate_w, up_w, down_w):
        import jax, jax.numpy as jnp
        import numpy as np
        E = 8
        TOPK = 2
        H = 256
        I = 256
        ISH = I * 2
        B, S = (2, 256)
        orig_shape = hidden_states.shape
        x = hidden_states.reshape(-1, orig_shape[-1])
        logits = x @ w_router
        top_logits, top_idx = jax.lax.top_k(logits, TOPK)
        scores = jax.nn.softmax(top_logits, axis=-1)
        flat_idx = top_idx.reshape(-1)
        sorted_idx = jnp.argsort(flat_idx)
        permuted = x[sorted_idx // TOPK]
        eid = flat_idx[sorted_idx]
        out_perm = jnp.zeros((permuted.shape[0], orig_shape[-1]), x.dtype)
        for e in range(E):
            m = (eid == e).astype(x.dtype)[:, None]
            h1 = permuted * m @ fc1_w[e]
            proj, gate = jnp.split(h1, 2, axis=-1)
            out_perm = out_perm + jax.nn.silu(proj) * gate @ fc2_w[e]
        unperm = jnp.zeros_like(out_perm).at[sorted_idx].set(out_perm)
        moe_out = (unperm.reshape(-1, TOPK, orig_shape[-1]) * scores[:, :, None]).sum(axis=1)
        moe_out = moe_out.reshape(orig_shape)
        shared = jax.nn.silu(hidden_states @ gate_w) * (hidden_states @ up_w) @ down_w
        return moe_out + shared
    x = x + jnp.tanh(g_xattn[0]) * _L0_xattn_ref(_layernorm(x, axis=-1), ctx_768, mask_BxS_bk0, L0_xattn_Wq, L0_xattn_Wkv)
    x = x + jnp.tanh(g_ffn[0]) * _L0_ffn_ref(_layernorm(x, axis=-1), L0_ffn_w_router, L0_ffn_fc1_w, L0_ffn_fc2_w, L0_ffn_gate_w, L0_ffn_up_w, L0_ffn_down_w)
    return x

_drawn_inputs = setup_inputs


def setup_inputs(seed=0):
    import zlib

    import numpy as np

    out = dict(_drawn_inputs(seed))
    spreads = {}
    factors = {'L0_ffn_w_router': 6.186,
     'L0_ffn_fc1_w': 5.336,
     'L0_ffn_fc2_w': 5.33,
     'L0_ffn_gate_w': 2.735,
     'L0_ffn_up_w': 2.711,
     'L0_ffn_down_w': 2.695}
    for name, (base, spread) in spreads.items():
        noise = np.random.default_rng([zlib.crc32(name.encode()), seed]).standard_normal(out[name].shape)
        drawn = base * np.exp(spread * noise) if base else spread * noise
        out[name] = jnp.asarray(drawn.astype(out[name].dtype))
    for name, factor in factors.items():
        out[name] = (out[name] * factor).astype(out[name].dtype)
    return out
```

```python
from contextlib import ExitStack

import concourse.bass as bass
from concourse import mybir

ALU = mybir.AluOpType
ACT = mybir.ActivationFunctionType
F32 = mybir.dt.float32
BF16 = mybir.dt.bfloat16
I32 = mybir.dt.int32
U32 = mybir.dt.uint32
U8 = mybir.dt.uint8
AX_X = mybir.AxisListType.X

P = 128
HEADS = 16
HD = 16
PIECES = 6
VW = HD + 1
NV = 96
Q_SLOTS = [(0, 0), (1, 1), (2, 2), (3, 0), (4, 1), (5, 0)]
K_SLOTS = [(0, 0), (1, 0), (2, 0), (3, 1), (4, 1), (5, 2)]
EPS = 1e-5


class Group:

    def __init__(self, i, c):
        self.i, self.c = i, c
        self.par = c % 2

    def n(self, k, d=0, plus=0):
        const = k * (self.c + d) + plus
        return const if isinstance(self.i, int) else self.i * (2 * k) + const

    def turns(self, k, d=0):
        const = k * ((self.c + d) // 2 + 1)
        return const if isinstance(self.i, int) else self.i * k + const


def build_program(nc, x, ctx_t, mask, gates, wq, wk, wv, w_router, fc1, fc2, gate_w, up_w, down_w, out):
    T, D = x.shape
    B = T // P
    G = B // 2
    TG = 2 * P
    KC = ctx_t.shape[0]
    E = w_router.shape[2]
    FI = fc1.shape[2] // 2
    ISH = gate_w.shape[2]
    R = T + P
    NULL_ROW = E * R
    NT = (2 * T + E * (P - 1)) // P
    ROW = D + 2
    CH = 4
    NCH = B // CH
    NJ = ISH // P

    xs = nc.dram_tensor("dispatched", (NULL_ROW + P, ROW), F32, kind="Internal").ap()
    ys = nc.dram_tensor("expert_rows", (2 * T, D), F32, kind="Internal").ap()
    x_view = x.rearrange("(b p) d -> p b d", p=P)
    out_view = out.rearrange("(b p) d -> p b d", p=P)
    y_view = ys.rearrange("(k b p) d -> p k b d", k=2, p=P)

    with ExitStack() as es:
        def sb(name, shape, dt=F32):
            return es.enter_context(nc.sbuf_tensor(name, shape, dt))

        def sem(name):
            return es.enter_context(nc.semaphore(name))

        wq_s = sb("wq_s", [P, 2, 2, P])
        wk_s = sb("wk_s", [KC, 2, 2, P])
        wv_s = sb("wv_s", [KC, 2, D])
        wr_s = sb("wr_s", [P, 2, NV])
        fc1_s = sb("fc1_s", [P, 2 * E, 2 * FI])
        fc2_s = sb("fc2_s", [P, 2 * E, D])
        gate_s = sb("gate_s", [P, 2, ISH])
        up_s = sb("up_s", [P, 2, ISH])
        down_s = sb("down_s", [P, NJ, D])
        x_all = sb("x_all", [P, B, D])
        xt_all = sb("xt_all", [P, 2, T])
        ctx_s = sb("ctx_s", [KC, 2, 2, TG])
        xn = sb("xn", [P, 2, D])
        xn_t = sb("xn_t", [P, 2, TG])
        q_pc = sb("q_pc", [P, 3, 2 * TG], BF16)
        k_pc = sb("k_pc", [P, 3, 2 * TG], BF16)
        q_rest = sb("q_rest", [P, 2 * TG])
        k_rest = sb("k_rest", [P, 2 * TG])
        q_st = sb("q_st", [P, 2, HEADS, TG], BF16)
        k_st = sb("k_st", [P, 2, HEADS, TG], BF16)
        v_s = sb("v_s", [P, 2, 2, VW * (HEADS - 1) + NV + 1])
        probs = sb("probs", [P, 4, 8, P])
        row_s = sb("row_s", [P, 2, 4, ROW])
        xt_grp = sb("xt_grp", [P, 2, TG])
        att = sb("att", [P, D])
        ident = sb("ident", [P, P])
        ident_b = sb("ident_b", [P, P], BF16)
        before = sb("before", [P, P], BF16)
        ones_b = sb("ones_b", [P, P], BF16)
        ones_r = sb("ones_r", [1, P])
        mask_u = sb("mask_u", [P, B // 4], U32)
        mask_f = sb("mask_f", [P, B])
        gate_r = sb("gate_r", [1, 2])
        tg = sb("tg", [P, 2])
        mhalf = sb("mhalf", [P, B])
        st1 = sb("st1", [P, B, 6])
        mv1 = sb("mv1", [P, B, 2])
        ve1 = sb("ve1", [P, B])
        rs1 = sb("rs1", [P, B])
        rm1 = sb("rm1", [P, B])
        st2 = sb("st2", [P, 6])
        mv2 = sb("mv2", [P, 2, 2])
        ve2 = sb("ve2", [P, 2])
        rs2 = sb("rs2", [P, 2])
        mx = sb("mx", [P, HEADS])
        mx_pc = sb("mx_pc", [P, 3, HEADS], BF16)
        mx_rest = sb("mx_rest", [P, HEADS])
        mx_t = sb("mx_t", [3 * HEADS, 2, P], BF16)
        rsum = sb("rsum", [P, HEADS])
        rsg = sb("rsg", [P, HEADS])
        lg = sb("lg", [P, 2, 8])
        top = sb("top", [P, 2, 8])
        topi = sb("topi", [P, 2, 8], U32)
        idx_f = sb("idx_f", [P, 4])
        dif = sb("dif", [P, 2, 1])
        ex = sb("ex", [P, 2, 1])
        den = sb("den", [P, 2, 1])
        sc1 = sb("sc1", [P, 2, 1])
        oh = sb("oh", [P, 2, 2, 8])
        cnt = sb("cnt", [P, 2, 8], BF16)
        cum = sb("cum", [P, 2, 8], BF16)
        slot = sb("slot", [P, 2, 8])
        slot_p = sb("slot_p", [P, 2, 2, 8])
        slot_f = sb("slot_f", [P, 4])
        slot_u = sb("slot_u", [P, 2, 4], U32)
        e_i = sb("e_i", [P, 8], I32)
        e_f = sb("e_f", [P, 8])
        er_f = sb("er_f", [P, 8])
        dest_i = sb("dest_i", [P, 4], I32)
        dest_f = sb("dest_f", [P, 4])
        t_i = sb("t_i", [1, NT], I32)
        t_f = sb("t_f", [1, NT])
        tri_f = sb("tri_f", [1, 8, 8])
        c_f = sb("c_f", [1, 8])
        c_up = sb("c_up", [1, 8], I32)
        c_sh = sb("c_sh", [1, 8], I32)
        nt_f = sb("nt_f", [1, 8])
        end_m = sb("end_m", [1, 8, 8])
        end_f = sb("end_f", [1, 8])
        jump = sb("jump", [1, 8])
        past = sb("past", [1, NT, 8])
        past_j = sb("past_j", [1, NT, 8])
        eid_f = sb("eid_f", [1, NT])
        base_f = sb("base_f", [1, NT])
        base_g = sb("base_g", [1, NT])
        eid_i = sb("eid_i", [1, NT], I32)
        base_i = sb("base_i", [1, NT], I32)
        pad_f = sb("pad_f", [1, 8])
        pad_i = sb("pad_i", [1, 8], I32)
        zrow = sb("zrow", [P, ROW])

        k_f = k_st[:, :, :, :].rearrange("p a h t -> p (a h t)").bitcast(F32)
        hid = k_f[:, 0:NJ * CH * P].rearrange("p (j t) -> p j t", j=NJ)
        sil_sh = k_f[:, NJ * CH * P:NJ * CH * P + 2 * CH * P].rearrange("p (r t) -> p r t", r=2)
        q_f = q_st[:, :, :, :].rearrange("p a h t -> p (a h t)").bitcast(F32)
        y_in = q_f[:, :].rearrange("p (r k t d) -> p r k t d", r=2, k=2, t=CH)
        pf = probs[:, :, :, :].rearrange("p a h t -> p (a h t)")
        xs_in = pf[:, 0:4 * ROW].rearrange("p (r c) -> p r c", r=4)
        o0 = 4 * ROW
        xs_t = pf[:, o0:o0 + 2 * 2 * P].rearrange("p (r k t) -> p r k t", r=2, k=2)
        o0 += 2 * 2 * P
        sil = pf[:, o0:o0 + 2 * FI].rearrange("p (r c) -> p r c", r=2)
        o0 += 2 * FI
        act = pf[:, o0:o0 + 2 * FI].rearrange("p (r c) -> p r c", r=2)
        o0 += 2 * FI
        act_t = pf[:, o0:o0 + 2 * 2 * P].rearrange("p (r k t) -> p r k t", r=2, k=2)
        y_out = v_s[:, :, :, :].rearrange("p a b c -> p (a b c)")[:, 0:4 * D].rearrange("p (r c) -> p r c", r=4)
        dst_u = slot_u[:, 0, :]

        ps = es.enter_context(nc.psum_tensor("ps", [P, 8, 512], F32))
        ps_s = ps[:, 0:2, :].rearrange("p b (h t) -> p (b h) t", h=4)
        ps_t = ps[:, 2:4, :].rearrange("p b (h t) -> p (b h) t", h=4)
        ps_o = ps[:, 4, :]
        ps_a = ps[:, 5, :].rearrange("p (k t) -> p k t", k=2)
        ps_b = ps[:, 6, :].rearrange("p (c t) -> p c t", c=2)
        ps_c = ps[:, 7, :]
        ps_x = ps_c.rearrange("p (k t) -> p k t", k=2)
        ps_m = ps_c[0:3 * HEADS, 256:256 + P // 2].bitcast(BF16)

        names = """x_in0 x_in1 x_rest ctx_in0 ctx_in1 wq_in wkv_in small_in wr_in ffn_in fc1_in fc2_in
            const_ok tanh_ok gates_done zero_row_ok v_ones_ok wr_ok mask_ok
            ln1_var rs1_ok rm1_ok xn_ok xnt_done xnt_ok q_done k_done v_done q1_ok q2_ok q3_ok k1_ok k2_ok k3_ok
            qr_ok kr_ok qst0 qst1 kst0 kst1 v_ok s_done max_ok pieces_ok maxt_done maxt_ok rows_in0 rows_in1
            st_done probs_ok pv_done o_read ln2_var rs2_ok xn2_ok dup_ok x2t_done xt_ok xt_out router_done lg_read
            dif_ok ex_ok oh_ok cum_ok pos_done pos_read slots_ok scat0 scat1 total_done table_ok pad_out
            dve_link pool_link act_link
            gu_done sil_ok hid_ok down_done base_ok
            tile_in0 tile_in1 tile_in2 tile_in3 xst_done xst_ok h_done silm_ok act_ok actt_done actt_ok y_done y_ok
            dst_ok ysc0 ysc1 ysc2 ysc3 y_in0 y_in1 fin_ok out_done""".split()
        S = {n: sem(n) for n in names}
        x_in0, x_in1, x_rest, wq_in, wkv_in = S["x_in0"], S["x_in1"], S["x_rest"], S["wq_in"], S["wkv_in"]
        small_in, wr_in, ffn_in, fc1_in, fc2_in = S["small_in"], S["wr_in"], S["ffn_in"], S["fc1_in"], S["fc2_in"]
        ctx_in = [S["ctx_in0"], S["ctx_in1"]]
        const_ok, tanh_ok, gates_done, zero_row_ok = S["const_ok"], S["tanh_ok"], S["gates_done"], S["zero_row_ok"]
        v_ones_ok, wr_ok, mask_ok, ln1_var, rs1_ok, rm1_ok = (S["v_ones_ok"], S["wr_ok"], S["mask_ok"], S["ln1_var"],
                                                              S["rs1_ok"], S["rm1_ok"])
        xn_ok, xnt_done, xnt_ok, q_done, k_done, v_done = (S["xn_ok"], S["xnt_done"], S["xnt_ok"], S["q_done"],
                                                           S["k_done"], S["v_done"])
        q1_ok, q2_ok, q3_ok, k1_ok, k2_ok, k3_ok = (S["q1_ok"], S["q2_ok"], S["q3_ok"], S["k1_ok"], S["k2_ok"],
                                                    S["k3_ok"])
        qr_ok, kr_ok, v_ok, s_done, max_ok, pieces_ok = (S["qr_ok"], S["kr_ok"], S["v_ok"], S["s_done"], S["max_ok"],
                                                         S["pieces_ok"])
        qst, kst, rows_in = [S["qst0"], S["qst1"]], [S["kst0"], S["kst1"]], [S["rows_in0"], S["rows_in1"]]
        maxt_done, maxt_ok, st_done, probs_ok, pv_done = (S["maxt_done"], S["maxt_ok"], S["st_done"], S["probs_ok"],
                                                          S["pv_done"])
        o_read, ln2_var, rs2_ok, xn2_ok, dup_ok = S["o_read"], S["ln2_var"], S["rs2_ok"], S["xn2_ok"], S["dup_ok"]
        x2t_done, xt_ok, xt_out, router_done, lg_read = (S["x2t_done"], S["xt_ok"], S["xt_out"], S["router_done"],
                                                         S["lg_read"])
        dif_ok, ex_ok, oh_ok, pos_done, pos_read, slots_ok = (S["dif_ok"], S["ex_ok"], S["oh_ok"], S["pos_done"],
                                                              S["pos_read"], S["slots_ok"])
        scat = [S["scat0"], S["scat1"]]
        cum_ok = S["cum_ok"]
        total_done, table_ok, pad_out = S["total_done"], S["table_ok"], S["pad_out"]
        dve_link, pool_link = S["dve_link"], S["pool_link"]
        gu_done, sil_ok, hid_ok, down_done, base_ok = (S["gu_done"], S["sil_ok"], S["hid_ok"], S["down_done"],
                                                       S["base_ok"])
        tile_in = [S[f"tile_in{r}"] for r in range(4)]
        ysc = [S[f"ysc{r}"] for r in range(4)]
        y_got = [S["y_in0"], S["y_in1"]]
        xst_done, xst_ok, h_done, silm_ok, act_ok = (S["xst_done"], S["xst_ok"], S["h_done"], S["silm_ok"],
                                                     S["act_ok"])
        actt_done, actt_ok, y_done, y_ok, dst_ok = (S["actt_done"], S["actt_ok"], S["y_done"], S["y_ok"],
                                                    S["dst_ok"])
        fin_ok, out_done = S["fin_ok"], S["out_done"]

        def held(eng, value):
            return value if isinstance(value, int) else eng.to_reg(value)

        def attention_steps(eng, body):
            body(Group(0, -1), cur=False, nxt=True, prev=False)
            body(Group(0, 0), cur=True, nxt=True, prev=False)
            with eng.Fori(0, (G - 2) // 2) as i:
                body(Group(i, 1), cur=True, nxt=True, prev=True)
                body(Group(i, 2), cur=True, nxt=True, prev=True)
            body(Group(0, G - 1), cur=True, nxt=False, prev=True)
            body(Group(0, G), cur=False, nxt=False, prev=True)

        MOE_LOOP = (NT - 3) // 4

        block = es.enter_context(nc.Block())

        @block.sync
        def _(sp):
            sp.dma_start(x_all[:, 0:2, :], x_view[:, 0:2, :]).then_inc(x_in0, 16)
            sp.dma_start(wq_s[:, :, :, :], wq).then_inc(wq_in, 16)
            sp.dma_start(mask_u[:, :], mask).then_inc(small_in, 16)
            sp.dma_start(gate_r[:, :], gates).then_inc(small_in, 16)
            sp.dma_start(wk_s[:, :, :, :], wk).then_inc(wkv_in, 16)
            sp.dma_start(wv_s[:, :, :], wv).then_inc(wkv_in, 16)
            sp.dma_start(x_all[:, 2:4, :], x_view[:, 2:4, :]).then_inc(x_in1, 16)
            sp.wait_ge(wr_ok, 1)
            sp.dma_start(wr_s[:, :, 0:E], w_router).then_inc(wr_in, 16)
            sp.dma_start(x_all[:, 4:B, :], x_view[:, 4:B, :]).then_inc(x_rest, 16)

            sp.sem_inc(xt_out, 16)

            def body(g, cur, nxt, prev):
                pn = 1 - g.par
                if nxt:
                    if cur:
                        sp.wait_ge(v_done, g.n(1))
                    off = g.n(TG, 1)
                    src = ctx_t[:, :, off:off + TG] if isinstance(off, int) else ctx_t[:, :, bass.ds(off, TG)]
                    sp.dma_start(ctx_s[:, pn], src).then_inc(ctx_in[pn], 16)
                    if cur:
                        if g.c >= 1:
                            old, new = held(sp, g.n(4)), held(sp, g.n(1, 2))
                            sp.wait_ge(small_in, 32)
                            sp.wait_ge(st_done, old)
                    for piece, ready in ((0, q1_ok), (1, q2_ok), (2, q3_ok)):
                        sp.wait_ge(ready, g.n(1, 2))
                        for s, p in Q_SLOTS:
                            if p == piece:
                                sp.dma_start(q_st[HD * s:HD * s + HD, pn].rearrange("p h t -> p (h t)"),
                                             q_pc[:, p, :]).then_inc(qst[pn], 16)
                if prev:
                    sp.wait_ge(xt_ok, g.n(1))
                    off = g.n(TG, -1)
                    dst = xt_all[:, :, off:off + TG] if isinstance(off, int) else xt_all[:, :, bass.ds(off, TG)]
                    sp.dma_start(dst, xt_grp[:, :, :]).then_inc(xt_out, 16)
                if nxt:
                    for piece, ready in ((0, k1_ok), (1, k2_ok), (2, k3_ok)):
                        sp.wait_ge(ready, g.n(1, 2))
                        for s, p in K_SLOTS:
                            if p == piece:
                                sp.dma_start(k_st[HD * s:HD * s + HD, pn].rearrange("p h t -> p (h t)"),
                                             k_pc[:, p, :]).then_inc(kst[pn], 16)
                if cur:
                    sp.wait_ge(maxt_ok, g.n(2, 1))
                    sp.dma_start(q_st[6 * HD:6 * HD + 3, g.par, :, P:2 * P], mx_t[:, 1, :]).then_inc(rows_in[1], 16)
                if nxt:
                    sp.wait_ge(maxt_ok, g.n(2, 1, 1))
                    sp.dma_start(q_st[6 * HD:6 * HD + 3, pn, :, 0:P], mx_t[:, 0, :]).then_inc(rows_in[0], 16)

            attention_steps(sp, body)

            sp.wait_ge(zero_row_ok, 1)
            sp.wait_ge(table_ok, 1)
            for e in range(E):
                row = sp.value_load(pad_i[0:1, e:e + 1], min_val=0, max_val=NULL_ROW - P)
                sp.dma_start(xs[bass.ds(row, P), :], zrow[:, :]).then_inc(pad_out, 16)
            sp.wait_ge(scat[0], 64 * (G // 2))
            sp.wait_ge(scat[1], 64 * (G // 2) + 16)
            sp.wait_ge(pad_out, 16 * E)

            def load_tile(t, r, turn):
                row = sp.value_load(base_i[0:1, t:t + 1] if isinstance(t, int) else base_i[0:1, bass.ds(t, 1)],
                                    min_val=0, max_val=NULL_ROW)
                if not (isinstance(turn, int) and turn == 0):
                    sp.wait_ge(y_ok, t - 3)
                    sp.wait_ge(dst_ok, t - 3)
                sp.dma_start(xs_in[:, r, :], xs[bass.ds(row, P), :]).then_inc(tile_in[r], 16)

            for t in range(4):
                load_tile(t, t, 0)
            with sp.Fori(1, MOE_LOOP) as i:
                for r in range(4):
                    load_tile(i * 4 + r, r, i)
            for t in range(4 * MOE_LOOP, NT):
                load_tile(t, t % 4, MOE_LOOP)

            for r in range(4):
                sp.wait_ge(ysc[r], 16 * len(range(r, NT, 4)))
            for c in range(NCH):
                if c >= 2:
                    sp.wait_ge(fin_ok, c - 1)
                sp.dma_start(y_in[:, c % 2, 0], y_view[:, 0, CH * c:CH * c + CH, :]).then_inc(y_got[c % 2], 16)
                sp.dma_start(y_in[:, c % 2, 1], y_view[:, 1, CH * c:CH * c + CH, :]).then_inc(y_got[c % 2], 16)
                if c >= 1:
                    sp.wait_ge(fin_ok, c)
                    sp.dma_start(out_view[:, CH * (c - 1):CH * c, :],
                                 x_all[:, CH * (c - 1):CH * c, :]).then_inc(out_done, 16)
            sp.wait_ge(fin_ok, NCH)
            sp.dma_start(out_view[:, B - CH:B, :], x_all[:, B - CH:B, :]).then_inc(out_done, 16)
            sp.wait_ge(out_done, 16 * NCH)

        @block.gpsimd
        def _(pool):
            nc.gpsimd.memset(wr_s[:, :, :], 0.0).then_inc(wr_ok, 1)
            nc.gpsimd.memset(ident[:, :], 0.0).then_inc(pool_link, 1)
            nc.gpsimd.memset(ident_b[:, :], 0.0).then_inc(pool_link, 1)
            nc.gpsimd.memset(before[:, :], 1.0).then_inc(pool_link, 1)
            nc.gpsimd.memset(tri_f[:, :, :], 1.0).then_inc(pool_link, 1)
            nc.gpsimd.memset(mhalf[:, :], -0.5).then_inc(pool_link, 1)
            pool.wait_ge(pool_link, 5)
            nc.gpsimd.affine_select(out=ident[:, :], in_=ident[:, :], compare_op=ALU.not_equal, fill=1.0,
                                    base=0, pattern=[[-1, P]], channel_multiplier=1).then_inc(const_ok, 1)
            nc.gpsimd.affine_select(out=ident_b[:, :], in_=ident_b[:, :], compare_op=ALU.not_equal, fill=1.0,
                                    base=0, pattern=[[-1, P]], channel_multiplier=1).then_inc(const_ok, 1)
            nc.gpsimd.affine_select(out=before[:, :], in_=before[:, :], compare_op=ALU.is_gt, fill=0.0,
                                    base=0, pattern=[[1, P]], channel_multiplier=-1).then_inc(const_ok, 1)
            nc.gpsimd.affine_select(out=tri_f[:, :, :], in_=tri_f[:, :, :], compare_op=ALU.is_ge, fill=0.0,
                                    base=0, pattern=[[1, 8], [-1, 8]], channel_multiplier=0).then_inc(const_ok, 1)
            nc.gpsimd.iota(e_i[:, :], pattern=[[1, 8]], base=0, channel_multiplier=0).then_inc(const_ok, 1)
            nc.gpsimd.iota(t_i[:, :], pattern=[[1, NT]], base=0, channel_multiplier=0).then_inc(const_ok, 1)
            nc.gpsimd.iota(dest_i[:, :], pattern=[[-P, 2], [-T, 2]], base=2 * T,
                           channel_multiplier=-1).then_inc(const_ok, 1)
            nc.gpsimd.memset(zrow[:, :], 0.0).then_inc(zero_row_ok, 1)
            pool.wait_ge(zero_row_ok, 1)
            nc.gpsimd.dma_start(xs[NULL_ROW:NULL_ROW + P, :], zrow[:, :]).then_inc(scat[1], 16)
            pool.wait_ge(ln1_var, 1)
            nc.gpsimd.tensor_tensor(rs1[:, 0:2], ve1[:, 0:2], mhalf[:, 0:2], ALU.pow).then_inc(rs1_ok, 1)
            pool.wait_ge(ln1_var, 2)
            nc.gpsimd.tensor_tensor(rs1[:, 2:B], ve1[:, 2:B], mhalf[:, 2:B], ALU.pow).then_inc(rs1_ok, 1)

            def body(g, cur, nxt, prev):
                if prev:
                    pool.wait_ge(ln2_var, g.n(2))
                    nc.gpsimd.tensor_tensor(rs2[:, 1:2], ve2[:, 1:2], mhalf[:, 0:1], ALU.pow).then_inc(rs2_ok, 1)
                if nxt:
                    pool.wait_ge(q2_ok, g.n(1, 2))
                    if cur:
                        pool.wait_ge(qst[g.par], g.turns(96))
                    nc.gpsimd.tensor_tensor(q_pc[:, 2, :], q_rest[:, :], q_pc[:, 1, :],
                                            ALU.subtract).then_inc(q3_ok, 1)
                    pool.wait_ge(k2_ok, g.n(1, 2))
                    if cur:
                        pool.wait_ge(kst[g.par], g.turns(96))
                    nc.gpsimd.tensor_tensor(k_pc[:, 2, :], k_rest[:, :], k_pc[:, 1, :],
                                            ALU.subtract).then_inc(k3_ok, 1)
                if cur:
                    pool.wait_ge(ln2_var, g.n(2, 0, 1))
                    nc.gpsimd.tensor_tensor(rs2[:, 0:1], ve2[:, 0:1], mhalf[:, 0:1], ALU.pow).then_inc(rs2_ok, 1)
                if prev:
                    pp = 1 - g.par
                    places, rows = held(pool, g.n(1)), held(pool, g.n(2))
                    pool.wait_ge(pool_link, 5)
                    pool.wait_ge(slots_ok, places)
                    pool.wait_ge(dup_ok, rows)
                    for m in range(4):
                        nc.gpsimd.indirect_dma_start(
                            xs, bass.IndirectOffsetOnAxis(slot_u[:, pp, m:m + 1], 0), row_s[:, pp, m, :], None,
                            bounds_check=NULL_ROW + P - 1, oob_is_err=False).then_inc(scat[pp], 16)

            attention_steps(pool, body)

            def scatter(t, r, turn):
                tiles = held(pool, t + 1)
                pool.wait_ge(pool_link, 5)
                pool.wait_ge(y_ok, tiles)
                pool.wait_ge(dst_ok, tiles)
                nc.gpsimd.indirect_dma_start(
                    ys, bass.IndirectOffsetOnAxis(dst_u[:, r:r + 1], 0), y_out[:, r, :], None,
                    bounds_check=2 * T - 1, oob_is_err=False).then_inc(ysc[r], 16)

            with pool.Fori(0, MOE_LOOP) as i:
                for r in range(4):
                    scatter(i * 4 + r, r, i)
            for t in range(4 * MOE_LOOP, NT):
                scatter(t, t % 4, MOE_LOOP)

        @block.scalar
        def _(sa):
            sa.dma_start(gate_s[:, :, :], gate_w).then_inc(ffn_in, 16)
            sa.dma_start(up_s[:, :, :], up_w).then_inc(ffn_in, 16)
            sa.dma_start(down_s[:, :, :], down_w).then_inc(ffn_in, 16)
            sa.wait_ge(gates_done, 1)
            nc.scalar.activation(tg[:, :], ps_c[:, 0:2], ACT.Tanh).then_inc(tanh_ok, 1)

            def body(g, cur, nxt, prev):
                pn = 1 - g.par

                def exp(j, h):
                    sa.wait_ge(st_done, g.n(4, 0, 2 * j + h + 1))
                    if not (isinstance(g.i, int) and g.c == 0):
                        sa.wait_ge(pv_done, g.n(4, -1, 2 * j + h + 1))
                    nc.scalar.activation(probs[:, 2 * j + h], ps_t, ACT.Exp, scale=HD ** -0.5).then_inc(probs_ok, 1)

                if nxt:
                    sa.wait_ge(xnt_done, g.n(1, 2))
                    if cur:
                        sa.wait_ge(q_done, g.n(1, 1))
                    nc.scalar.activation(xn_t[:, :, :], ps_a, ACT.Copy).then_inc(xnt_ok, 1)
                if cur:
                    exp(0, 0)
                if prev:
                    sa.wait_ge(xn2_ok, g.n(2))
                    nc.scalar.activation(row_s[:, pn, 3, 0:D], row_s[:, pn, 2, 0:D], ACT.Copy).then_inc(dup_ok, 1)
                if nxt:
                    sa.wait_ge(q_done, g.n(1, 2))
                    if cur:
                        sa.wait_ge(qst[g.par], g.turns(96))
                    nc.scalar.activation(q_pc[:, 0, :], ps[:, 6, :], ACT.Copy).then_inc(q1_ok, 1)
                if cur:
                    exp(0, 1)
                if nxt:
                    sa.wait_ge(qr_ok, g.n(1, 2))
                    nc.scalar.activation(q_pc[:, 1, :], q_rest[:, :], ACT.Copy).then_inc(q2_ok, 1)
                if prev:
                    sa.wait_ge(x2t_done, g.n(1))
                    sa.wait_ge(xt_out, g.n(16))
                    nc.scalar.activation(xt_grp[:, :, :], ps_x, ACT.Copy).then_inc(xt_ok, 1)
                if nxt:
                    sa.wait_ge(k_done, g.n(1, 2))
                    if cur:
                        sa.wait_ge(kst[g.par], g.turns(96))
                    nc.scalar.activation(k_pc[:, 0, :], ps[:, 6, :], ACT.Copy).then_inc(k1_ok, 1)
                    sa.wait_ge(kr_ok, g.n(1, 2))
                    nc.scalar.activation(k_pc[:, 1, :], k_rest[:, :], ACT.Copy).then_inc(k2_ok, 1)
                if prev:
                    sa.wait_ge(dif_ok, g.n(1))
                    nc.scalar.activation(ex[:, :, :], dif[:, :, :], ACT.Exp).then_inc(ex_ok, 1)
                if cur:
                    sa.wait_ge(maxt_done, g.n(2, 1))
                    if not (isinstance(g.i, int) and g.c == 0):
                        sa.wait_ge(rows_in[1], g.n(16))
                    nc.scalar.activation(mx_t[:, 1, :], ps_m, ACT.Copy).then_inc(maxt_ok, 1)
                if nxt:
                    sa.wait_ge(v_done, g.n(1, 2))
                    if cur and not (isinstance(g.i, int) and g.c == 0):
                        sa.wait_ge(pv_done, g.n(4))
                    if not cur:
                        sa.wait_ge(v_ones_ok, 1)
                    dst = v_s[:, pn, :, 0:VW * HEADS].rearrange("p j (h e) -> p j h e", e=VW)[:, :, :, 0:HD]
                    nc.scalar.activation(dst, ps[:, 5, :].rearrange("p (j h e) -> p j h e", j=2, h=HEADS),
                                         ACT.Copy).then_inc(v_ok, 1)
                if cur:
                    exp(1, 0)
                    exp(1, 1)
                    sa.wait_ge(xn2_ok, g.n(2, 0, 1))
                    nc.scalar.activation(row_s[:, g.par, 1, 0:D], row_s[:, g.par, 0, 0:D],
                                         ACT.Copy).then_inc(dup_ok, 1)
                if nxt:
                    sa.wait_ge(maxt_done, g.n(2, 1, 1))
                    if cur:
                        sa.wait_ge(rows_in[0], g.n(16, 1))
                    nc.scalar.activation(mx_t[:, 0, :], ps_m, ACT.Copy).then_inc(maxt_ok, 1)
                if nxt and not cur:
                    sa.dma_start(fc1_s[:, :, :], fc1).then_inc(fc1_in, 16)
                    sa.dma_start(fc2_s[:, :, :], fc2).then_inc(fc2_in, 16)

            attention_steps(sa, body)

            def shared(c):
                for j in range(NJ):
                    sa.wait_ge(gu_done, c * NJ + j + 1)
                    if j >= 2 or not isinstance(c, int):
                        sa.wait_ge(hid_ok, c * NJ + j - 1)
                    nc.scalar.activation(sil_sh[:, j % 2], ps[:, j % 2, :], ACT.Silu).then_inc(sil_ok, 1)

            shared(0)

            def expert(t, r):
                par = r % 2

                def first():
                    return isinstance(t, int) and t < 2

                sa.wait_ge(h_done, t + 1)
                if not first():
                    sa.wait_ge(act_ok, t - 1)
                nc.scalar.activation(sil[:, par], ps[:, 2 + par, 0:FI], ACT.Silu).then_inc(silm_ok, 1)

            def expert_x(t, r):
                par = r % 2
                sa.wait_ge(xst_done, t + 1)
                if not (isinstance(t, int) and t < 2):
                    sa.wait_ge(h_done, t - 1)
                nc.scalar.activation(xs_t[:, par], ps[:, par, 0:2 * P].rearrange("p (k t) -> p k t", k=2),
                                     ACT.Copy).then_inc(xst_ok, 1)

            def expert_y(t, r):
                sa.wait_ge(y_done, t + 1)
                if not (isinstance(t, int) and t < 4):
                    sa.wait_ge(ysc[r], (t // 4) * 16 if isinstance(t, int) else t4(t))
                nc.scalar.activation(y_out[:, r, :], ps[:, 5 + r % 2, 0:D], ACT.Copy,
                                     scale=xs_in[:, r, D + 1:D + 2]).then_inc(y_ok, 1)

            turn = [None]

            def t4(_):
                return turn[0] * 16

            expert_x(0, 0)
            expert_x(1, 1)
            expert(0, 0)
            for r in range(4):
                expert_x(r + 2, (r + 2) % 4)
                expert(r + 1, (r + 1) % 4)
                expert_y(r, r)
            with sa.Fori(1, MOE_LOOP) as i:
                turn[0] = i
                for r in range(4):
                    expert_x(i * 4 + r + 2, (r + 2) % 4)
                    expert(i * 4 + r + 1, (r + 1) % 4)
                    expert_y(i * 4 + r, r)
            for t in range(4 * MOE_LOOP, NT):
                if t + 2 < NT:
                    expert_x(t + 2, (t + 2) % 4)
                if t + 1 < NT:
                    expert(t + 1, (t + 1) % 4)
                expert_y(t, t % 4)

            with sa.Fori(1, NCH) as c:
                shared(c)

        @block.vector
        def _(ve):
            links = [0]

            def link(ins):
                links[0] += 1
                ins.then_inc(dve_link, 1)
                ve.wait_ge(dve_link, links[0])

            def relink():
                if links[0]:
                    ve.wait_ge(dve_link, links[0])
                    ve.sem_clear(dve_link)
                    links[0] = 0

            nc.vector.memset(ones_r[:, :], 1.0).then_inc(const_ok, 1)
            nc.vector.memset(ones_b[:, :], 1.0).then_inc(const_ok, 1)
            nc.vector.memset(cum[:, :, :], 0.0).then_inc(cum_ok, 1)
            nc.vector.memset(k_st[96:99, :, :, :], 1.0).then_inc(const_ok, 1)
            nc.vector.memset(v_s[:, :, :, :], 1.0).then_inc(v_ones_ok, 1)

            def stats(b0, b1):
                for b in range(b0, b1):
                    nc.vector.bn_stats(st1[:, b, :], x_all[:, b, :]).then_inc(dve_link, 1)
                links[0] += b1 - b0
                ve.wait_ge(dve_link, links[0])
                for b in range(b0, b1):
                    nc.vector.bn_aggr(mv1[:, b, :], st1[:, b, :]).then_inc(dve_link, 1)
                links[0] += b1 - b0
                ve.wait_ge(dve_link, links[0])
                nc.vector.tensor_scalar(ve1[:, b0:b1], mv1[:, b0:b1, 1], EPS, None, ALU.add).then_inc(ln1_var, 1)

            ve.wait_ge(x_in0, 16)
            stats(0, 2)
            ve.wait_ge(small_in, 32)
            link(nc.vector.tensor_copy(mask_f[:, :], mask_u[:, :].bitcast(U8)))
            ve.wait_ge(rs1_ok, 1)
            link(nc.vector.tensor_tensor(rm1[:, 0:2], rs1[:, 0:2], mask_f[:, 0:2], ALU.mult))

            def norm1(g):
                b = g.n(2, 1)
                for j in range(2):
                    at = b + j
                    if isinstance(at, int):
                        src, mean, rstd = x_all[:, at, :], mv1[:, at, 0:1], rm1[:, at:at + 1]
                    else:
                        src = x_all[:, bass.ds(at, 1), :].rearrange("p a d -> p (a d)")
                        mean = mv1[:, bass.ds(at, 1), 0:1].rearrange("p a d -> p (a d)")
                        rstd = rm1[:, bass.ds(at, 1)]
                    nc.vector.tensor_scalar(xn[:, j, :], src, mean, rstd, ALU.subtract, ALU.mult).then_inc(xn_ok, 1)

            def maxima(g, j, h, d=0):
                ve.wait_ge(s_done, g.n(4, d, 2 * j + h + 1))
                nc.vector.reduce_max(mx[:, 8 * h:8 * h + 8], ps_s, AX_X).then_inc(max_ok, 1)

            def pieces(g, j, d=0):
                ve.wait_ge(max_ok, g.n(4, d, 2 * j + 2))
                if not (isinstance(g.i, int) and g.c + d == 0 and j == 0):
                    ve.wait_ge(maxt_done, g.n(2, d, j))
                link(nc.vector.tensor_scalar(mx_pc[:, 0, :], mx[:, :], -1.0, None, ALU.mult))
                link(nc.vector.scalar_tensor_tensor(mx_rest[:, :], mx[:, :], -1.0, mx_pc[:, 0, :],
                                                    ALU.mult, ALU.subtract))
                link(nc.vector.tensor_copy(mx_pc[:, 1, :], mx_rest[:, :]))
                nc.vector.tensor_tensor(mx_pc[:, 2, :], mx_rest[:, :], mx_pc[:, 1, :],
                                        ALU.subtract).then_inc(pieces_ok, 1)

            def attended(g, j):
                ve.wait_ge(pv_done, g.n(4, 0, 2 * j + 2))
                o = ps_o[:, 0:VW * HEADS].rearrange("p (h e) -> p h e", e=VW)
                link(nc.vector.reciprocal(rsum[:, :], o[:, :, HD]))
                link(nc.vector.tensor_scalar(rsg[:, :], rsum[:, :], tg[:, 0:1], None, ALU.mult))
                nc.vector.tensor_tensor(att[:, :].rearrange("p (h e) -> p h e", e=HD), o[:, :, 0:HD],
                                        rsg[:, :].unsqueeze(2).broadcast_to([P, HEADS, HD]),
                                        ALU.mult).then_inc(o_read, 1)
                ve.wait_ge(o_read, g.n(2, 0, j + 1))
                b = g.n(2, 0, j)
                xb = x_all[:, b, :] if isinstance(b, int) else x_all[:, bass.ds(b, 1), :].rearrange("p a d -> p (a d)")
                link(nc.vector.tensor_tensor(xb, xb, att[:, :], ALU.add))
                link(nc.vector.bn_stats(st2[:, :], xb))
                link(nc.vector.bn_aggr(mv2[:, j, :], st2[:, :]))
                nc.vector.tensor_scalar(ve2[:, j:j + 1], mv2[:, j, 1:2], EPS, None, ALU.add).then_inc(ln2_var, 1)

            def norm2(g, j, d=0):
                par = (g.c + d) % 2
                ve.wait_ge(rs2_ok, g.n(2, d, j + 1))
                if j == 0 and g.c + d >= 1:
                    ve.wait_ge(scat[par], g.turns(64, d - 2) + 16 * par)
                b = g.n(2, d, j)
                xb = x_all[:, b, :] if isinstance(b, int) else x_all[:, bass.ds(b, 1), :].rearrange("p a d -> p (a d)")
                nc.vector.tensor_scalar(row_s[:, par, 2 * j, 0:D], xb, mv2[:, j, 0:1], rs2[:, j:j + 1],
                                        ALU.subtract, ALU.mult).then_inc(xn2_ok, 1)

            def body(g, cur, nxt, prev):
                pp = 1 - g.par
                if prev:
                    norm2(g, 1, -1)
                if nxt:
                    if cur:
                        ve.wait_ge(xnt_done, g.n(1, 1))
                    norm1(g)
                if nxt and not cur:
                    ve.wait_ge(tanh_ok, 1)
                    ve.wait_ge(const_ok, 10)
                    nc.vector.tensor_copy(e_f[:, :], e_i[:, :]).then_inc(dve_link, 1)
                    nc.vector.tensor_copy(t_f[:, :], t_i[:, :]).then_inc(dve_link, 1)
                    links[0] += 2
                    link(nc.vector.tensor_copy(dest_f[:, :], dest_i[:, :]))
                    link(nc.vector.tensor_scalar(er_f[:, :], e_f[:, :], float(R), None, ALU.mult))
                if nxt:
                    ve.wait_ge(q1_ok, g.n(1, 2))
                    if cur:
                        ve.wait_ge(q3_ok, g.n(1, 1))
                    nc.vector.tensor_tensor(q_rest[:, :], ps[:, 6, :], q_pc[:, 0, :], ALU.subtract).then_inc(qr_ok, 1)
                if cur:
                    maxima(g, 1, 0)
                if prev:
                    ve.wait_ge(router_done, g.n(1))
                    nc.vector.tensor_copy(lg[:, :, :], ps_c[:, 0:2 * NV].rearrange("p (j e) -> p j e", j=2)[:, :, 0:8]
                                          ).then_inc(lg_read, 1)
                    ve.wait_ge(const_ok, 10)
                    ve.wait_ge(lg_read, g.n(1))
                    nc.vector.max(top[:, 0, :], lg[:, 0, :]).then_inc(dve_link, 1)
                    links[0] += 1
                    link(nc.vector.max(top[:, 1, :], lg[:, 1, :]))
                    nc.vector.tensor_tensor(dif[:, :, :], top[:, :, 1:2], top[:, :, 0:1],
                                            ALU.subtract).then_inc(dif_ok, 1)
                    nc.vector.max_index(topi[:, 0, :], top[:, 0, :], lg[:, 0, :]).then_inc(dve_link, 1)
                    links[0] += 1
                    link(nc.vector.max_index(topi[:, 1, :], top[:, 1, :], lg[:, 1, :]))
                    link(nc.vector.tensor_copy(idx_f[:, :].rearrange("p (j k) -> p j k", j=2), topi[:, :, 0:2]))
                    link(nc.vector.tensor_tensor(oh[:, :, :, :].rearrange("p j k e -> p (j k) e"),
                                                 e_f[:, :].unsqueeze(1).broadcast_to([P, 4, 8]),
                                                 idx_f[:, :].unsqueeze(2).broadcast_to([P, 4, 8]), ALU.is_equal))
                    ve.wait_ge(cum_ok, g.n(1))
                    link(nc.vector.tensor_tensor(cnt[:, :, :], oh[:, :, 0, :], oh[:, :, 1, :], ALU.add))
                    nc.vector.tensor_tensor(cum[:, 1, :], cum[:, 0, :], cnt[:, 0, :], ALU.add).then_inc(oh_ok, 1)
                if nxt:
                    ve.wait_ge(k1_ok, g.n(1, 2))
                    if cur:
                        ve.wait_ge(k3_ok, g.n(1, 1))
                    nc.vector.tensor_tensor(k_rest[:, :], ps[:, 6, :], k_pc[:, 0, :], ALU.subtract).then_inc(kr_ok, 1)
                if nxt and not cur:
                    ve.wait_ge(x_in1, 16)
                    ve.wait_ge(x_rest, 16)
                    stats(2, B)
                    ve.wait_ge(rs1_ok, 2)
                    link(nc.vector.tensor_tensor(rm1[:, 2:B], rs1[:, 2:B], mask_f[:, 2:B], ALU.mult))
                if cur:
                    maxima(g, 1, 1)
                    pieces(g, 1)
                if prev:
                    ve.wait_ge(ex_ok, g.n(1))
                    link(nc.vector.tensor_scalar(den[:, :, :], ex[:, :, :], 1.0, None, ALU.add))
                    link(nc.vector.reciprocal(sc1[:, :, :], den[:, :, :]))
                    rows = row_s[:, pp, :, :].rearrange("p (j k) c -> p j k c", j=2)
                    link(nc.vector.tensor_scalar(rows[:, :, 0, D + 1:D + 2], sc1[:, :, :], tg[:, 1:2], None, ALU.mult))
                    nc.vector.tensor_tensor(rows[:, :, 1, D + 1:D + 2], rows[:, :, 0, D + 1:D + 2], ex[:, :, :],
                                            ALU.mult).then_inc(dve_link, 1)
                    links[0] += 1
                    link(nc.vector.tensor_copy(row_s[:, pp, :, D], dest_f[:, :]))
                    link(nc.vector.tensor_scalar(dest_f[:, :], dest_f[:, :], float(-TG), None, ALU.add))
                if cur:
                    attended(g, 0)
                if prev:
                    ve.wait_ge(pos_done, g.n(1))
                    nc.vector.tensor_tensor(slot[:, :, :], ps_c[:, 192:208].rearrange("p (j e) -> p j e", j=2),
                                            er_f[:, :].unsqueeze(1).broadcast_to([P, 2, 8]), ALU.add
                                            ).then_inc(pos_read, 1)
                    ve.wait_ge(pos_read, g.n(1))
                    link(nc.vector.tensor_tensor(slot_p[:, :, :, :], oh[:, :, :, :],
                                                 slot[:, :, :].unsqueeze(2).broadcast_to([P, 2, 2, 8]), ALU.mult))
                    link(nc.vector.reduce_sum(slot_f[:, :], slot_p[:, :, :, :].rearrange("p j k e -> p (j k) e"), AX_X))
                    nc.vector.tensor_copy(slot_u[:, pp, :], slot_f[:, :]).then_inc(slots_ok, 1)
                    nc.vector.tensor_tensor(cum[:, 0, :], cum[:, 1, :], cnt[:, 1, :], ALU.add).then_inc(cum_ok, 1)
                if cur:
                    norm2(g, 0)
                if nxt:
                    maxima(g, 0, 0, 1)
                    maxima(g, 0, 1, 1)
                    pieces(g, 0, 1)
                if cur:
                    attended(g, 1)
                relink()

            relink()
            attention_steps(ve, body)

            ve.wait_ge(total_done, 1)
            link(nc.vector.tensor_copy(c_f[:, :], ps_c[0:1, 224:232]))
            nc.vector.tensor_tensor(pad_f[:, :], er_f[0:1, :], c_f[:, :], ALU.add).then_inc(dve_link, 1)
            links[0] += 1
            link(nc.vector.tensor_scalar(c_up[:, :], c_f[:, :], float(P - 1), None, ALU.add))
            link(nc.vector.tensor_copy(pad_i[:, :], pad_f[:, :]))
            link(nc.vector.tensor_scalar(c_sh[:, :], c_up[:, :], 7, None, ALU.logical_shift_right))
            link(nc.vector.tensor_copy(nt_f[:, :], c_sh[:, :]))
            link(nc.vector.tensor_tensor(end_m[:, :, :], tri_f[:, :, :],
                                         nt_f[:, :].unsqueeze(1).broadcast_to([1, 8, 8]), ALU.mult))
            link(nc.vector.reduce_sum(end_f[:, :], end_m[:, :, :], AX_X))
            nc.vector.tensor_scalar(jump[:, :], nt_f[:, :], float(-P), float(R), ALU.mult, ALU.add
                                    ).then_inc(dve_link, 1)
            links[0] += 1
            link(nc.vector.tensor_tensor(past[:, :, :], t_f[:, :].unsqueeze(2).broadcast_to([1, NT, 8]),
                                         end_f[:, :].unsqueeze(1).broadcast_to([1, NT, 8]), ALU.is_ge))
            nc.vector.tensor_tensor(past_j[:, :, :], past[:, :, :],
                                    jump[:, :].unsqueeze(1).broadcast_to([1, NT, 8]), ALU.mult
                                    ).then_inc(dve_link, 1)
            links[0] += 1
            link(nc.vector.reduce_sum(eid_f[:, :], past[:, :, :], AX_X))
            link(nc.vector.reduce_sum(base_f[:, :], past_j[:, :, :], AX_X))
            link(nc.vector.scalar_tensor_tensor(base_g[:, :], t_f[:, :], float(P), base_f[:, :], ALU.mult, ALU.add))
            link(nc.vector.tensor_scalar(eid_i[:, :], eid_f[:, :], float(E - 1), None, ALU.min))
            nc.vector.tensor_scalar(base_i[:, :], base_g[:, :], float(NULL_ROW), None, ALU.min).then_inc(table_ok, 1)

            def shared(c):
                def times(j):
                    ve.wait_ge(sil_ok, c * NJ + j + 1)
                    if j == 0 and not isinstance(c, int):
                        ve.wait_ge(down_done, c * CH)
                    nc.vector.tensor_tensor(hid[:, j, :], ps[:, 2 + j % 2, :], sil_sh[:, j % 2], ALU.mult
                                            ).then_inc(hid_ok, 1)
                for j in range(NJ):
                    times(j)
                for t in range(CH):
                    ve.wait_ge(down_done, c * CH + t + 1)
                    at = c * CH + t
                    xb = x_all[:, at, :] if isinstance(at, int) else x_all[:, bass.ds(at, 1), :].rearrange(
                        "p a d -> p (a d)")
                    nc.vector.scalar_tensor_tensor(xb, ps[:, 4 + t, 0:D], tg[:, 1:2], xb, ALU.mult, ALU.add
                                                   ).then_inc(base_ok, 1)

            shared(0)

            def expert_dst(t, r):
                ve.wait_ge(tile_in[r], (t // 4 + 1) * 16 if isinstance(t, int) else turn[0] * 16 + turn[1])
                if not (isinstance(t, int) and t < 4):
                    ve.wait_ge(ysc[r], (t // 4) * 16 if isinstance(t, int) else turn[0] * 16 + turn[1] - 16)
                nc.vector.tensor_scalar(dst_u[:, r:r + 1], xs_in[:, r, D:D + 1], -1.0, float(2 * T),
                                        ALU.mult, ALU.add).then_inc(dst_ok, 1)

            turn = [None, 0]

            def expert_act(t, r):
                par = r % 2
                ve.wait_ge(silm_ok, t + 1)
                if not (isinstance(t, int) and t < 2):
                    ve.wait_ge(actt_done, t - 1)
                nc.vector.tensor_tensor(act[:, par], ps[:, 2 + par, FI:2 * FI], sil[:, par], ALU.mult
                                        ).then_inc(act_ok, 1)

            def expert_actt(t, r):
                par = r % 2
                ve.wait_ge(actt_done, t + 1)
                if not (isinstance(t, int) and t < 2):
                    ve.wait_ge(y_done, t - 1)
                nc.vector.tensor_copy(act_t[:, par], ps[:, 4, 0:2 * P].rearrange("p (k t) -> p k t", k=2)
                                      ).then_inc(actt_ok, 1)

            def step(t, r):
                expert_actt(t, r)
                if not isinstance(t, int) or t + 1 < NT:
                    expert_act(t + 1, (r + 1) % 4)
                    turn[1] = 16 if r < 3 else 32
                    expert_dst(t + 1, (r + 1) % 4)

            expert_act(0, 0)
            expert_dst(0, 0)
            for r in range(4):
                step(r, r)
            with ve.Fori(1, MOE_LOOP) as i:
                turn[0] = i
                for r in range(4):
                    step(i * 4 + r, r)
            for t in range(4 * MOE_LOOP, NT):
                step(t, t % 4)

            with ve.Fori(1, NCH) as c:
                shared(c)
            for c in range(NCH):
                ve.wait_ge(y_got[c % 2], 32 * (c // 2 + 1))
                xc = x_all[:, CH * c:CH * c + CH, :]
                ve.wait_ge(base_ok, CH * (c + 1))
                link(nc.vector.tensor_tensor(xc, xc, y_in[:, c % 2, 0], ALU.add))
                nc.vector.tensor_tensor(xc, xc, y_in[:, c % 2, 1], ALU.add).then_inc(fin_ok, 1)

        @block.tensor
        def _(pe):
            pe.wait_ge(const_ok, 10)
            pe.wait_ge(small_in, 32)
            nc.tensor.matmul(ps_c[:, 0:2], ones_r[:, :], gate_r[:, :], start=True, stop=True).then_inc(gates_done, 1)

            def body(g, cur, nxt, prev):
                pn = 1 - g.par

                def scores(j, h, d=0):
                    par = (g.c + d) % 2
                    if not (isinstance(g.i, int) and g.c + d == 0 and j == 0 and h == 0):
                        pe.wait_ge(max_ok, g.n(4, d, 2 * j + h))
                    for n in range(8):
                        at = (slice(0, 96), par, 8 * h + n, slice(P * j, P * j + P))
                        last = nc.tensor.matmul(ps_s[:, n, :], q_st[at], k_st[at], start=True, stop=True)
                    last.then_inc(s_done, 1)

                def scores_t(j, h):
                    if h == 0:
                        pe.wait_ge(rows_in[j], g.n(16, 1))
                    if not (isinstance(g.i, int) and g.c == 0 and j == 0 and h == 0):
                        pe.wait_ge(probs_ok, g.n(4, 0, 2 * j + h))
                    for n in range(8):
                        at = (slice(0, 99), g.par, 8 * h + n, slice(P * j, P * j + P))
                        last = nc.tensor.matmul(ps_t[:, n, :], k_st[at], q_st[at], start=True, stop=True)
                    last.then_inc(st_done, 1)

                def values(j, h):
                    pe.wait_ge(probs_ok, g.n(4, 0, 2 * j + h + 1))
                    if h == 0 and not (isinstance(g.i, int) and g.c == 0 and j == 0):
                        pe.wait_ge(o_read, g.n(2, 0, j))
                    if h == 0 and j == 0:
                        pe.wait_ge(v_ok, g.n(1, 1))
                    for n in range(8):
                        c = VW * (8 * h + n)
                        last = nc.tensor.matmul(ps_o[:, c:c + NV], probs[:, 2 * j + h, n, :],
                                                v_s[:, g.par, j, c:c + NV], start=True, stop=True)
                    last.then_inc(pv_done, 1)

                def max_rows(j, d, bank_read):
                    ready, read = held(pe, g.n(2, d, j + 1)), held(pe, g.n(1))
                    pe.wait_ge(const_ok, 10)
                    if prev:
                        pe.wait_ge(bank_read, read)
                    pe.wait_ge(pieces_ok, ready)
                    nc.tensor.matmul(ps_m, mx_pc[:, :, :].rearrange("p c h -> p (c h)"), ident_b[:, :],
                                     is_transpose=True, start=True, stop=True).then_inc(maxt_done, 1)

                if cur:
                    scores_t(0, 0)
                if nxt:
                    if not cur:
                        pe.wait_ge(tanh_ok, 1)
                    pe.wait_ge(xn_ok, g.n(2, 2))
                    if cur:
                        pe.wait_ge(v_ok, g.n(1, 1))
                    for k in range(2):
                        for j in range(2):
                            last = nc.tensor.matmul(ps_a[:, k, P * j:P * j + P], xn[:, j, P * k:P * k + P],
                                                    ident[:, :], is_transpose=True, start=True, stop=True)
                    last.then_inc(xnt_done, 1)
                    if not cur:
                        pe.wait_ge(wq_in, 16)
                    pe.wait_ge(xnt_ok, g.n(1, 2))
                    if cur:
                        pe.wait_ge(kr_ok, g.n(1, 1))
                    for c in range(2):
                        for k in range(2):
                            last = nc.tensor.matmul(ps_b[:, c, :], wq_s[:, k, c, :], xn_t[:, k, :],
                                                    start=k == 0, stop=k == 1)
                    last.then_inc(q_done, 1)
                if cur:
                    scores_t(0, 1)
                    scores(1, 0)
                if prev:
                    pe.wait_ge(xn2_ok, g.n(2))
                    if cur:
                        pe.wait_ge(maxt_ok, g.n(2, 0, 1))
                    else:
                        pe.wait_ge(maxt_ok, g.n(2))
                        pe.wait_ge(pos_read, g.n(1, -1))
                    for k in range(2):
                        for j in range(2):
                            last = nc.tensor.matmul(ps_x[:, k, P * j:P * j + P],
                                                    row_s[:, pn, 2 * j, P * k:P * k + P], ident[:, :],
                                                    is_transpose=True, start=True, stop=True)
                    last.then_inc(x2t_done, 1)
                if cur:
                    values(0, 0)
                if nxt:
                    if not cur:
                        pe.wait_ge(wkv_in, 32)
                    pe.wait_ge(ctx_in[pn], g.turns(16, 1))
                    pe.wait_ge(qr_ok, g.n(1, 2))
                    for c in range(2):
                        for k in range(2):
                            last = nc.tensor.matmul(ps_b[:, c, :], wk_s[:, k, c, :], ctx_s[:, pn, k, :],
                                                    start=k == 0, stop=k == 1)
                    last.then_inc(k_done, 1)
                if prev:
                    pe.wait_ge(xt_ok, g.n(1))
                    if not cur:
                        pe.wait_ge(wr_in, 16)
                    elif g.c == 1:
                        pe.wait_ge(wr_in, 16)
                    for j in range(2):
                        for k in range(2):
                            last = nc.tensor.matmul(ps_c[:, NV * j:NV * j + NV], xt_grp[:, k, P * j:P * j + P],
                                                    wr_s[:, k, :], start=k == 0, stop=k == 1)
                    last.then_inc(router_done, 1)
                if cur:
                    scores(1, 1)
                    values(0, 1)
                    max_rows(1, 0, lg_read)
                if nxt:
                    for j in range(2):
                        for k in range(2):
                            last = nc.tensor.matmul(ps[:, 5, D * j:D * j + D], ctx_s[:, pn, k, P * j:P * j + P],
                                                    wv_s[:, k, :], start=k == 0, stop=k == 1)
                    last.then_inc(v_done, 1)
                if cur:
                    scores_t(1, 0)
                if prev:
                    pe.wait_ge(oh_ok, g.n(1))
                    if cur:
                        pe.wait_ge(maxt_ok, g.n(2, 1))
                    for j in range(2):
                        nc.tensor.matmul(ps_c[:, 192 + 8 * j:200 + 8 * j], before[:, :], cnt[:, j, :],
                                         start=True, stop=False)
                        last = nc.tensor.matmul(ps_c[:, 192 + 8 * j:200 + 8 * j], ones_b[:, :], cum[:, j, :],
                                                start=False, stop=True)
                    last.then_inc(pos_done, 1)
                if nxt:
                    pe.wait_ge(qst[pn], g.turns(96, 1))
                    pe.wait_ge(kst[pn], g.turns(96, 1))
                    scores(0, 0, 1)
                if cur:
                    scores_t(1, 1)
                    values(1, 0)
                if nxt:
                    scores(0, 1, 1)
                if cur:
                    values(1, 1)
                if nxt:
                    max_rows(0, 1, pos_read)

            attention_steps(pe, body)

            pe.wait_ge(cum_ok, G + 1)
            nc.tensor.matmul(ps_c[:, 224:232], ones_b[:, :], cum[:, 0, :], start=True, stop=True
                             ).then_inc(total_done, 1)
            pe.wait_ge(ffn_in, 48)
            pe.wait_ge(xt_out, 16 * (G + 1))
            pe.wait_ge(table_ok, 1)

            def shared(c):
                at = c * (CH * P)
                xt = xt_all[:, :, 0:CH * P] if isinstance(c, int) else xt_all[:, :, bass.ds(at, CH * P)]

                def gate_up(j):
                    if j >= 2:
                        pe.wait_ge(hid_ok, c * NJ + j - 1)
                    elif not isinstance(c, int):
                        pe.wait_ge(hid_ok, c * NJ + j - 1)
                    for w, bank in ((gate_s, j % 2), (up_s, 2 + j % 2)):
                        for k in range(2):
                            last = nc.tensor.matmul(ps[:, bank, :], w[:, k, P * j:P * j + P], xt[:, k, :],
                                                    start=k == 0, stop=k == 1)
                    last.then_inc(gu_done, 1)

                def down(j):
                    pe.wait_ge(hid_ok, c * NJ + j + 1)
                    if j == 0 and not isinstance(c, int):
                        pe.wait_ge(base_ok, c * CH)
                    for t in range(CH):
                        last = nc.tensor.matmul(ps[:, 4 + t, 0:D], hid[:, j, P * t:P * t + P], down_s[:, j, :],
                                                start=j == 0, stop=j == NJ - 1)
                        if j == NJ - 1:
                            last.then_inc(down_done, 1)

                gate_up(0)
                for j in range(1, NJ):
                    gate_up(j)
                    down(j - 1)
                down(NJ - 1)

            shared(0)
            pe.wait_ge(base_ok, CH)
            pe.wait_ge(fc1_in, 16)
            pe.wait_ge(fc2_in, 16)

            turn = [None, 0]

            def expert_x(t, r):
                par = r % 2
                pe.wait_ge(tile_in[r], (t // 4 + 1) * 16 if isinstance(t, int) else turn[0] * 16 + turn[1])
                if not (isinstance(t, int) and t < 2):
                    pe.wait_ge(xst_ok, t - 1)
                for k in range(2):
                    last = nc.tensor.matmul(ps[:, par, P * k:P * k + P], xs_in[:, r, P * k:P * k + P], ident[:, :],
                                            is_transpose=True, start=True, stop=True)
                last.then_inc(xst_done, 1)

            def expert_of(t):
                return pe.value_load(eid_i[0:1, t:t + 1] if isinstance(t, int) else eid_i[0:1, bass.ds(t, 1)],
                                     min_val=0, max_val=E - 1)

            def expert_h(t, r):
                par = r % 2
                e = expert_of(t)
                pe.wait_ge(xst_ok, t + 1)
                if not (isinstance(t, int) and t < 2):
                    pe.wait_ge(act_ok, t - 1)
                for k in range(2):
                    w = fc1_s[:, bass.ds(e * 2 + k, 1), :].rearrange("p a n -> p (a n)")
                    last = nc.tensor.matmul(ps[:, 2 + par, :], xs_t[:, par, k, :], w, start=k == 0, stop=k == 1)
                last.then_inc(h_done, 1)

            def expert_at(t, r):
                par = r % 2
                pe.wait_ge(act_ok, t + 1)
                if not (isinstance(t, int) and t < 1):
                    pe.wait_ge(actt_ok, t)
                for k in range(2):
                    last = nc.tensor.matmul(ps[:, 4, P * k:P * k + P], act[:, par, P * k:P * k + P], ident[:, :],
                                            is_transpose=True, start=True, stop=True)
                last.then_inc(actt_done, 1)

            def expert_y(t, r):
                par = r % 2
                e = expert_of(t)
                pe.wait_ge(actt_ok, t + 1)
                if not (isinstance(t, int) and t < 2):
                    pe.wait_ge(y_ok, t - 1)
                for k in range(2):
                    w = fc2_s[:, bass.ds(e * 2 + k, 1), :].rearrange("p a n -> p (a n)")
                    last = nc.tensor.matmul(ps[:, 5 + par, 0:D], act_t[:, par, k, :], w, start=k == 0, stop=k == 1)
                last.then_inc(y_done, 1)

            def step(t, r):
                if not isinstance(t, int) or t + 2 < NT:
                    turn[1] = 16 if r < 2 else 32
                    expert_x(t + 2, (r + 2) % 4)
                expert_at(t, r)
                if not isinstance(t, int) or t + 1 < NT:
                    expert_h(t + 1, (r + 1) % 4)
                expert_y(t, r)

            expert_x(0, 0)
            expert_x(1, 1)
            expert_h(0, 0)
            for r in range(4):
                step(r, r)
            with pe.Fori(1, MOE_LOOP) as i:
                turn[0] = i
                for r in range(4):
                    step(i * 4 + r, r)
            for t in range(4 * MOE_LOOP, NT):
                step(t, t % 4)

            pe.wait_ge(y_ok, NT)
            with pe.Fori(1, NCH) as c:
                shared(c)



def kernel(x, ctx_768, mask_BxS_bk0, g_xattn, g_ffn, L0_xattn_Wq, L0_xattn_Wkv, L0_ffn_w_router,
           L0_ffn_fc1_w, L0_ffn_fc2_w, L0_ffn_gate_w, L0_ffn_up_w, L0_ffn_down_w):
    import numpy as np
    import concourse.bacc as bacc
    from concourse.bass_utils import run_bass_kernel_spmd

    def tiles(w, p):
        w = np.asarray(w)
        w = w.reshape(*w.shape[:-2], w.shape[-2] // p, p, w.shape[-1])
        return np.moveaxis(w, -2, 0)

    x = np.asarray(x)
    ctx_768 = np.asarray(ctx_768)
    batch, seq, d = x.shape
    cy = ctx_768.shape[2]
    kc = cy // 2
    w_q, w_kv = np.asarray(L0_xattn_Wq), np.asarray(L0_xattn_Wkv)
    fc1, fc2 = tiles(L0_ffn_fc1_w, 128), tiles(L0_ffn_fc2_w, 128)
    arrays = {
        "x": x.reshape(batch * seq, d),
        "ctx_t": ctx_768.reshape(batch * seq, 2, kc).transpose(2, 1, 0),
        "mask": np.ascontiguousarray(np.asarray(mask_BxS_bk0).T).view(np.uint32),
        "gates": np.stack([np.asarray(g_xattn), np.asarray(g_ffn)], axis=1),
        "wq": w_q.reshape(8, 2, 16, 2, 128).transpose(4, 3, 1, 2, 0).reshape(128, 2, 2, 128),
        "wk": w_kv[:d].reshape(8, 2, 16, 2, kc).transpose(4, 3, 1, 2, 0).reshape(kc, 2, 2, 128),
        "wv": w_kv[d:].reshape(d, 2, kc).transpose(2, 1, 0),
        "w_router": tiles(L0_ffn_w_router, 128),
        "fc1": fc1.reshape(128, -1, fc1.shape[-1]),
        "fc2": fc2.reshape(128, -1, fc2.shape[-1]),
        "gate_w": tiles(L0_ffn_gate_w, 128),
        "up_w": tiles(L0_ffn_up_w, 128),
        "down_w": tiles(L0_ffn_down_w, 128),
    }
    arrays = {f"in_{n}": np.ascontiguousarray(a) for n, a in arrays.items()}
    nc = bacc.Bacc("TRN2", target_bir_lowering=False, num_devices=1)
    args = [nc.dram_tensor(n, a.shape, mybir.dt.from_np(a.dtype), kind="ExternalInput").ap()
            for n, a in arrays.items()]
    out = nc.dram_tensor("out", (batch * seq, d), F32, kind="ExternalOutput").ap()
    build_program(nc, *args, out)
    r = run_bass_kernel_spmd(nc, [arrays], core_ids=[0])
    return r.results[0]["out"].reshape(batch, seq, d)
```

```python
from contextlib import ExitStack

import numpy as np

import concourse.bass as bass
from concourse import mybir

ALU = mybir.AluOpType
ACT = mybir.ActivationFunctionType
F32 = mybir.dt.float32
BF16 = mybir.dt.bfloat16
I32 = mybir.dt.int32
U32 = mybir.dt.uint32
U8 = mybir.dt.uint8
AX_X = mybir.AxisListType.X

P = 128
HEADS = 16
HD = 16
PIECES = 6
VW = HD + 1
NV = 96
Q_SLOTS = [(0, 0), (1, 1), (2, 2), (3, 0), (4, 1), (5, 0)]
K_SLOTS = [(0, 0), (1, 0), (2, 0), (3, 1), (4, 1), (5, 2)]
EPS = 1e-5
TWO_ONES = float(np.array([0x3F803F80], np.uint32).view(np.float32)[0])


class Group:

    def __init__(self, i, c):
        self.i, self.c = i, c
        self.par = c % 2

    def n(self, k, d=0, plus=0):
        const = k * (self.c + d) + plus
        return const if isinstance(self.i, int) else self.i * (2 * k) + const

    def turns(self, k, d=0):
        const = k * ((self.c + d) // 2 + 1)
        return const if isinstance(self.i, int) else self.i * k + const


def build_program(nc, x, ctx_t, mask, gates, wq, wk, wv, w_router, fc1, fc2, gate_w, up_w, down_w, out):
    T, D = x.shape
    B = T // P
    G = B // 2
    TG = 2 * P
    KC = ctx_t.shape[0]
    E = w_router.shape[2]
    FI = fc1.shape[2] // 2
    ISH = gate_w.shape[2]
    R = T + P
    NULL_ROW = E * R
    NT = (2 * T + E * (P - 1)) // P
    ROW = D + 2
    CH = 4
    NCH = B // CH
    NJ = ISH // P

    xs = nc.dram_tensor("dispatched", (NULL_ROW + P, ROW), F32, kind="Internal").ap()
    ys = nc.dram_tensor("expert_rows", (2 * T, D), F32, kind="Internal").ap()
    x_view = x.rearrange("(b p) d -> p b d", p=P)
    out_view = out.rearrange("(b p) d -> p b d", p=P)
    y_view = ys.rearrange("(k b p) d -> p k b d", k=2, p=P)

    with ExitStack() as es:
        def sb(name, shape, dt=F32):
            return es.enter_context(nc.sbuf_tensor(name, shape, dt))

        def sem(name):
            return es.enter_context(nc.semaphore(name))

        wq_s = sb("wq_s", [P, 2, 2, P])
        wk_s = sb("wk_s", [KC, 2, 2, P])
        wv_s = sb("wv_s", [KC, 2, D])
        wr_s = sb("wr_s", [P, 2, NV])
        fc1_s = sb("fc1_s", [P, 2 * E, 2 * FI])
        fc2_s = sb("fc2_s", [P, 2 * E, D])
        gate_s = sb("gate_s", [P, 2, ISH])
        up_s = sb("up_s", [P, 2, ISH])
        down_s = sb("down_s", [P, NJ, D])
        x_all = sb("x_all", [P, B, D])
        xt_all = sb("xt_all", [P, 2, T])
        ctx_s = sb("ctx_s", [KC, 2, 2, TG])
        xn = sb("xn", [P, 2, D])
        xn_t = sb("xn_t", [P, 2, TG])
        q_pc = sb("q_pc", [P, 3, 2 * TG], BF16)
        k_pc = sb("k_pc", [P, 3, 2 * TG], BF16)
        q_rest = sb("q_rest", [P, 2 * TG])
        k_rest = sb("k_rest", [P, 2 * TG])
        q_st = sb("q_st", [P, 2, HEADS, TG], BF16)
        k_st = sb("k_st", [P, 2, HEADS, TG], BF16)
        v_s = sb("v_s", [P, 2, 2, VW * (HEADS - 1) + NV + 1])
        probs = sb("probs", [P, 4, 8, P])
        row_s = sb("row_s", [P, 2, 4, ROW])
        xt_grp = sb("xt_grp", [P, 2, TG])
        att = sb("att", [P, D])
        ident = sb("ident", [P, P])
        ident_b = sb("ident_b", [P, P], BF16)
        before = sb("before", [P, P], BF16)
        ones_b = sb("ones_b", [P, P], BF16)
        ones_r = sb("ones_r", [1, P])
        mask_u = sb("mask_u", [P, B // 4], U32)
        mask_f = sb("mask_f", [P, B])
        gate_r = sb("gate_r", [1, 2])
        tg = sb("tg", [P, 2])
        mhalf = sb("mhalf", [P, B])
        st1 = sb("st1", [P, B, 6])
        mv1 = sb("mv1", [P, B, 2])
        ve1 = sb("ve1", [P, B])
        rs1 = sb("rs1", [P, B])
        rm1 = sb("rm1", [P, B])
        st2 = sb("st2", [P, 6])
        mv2 = sb("mv2", [P, 2, 2])
        ve2 = sb("ve2", [P, 2])
        rs2 = sb("rs2", [P, 2])
        mx = sb("mx", [P, HEADS])
        mx_pc = sb("mx_pc", [P, 3, HEADS], BF16)
        mx_rest = sb("mx_rest", [P, HEADS])
        mx_t = sb("mx_t", [3 * HEADS, 2, P], BF16)
        rsum = sb("rsum", [P, HEADS])
        rsg = sb("rsg", [P, HEADS])
        lg = sb("lg", [P, 2, 8])
        top = sb("top", [P, 2, 8])
        topi = sb("topi", [P, 2, 8], U32)
        idx_f = sb("idx_f", [P, 4])
        dif = sb("dif", [P, 2, 1])
        ex = sb("ex", [P, 2, 1])
        den = sb("den", [P, 2, 1])
        sc1 = sb("sc1", [P, 2, 1])
        oh = sb("oh", [P, 2, 2, 8])
        cnt = sb("cnt", [P, 2, 8], BF16)
        cum = sb("cum", [P, 2, 8], BF16)
        slot = sb("slot", [P, 2, 8])
        slot_p = sb("slot_p", [P, 2, 2, 8])
        slot_f = sb("slot_f", [P, 4])
        slot_u = sb("slot_u", [P, 2, 4], U32)
        e_i = sb("e_i", [P, 8], I32)
        e_f = sb("e_f", [P, 8])
        er_f = sb("er_f", [P, 8])
        dest_i = sb("dest_i", [P, 4], I32)
        dest_f = sb("dest_f", [P, 4])
        t_i = sb("t_i", [1, NT], I32)
        t_f = sb("t_f", [1, NT])
        tri_f = sb("tri_f", [1, 8, 8])
        c_f = sb("c_f", [1, 8])
        c_up = sb("c_up", [1, 8], I32)
        c_sh = sb("c_sh", [1, 8], I32)
        nt_f = sb("nt_f", [1, 8])
        end_m = sb("end_m", [1, 8, 8])
        end_f = sb("end_f", [1, 8])
        jump = sb("jump", [1, 8])
        past = sb("past", [1, NT, 8])
        past_j = sb("past_j", [1, NT, 8])
        eid_f = sb("eid_f", [1, NT])
        base_f = sb("base_f", [1, NT])
        base_g = sb("base_g", [1, NT])
        eid_i = sb("eid_i", [1, NT], I32)
        base_i = sb("base_i", [1, NT], I32)
        pad_f = sb("pad_f", [1, 8])
        pad_i = sb("pad_i", [1, 8], I32)
        zrow = sb("zrow", [P, ROW])

        k_f = k_st[:, :, :, :].rearrange("p a h t -> p (a h t)").bitcast(F32)
        hid = k_f[:, 0:NJ * CH * P].rearrange("p (j t) -> p j t", j=NJ)
        sil_sh = k_f[:, NJ * CH * P:NJ * CH * P + 2 * CH * P].rearrange("p (r t) -> p r t", r=2)
        q_f = q_st[:, :, :, :].rearrange("p a h t -> p (a h t)").bitcast(F32)
        y_in = q_f[:, :].rearrange("p (r k t d) -> p r k t d", r=2, k=2, t=CH)
        pf = probs[:, :, :, :].rearrange("p a h t -> p (a h t)")
        xs_in = pf[:, 0:4 * ROW].rearrange("p (r c) -> p r c", r=4)
        o0 = 4 * ROW
        xs_t = pf[:, o0:o0 + 2 * 2 * P].rearrange("p (r k t) -> p r k t", r=2, k=2)
        o0 += 2 * 2 * P
        sil = pf[:, o0:o0 + 2 * FI].rearrange("p (r c) -> p r c", r=2)
        o0 += 2 * FI
        act = pf[:, o0:o0 + 2 * FI].rearrange("p (r c) -> p r c", r=2)
        o0 += 2 * FI
        act_t = pf[:, o0:o0 + 2 * 2 * P].rearrange("p (r k t) -> p r k t", r=2, k=2)
        y_out = v_s[:, :, :, :].rearrange("p a b c -> p (a b c)")[:, 0:4 * D].rearrange("p (r c) -> p r c", r=4)
        dst_u = slot_u[:, 0, :]

        ps = es.enter_context(nc.psum_tensor("ps", [P, 8, 512], F32))
        ps_s = ps[:, 0:2, :].rearrange("p b (h t) -> p (b h) t", h=4)
        ps_t = ps[:, 2:4, :].rearrange("p b (h t) -> p (b h) t", h=4)
        ps_o = ps[:, 4, :]
        ps_a = ps[:, 5, :].rearrange("p (k t) -> p k t", k=2)
        ps_b = ps[:, 6, :].rearrange("p (c t) -> p c t", c=2)
        ps_c = ps[:, 7, :]
        ps_x = ps_c.rearrange("p (k t) -> p k t", k=2)
        ps_m = ps_c[0:3 * HEADS, 256:256 + P // 2].bitcast(BF16)

        names = """x_in0 x_in1 x_rest ctx_in0 ctx_in1 wq_in wk_in wv_in kones_ok small_in wr_in ffn_in fc1_in fc2_in
            const_ok tanh_ok gates_done zero_row_ok v_ones_ok wr_ok mask_ok
            ln1_var rs1_ok rm1_ok xn_ok xnt_done xnt_ok q_done k_done v_done q1_ok q2_ok q3_ok k1_ok k2_ok k3_ok
            qr_ok kr_ok qst0 qst1 kst0 kst1 v_ok s_done max_ok pieces_ok maxt_done maxt_ok rows_in0 rows_in1
            st_done probs_ok pv_done o_read ln2_var rs2_ok xn2_ok dup_ok x2t_done xt_ok xt_out router_done lg_read
            dif_ok ex_ok oh_ok cum_ok pos_done pos_read slots_ok scat0 scat1 total_done table_ok pad_out
            dve_link pool_link act_link
            gu_done sil_ok hid_ok down_done base_ok
            tile_in0 tile_in1 tile_in2 tile_in3 xst_done xst_ok h_done silm_ok act_ok actt_done actt_ok y_done y_ok
            dst_ok ysc0 ysc1 ysc2 ysc3 y_in0 y_in1 fin_ok out_done""".split()
        S = {n: sem(n) for n in names}
        x_in0, x_in1, x_rest = S["x_in0"], S["x_in1"], S["x_rest"]
        wq_in, wk_in, wv_in, kones_ok = S["wq_in"], S["wk_in"], S["wv_in"], S["kones_ok"]
        small_in, wr_in, ffn_in, fc1_in, fc2_in = S["small_in"], S["wr_in"], S["ffn_in"], S["fc1_in"], S["fc2_in"]
        ctx_in = [S["ctx_in0"], S["ctx_in1"]]
        const_ok, tanh_ok, gates_done, zero_row_ok = S["const_ok"], S["tanh_ok"], S["gates_done"], S["zero_row_ok"]
        v_ones_ok, wr_ok, mask_ok, ln1_var, rs1_ok, rm1_ok = (S["v_ones_ok"], S["wr_ok"], S["mask_ok"], S["ln1_var"],
                                                              S["rs1_ok"], S["rm1_ok"])
        xn_ok, xnt_done, xnt_ok, q_done, k_done, v_done = (S["xn_ok"], S["xnt_done"], S["xnt_ok"], S["q_done"],
                                                           S["k_done"], S["v_done"])
        q1_ok, q2_ok, q3_ok, k1_ok, k2_ok, k3_ok = (S["q1_ok"], S["q2_ok"], S["q3_ok"], S["k1_ok"], S["k2_ok"],
                                                    S["k3_ok"])
        qr_ok, kr_ok, v_ok, s_done, max_ok, pieces_ok = (S["qr_ok"], S["kr_ok"], S["v_ok"], S["s_done"], S["max_ok"],
                                                         S["pieces_ok"])
        qst, kst, rows_in = [S["qst0"], S["qst1"]], [S["kst0"], S["kst1"]], [S["rows_in0"], S["rows_in1"]]
        maxt_done, maxt_ok, st_done, probs_ok, pv_done = (S["maxt_done"], S["maxt_ok"], S["st_done"], S["probs_ok"],
                                                          S["pv_done"])
        o_read, ln2_var, rs2_ok, xn2_ok, dup_ok = S["o_read"], S["ln2_var"], S["rs2_ok"], S["xn2_ok"], S["dup_ok"]
        x2t_done, xt_ok, xt_out, router_done, lg_read = (S["x2t_done"], S["xt_ok"], S["xt_out"], S["router_done"],
                                                         S["lg_read"])
        dif_ok, ex_ok, oh_ok, pos_done, pos_read, slots_ok = (S["dif_ok"], S["ex_ok"], S["oh_ok"], S["pos_done"],
                                                              S["pos_read"], S["slots_ok"])
        scat = [S["scat0"], S["scat1"]]
        cum_ok = S["cum_ok"]
        total_done, table_ok, pad_out = S["total_done"], S["table_ok"], S["pad_out"]
        dve_link, pool_link = S["dve_link"], S["pool_link"]
        gu_done, sil_ok, hid_ok, down_done, base_ok = (S["gu_done"], S["sil_ok"], S["hid_ok"], S["down_done"],
                                                       S["base_ok"])
        tile_in = [S[f"tile_in{r}"] for r in range(4)]
        ysc = [S[f"ysc{r}"] for r in range(4)]
        y_got = [S["y_in0"], S["y_in1"]]
        xst_done, xst_ok, h_done, silm_ok, act_ok = (S["xst_done"], S["xst_ok"], S["h_done"], S["silm_ok"],
                                                     S["act_ok"])
        actt_done, actt_ok, y_done, y_ok, dst_ok = (S["actt_done"], S["actt_ok"], S["y_done"], S["y_ok"],
                                                    S["dst_ok"])
        fin_ok, out_done = S["fin_ok"], S["out_done"]

        def held(eng, value):
            return value if isinstance(value, int) else eng.to_reg(value)

        def attention_steps(eng, body):
            def step(i, c):
                body(Group(i, c), now=0 <= c < G, soon=-1 <= c < G - 1, later=c < G - 2, past=c >= 1)

            step(0, -2)
            step(0, -1)
            step(0, 0)
            with eng.Fori(0, (G - 4) // 2) as i:
                step(i, 1)
                step(i, 2)
            for c in range(G - 3, G + 1):
                step(0, c)

        MOE_LOOP = (NT - 3) // 4

        block = es.enter_context(nc.Block())

        @block.sync
        def _(sp):
            sp.dma_start(x_all[:, 0:2, :], x_view[:, 0:2, :]).then_inc(x_in0, 16)
            sp.dma_start(mask_u[:, :], mask).then_inc(small_in, 16)
            sp.dma_start(gate_r[:, :], gates).then_inc(small_in, 16)
            sp.sem_inc(xt_out, 16)

            def body(g, now, soon, later, past):
                pn = 1 - g.par
                if later:
                    if now:
                        sp.wait_ge(v_done, g.n(1, 1))
                    off = g.n(TG, 2)
                    src = ctx_t[:, :, off:off + TG] if isinstance(off, int) else ctx_t[:, :, bass.ds(off, TG)]
                    sp.dma_start(ctx_s[:, g.par], src).then_inc(ctx_in[g.par], 16)
                if g.c == -2:
                    sp.dma_start(x_all[:, 2:4, :], x_view[:, 2:4, :]).then_inc(x_in1, 16)
                    sp.dma_start(wv_s[:, :, :], wv).then_inc(wv_in, 16)
                    sp.wait_ge(wr_ok, 1)
                    sp.dma_start(wr_s[:, :, 0:E], w_router).then_inc(wr_in, 16)
                if soon:
                    if g.c >= 1:
                        old, new = held(sp, g.n(4)), held(sp, g.n(1, 2))
                        sp.wait_ge(small_in, 32)
                        sp.wait_ge(st_done, old)
                    for piece, ready in ((0, k1_ok), (1, k2_ok), (2, k3_ok)):
                        sp.wait_ge(ready, g.n(1, 2))
                        for s, p in K_SLOTS:
                            if p == piece:
                                sp.dma_start(k_st[HD * s:HD * s + HD, pn].rearrange("p h t -> p (h t)"),
                                             k_pc[:, p, :]).then_inc(kst[pn], 16)
                if past:
                    sp.wait_ge(xt_ok, g.n(1))
                    off = g.n(TG, -1)
                    dst = xt_all[:, :, off:off + TG] if isinstance(off, int) else xt_all[:, :, bass.ds(off, TG)]
                    sp.dma_start(dst, xt_grp[:, :, :]).then_inc(xt_out, 16)
                if soon:
                    e2 = g.n(2, 1)
                    part = slice(e2, e2 + 2) if isinstance(e2, int) else bass.ds(e2, 2)
                    sp.dma_start(fc1_s[:, part, :], fc1[:, part, :]).then_inc(fc1_in, 16)
                    sp.dma_start(fc2_s[:, part, :], fc2[:, part, :]).then_inc(fc2_in, 16)
                if later:
                    if now:
                        old = held(sp, g.n(4, 1))
                        sp.wait_ge(small_in, 32)
                        sp.wait_ge(st_done, old)
                    for piece, ready in ((0, q1_ok), (1, q2_ok), (2, q3_ok)):
                        sp.wait_ge(ready, g.n(1, 3))
                        for s, p in Q_SLOTS:
                            if p == piece:
                                sp.dma_start(q_st[HD * s:HD * s + HD, g.par].rearrange("p h t -> p (h t)"),
                                             q_pc[:, p, :]).then_inc(qst[g.par], 16)
                if g.c == -2:
                    sp.dma_start(x_all[:, 4:B, :], x_view[:, 4:B, :]).then_inc(x_rest, 16)
                if g.c == G - 2:
                    sp.dma_start(gate_s[:, :, :], gate_w).then_inc(ffn_in, 16)
                    sp.dma_start(up_s[:, :, :], up_w).then_inc(ffn_in, 16)
                    sp.dma_start(down_s[:, :, :], down_w).then_inc(ffn_in, 16)

            attention_steps(sp, body)

            sp.wait_ge(zero_row_ok, 1)
            sp.wait_ge(table_ok, 1)
            for e in range(E):
                row = sp.value_load(pad_i[0:1, e:e + 1], min_val=0, max_val=NULL_ROW - P)
                sp.dma_start(xs[bass.ds(row, P), :], zrow[:, :]).then_inc(pad_out, 16)
            sp.wait_ge(scat[0], 64 * (G // 2))
            sp.wait_ge(scat[1], 64 * (G // 2) + 16)
            sp.wait_ge(pad_out, 16 * E)

            def first_rows(t, n):
                at = base_i[0:1, t:t + n] if isinstance(t, int) else base_i[0:1, bass.ds(t, n)]
                _, values = nc.values_load_multi_w_load_instructions(
                    at, engines=[mybir.EngineType.SP], min_val=0, max_val=NULL_ROW)
                return values

            def load_tile(t, r, turn, row):
                if not (isinstance(turn, int) and turn == 0):
                    sp.wait_ge(y_ok, t - 3)
                    sp.wait_ge(dst_ok, t - 3)
                sp.dma_start(xs_in[:, r, :], xs[bass.ds(row, P), :]).then_inc(tile_in[r], 16)

            rows = first_rows(0, 4)
            for t in range(4):
                load_tile(t, t, 0, rows[t])
            with sp.Fori(1, MOE_LOOP) as i:
                rows = first_rows(i * 4, 4)
                for r in range(4):
                    load_tile(i * 4 + r, r, i, rows[r])
            rows = first_rows(4 * MOE_LOOP, NT - 4 * MOE_LOOP)
            for t in range(4 * MOE_LOOP, NT):
                load_tile(t, t % 4, MOE_LOOP, rows[t - 4 * MOE_LOOP])

            for r in range(4):
                sp.wait_ge(ysc[r], 16 * len(range(r, NT, 4)))
            for c in range(NCH):
                if c >= 2:
                    sp.wait_ge(fin_ok, c - 1)
                sp.dma_start(y_in[:, c % 2, 0], y_view[:, 0, CH * c:CH * c + CH, :]).then_inc(y_got[c % 2], 16)
                sp.dma_start(y_in[:, c % 2, 1], y_view[:, 1, CH * c:CH * c + CH, :]).then_inc(y_got[c % 2], 16)
                if c >= 1:
                    sp.wait_ge(fin_ok, c)
                    sp.dma_start(out_view[:, CH * (c - 1):CH * c, :],
                                 x_all[:, CH * (c - 1):CH * c, :]).then_inc(out_done, 16)
            sp.wait_ge(fin_ok, NCH)
            sp.dma_start(out_view[:, B - CH:B, :], x_all[:, B - CH:B, :]).then_inc(out_done, 16)
            sp.wait_ge(out_done, 16 * NCH)

        @block.gpsimd
        def _(pool):
            nc.gpsimd.memset(wr_s[:, :, :], 0.0).then_inc(wr_ok, 1)
            nc.gpsimd.memset(ident[:, :], 0.0).then_inc(pool_link, 1)
            nc.gpsimd.memset(ident_b[:, :], 0.0).then_inc(pool_link, 1)
            nc.gpsimd.memset(before[:, :], 1.0).then_inc(pool_link, 1)
            nc.gpsimd.memset(tri_f[:, :, :], 1.0).then_inc(pool_link, 1)
            nc.gpsimd.memset(mhalf[:, :], -0.5).then_inc(pool_link, 1)
            pool.wait_ge(pool_link, 5)
            nc.gpsimd.affine_select(out=ident[:, :], in_=ident[:, :], compare_op=ALU.not_equal, fill=1.0,
                                    base=0, pattern=[[-1, P]], channel_multiplier=1).then_inc(const_ok, 1)
            nc.gpsimd.affine_select(out=ident_b[:, :], in_=ident_b[:, :], compare_op=ALU.not_equal, fill=1.0,
                                    base=0, pattern=[[-1, P]], channel_multiplier=1).then_inc(const_ok, 1)
            nc.gpsimd.affine_select(out=before[:, :], in_=before[:, :], compare_op=ALU.is_gt, fill=0.0,
                                    base=0, pattern=[[1, P]], channel_multiplier=-1).then_inc(const_ok, 1)
            nc.gpsimd.affine_select(out=tri_f[:, :, :], in_=tri_f[:, :, :], compare_op=ALU.is_ge, fill=0.0,
                                    base=0, pattern=[[1, 8], [-1, 8]], channel_multiplier=0).then_inc(const_ok, 1)
            nc.gpsimd.iota(e_i[:, :], pattern=[[1, 8]], base=0, channel_multiplier=0).then_inc(const_ok, 1)
            nc.gpsimd.iota(t_i[:, :], pattern=[[1, NT]], base=0, channel_multiplier=0).then_inc(const_ok, 1)
            nc.gpsimd.iota(dest_i[:, :], pattern=[[-P, 2], [-T, 2]], base=2 * T,
                           channel_multiplier=-1).then_inc(const_ok, 1)
            nc.gpsimd.memset(zrow[:, :], 0.0).then_inc(zero_row_ok, 1)
            pool.wait_ge(zero_row_ok, 1)
            nc.gpsimd.dma_start(xs[NULL_ROW:NULL_ROW + P, :], zrow[:, :]).then_inc(scat[1], 16)
            pool.wait_ge(ln1_var, 1)
            nc.gpsimd.tensor_tensor(rs1[:, 0:2], ve1[:, 0:2], mhalf[:, 0:2], ALU.pow).then_inc(rs1_ok, 1)
            pool.wait_ge(ln1_var, 2)
            nc.gpsimd.tensor_tensor(rs1[:, 2:4], ve1[:, 2:4], mhalf[:, 2:4], ALU.pow).then_inc(rs1_ok, 1)

            def body(g, now, soon, later, past):
                pn = 1 - g.par
                if past:
                    pool.wait_ge(ln2_var, g.n(2))
                    nc.gpsimd.tensor_tensor(rs2[:, 1:2], ve2[:, 1:2], mhalf[:, 0:1], ALU.pow).then_inc(rs2_ok, 1)
                if soon:
                    pool.wait_ge(k2_ok, g.n(1, 2))
                    if now:
                        pool.wait_ge(kst[g.par], g.turns(96))
                    nc.gpsimd.tensor_tensor(k_pc[:, 2, :], k_rest[:, :], k_pc[:, 1, :],
                                            ALU.subtract).then_inc(k3_ok, 1)
                if now:
                    pool.wait_ge(ln2_var, g.n(2, 0, 1))
                    nc.gpsimd.tensor_tensor(rs2[:, 0:1], ve2[:, 0:1], mhalf[:, 0:1], ALU.pow).then_inc(rs2_ok, 1)
                if past:
                    places, rows = held(pool, g.n(1)), held(pool, g.n(2))
                    pool.wait_ge(pool_link, 5)
                    pool.wait_ge(slots_ok, places)
                    pool.wait_ge(dup_ok, rows)
                    for m in range(4):
                        nc.gpsimd.indirect_dma_start(
                            xs, bass.IndirectOffsetOnAxis(slot_u[:, pn, m:m + 1], 0), row_s[:, pn, m, :], None,
                            bounds_check=NULL_ROW + P - 1, oob_is_err=False).then_inc(scat[pn], 16)
                if later:
                    pool.wait_ge(q2_ok, g.n(1, 3))
                    if g.c >= -1:
                        pool.wait_ge(qst[pn], g.turns(96, 1))
                    nc.gpsimd.tensor_tensor(q_pc[:, 2, :], q_rest[:, :], q_pc[:, 1, :],
                                            ALU.subtract).then_inc(q3_ok, 1)
                if g.c == -1:
                    pool.wait_ge(ln1_var, 3)
                    nc.gpsimd.tensor_tensor(rs1[:, 4:B], ve1[:, 4:B], mhalf[:, 4:B], ALU.pow).then_inc(rs1_ok, 1)

            attention_steps(pool, body)

            def scatter(t, r, turn):
                tiles = held(pool, t + 1)
                pool.wait_ge(pool_link, 5)
                pool.wait_ge(y_ok, tiles)
                pool.wait_ge(dst_ok, tiles)
                nc.gpsimd.indirect_dma_start(
                    ys, bass.IndirectOffsetOnAxis(dst_u[:, r:r + 1], 0), y_out[:, r, :], None,
                    bounds_check=2 * T - 1, oob_is_err=False).then_inc(ysc[r], 16)

            with pool.Fori(0, MOE_LOOP) as i:
                for r in range(4):
                    scatter(i * 4 + r, r, i)
            for t in range(4 * MOE_LOOP, NT):
                scatter(t, t % 4, MOE_LOOP)

        @block.scalar
        def _(sa):
            sa.dma_start(wq_s[:, :, :, :], wq).then_inc(wq_in, 16)
            sa.dma_start(wk_s[:, :, :, :], wk).then_inc(wk_in, 16)

            def body(g, now, soon, later, past):
                pn = 1 - g.par

                def exp(j, h):
                    sa.wait_ge(st_done, g.n(4, 0, 2 * j + h + 1))
                    if not (isinstance(g.i, int) and g.c == 0):
                        sa.wait_ge(pv_done, g.n(4, -1, 2 * j + h + 1))
                    nc.scalar.activation(probs[:, 2 * j + h], ps_t, ACT.Exp, scale=HD ** -0.5).then_inc(probs_ok, 1)

                def max_rows(j, d):
                    par = (g.par + d) % 2
                    count = held(sa, g.n(2, d, j + 1))
                    if not (isinstance(g.i, int) and g.c + d == 0):
                        taken = held(sa, g.n(16, d))
                        sa.wait_ge(small_in, 32)
                        sa.wait_ge(rows_in[j], taken)
                    sa.wait_ge(maxt_done, count)
                    nc.scalar.activation(mx_t[:, j, :], ps_m, ACT.Copy).then_inc(maxt_ok, 1)
                    sa.wait_ge(small_in, 32)
                    sa.wait_ge(maxt_ok, count)
                    sa.dma_start(q_st[6 * HD:6 * HD + 3, par, :, P * j:P * j + P],
                                 mx_t[:, j, :]).then_inc(rows_in[j], 16)

                if soon:
                    sa.wait_ge(k_done, g.n(1, 2))
                    if now:
                        sa.wait_ge(kst[g.par], g.turns(96))
                    nc.scalar.activation(k_pc[:, 0, :], ps[:, 6, :], ACT.Copy).then_inc(k1_ok, 1)
                if past:
                    sa.wait_ge(x2t_done, g.n(1))
                    sa.wait_ge(xt_out, g.n(16))
                    nc.scalar.activation(xt_grp[:, :, :], ps_x, ACT.Copy).then_inc(xt_ok, 1)
                if soon:
                    sa.wait_ge(kr_ok, g.n(1, 2))
                    nc.scalar.activation(k_pc[:, 1, :], k_rest[:, :], ACT.Copy).then_inc(k2_ok, 1)
                if past:
                    sa.wait_ge(xn2_ok, g.n(2))
                    nc.scalar.activation(row_s[:, pn, 3, 0:D], row_s[:, pn, 2, 0:D], ACT.Copy).then_inc(dup_ok, 1)
                if now:
                    exp(0, 0)
                if soon:
                    sa.wait_ge(v_done, g.n(1, 2))
                    if g.c >= 1:
                        sa.wait_ge(pv_done, g.n(4))
                    if g.c == -1:
                        sa.wait_ge(v_ones_ok, 1)
                    dst = v_s[:, pn, :, 0:VW * HEADS].rearrange("p j (h e) -> p j h e", e=VW)[:, :, :, 0:HD]
                    nc.scalar.activation(dst, ps[:, 5, :].rearrange("p (j h e) -> p j h e", j=2, h=HEADS),
                                         ACT.Copy).then_inc(v_ok, 1)
                if now:
                    max_rows(1, 0)
                    exp(0, 1)
                if past:
                    sa.wait_ge(dif_ok, g.n(1))
                    nc.scalar.activation(ex[:, :, :], dif[:, :, :], ACT.Exp).then_inc(ex_ok, 1)
                if later:
                    sa.wait_ge(xnt_done, g.n(1, 3))
                    if g.c >= -1:
                        sa.wait_ge(q_done, g.n(1, 2))
                    nc.scalar.activation(xn_t[:, :, :], ps_b, ACT.Copy).then_inc(xnt_ok, 1)
                if now:
                    exp(1, 0)
                    sa.wait_ge(xn2_ok, g.n(2, 0, 1))
                    nc.scalar.activation(row_s[:, g.par, 1, 0:D], row_s[:, g.par, 0, 0:D],
                                         ACT.Copy).then_inc(dup_ok, 1)
                if later:
                    sa.wait_ge(q_done, g.n(1, 3))
                    if g.c >= -1:
                        sa.wait_ge(qst[pn], g.turns(96, 1))
                    nc.scalar.activation(q_pc[:, 0, :], ps[:, 6, :], ACT.Copy).then_inc(q1_ok, 1)
                if now:
                    exp(1, 1)
                if later:
                    sa.wait_ge(qr_ok, g.n(1, 3))
                    nc.scalar.activation(q_pc[:, 1, :], q_rest[:, :], ACT.Copy).then_inc(q2_ok, 1)
                if g.c == -2:
                    sa.wait_ge(gates_done, 1)
                    nc.scalar.activation(tg[:, :], ps_c[:, 0:2], ACT.Tanh).then_inc(tanh_ok, 1)
                if soon:
                    max_rows(0, 1)

            attention_steps(sa, body)

            def shared(c):
                for j in range(NJ):
                    sa.wait_ge(gu_done, c * NJ + j + 1)
                    if j >= 2 or not isinstance(c, int):
                        sa.wait_ge(hid_ok, c * NJ + j - 1)
                    nc.scalar.activation(sil_sh[:, j % 2], ps[:, j % 2, :], ACT.Silu).then_inc(sil_ok, 1)

            shared(0)

            def expert(t, r):
                par = r % 2

                def first():
                    return isinstance(t, int) and t < 2

                sa.wait_ge(h_done, t + 1)
                if not first():
                    sa.wait_ge(act_ok, t - 1)
                nc.scalar.activation(sil[:, par], ps[:, 2 + par, 0:FI], ACT.Silu).then_inc(silm_ok, 1)

            def expert_x(t, r):
                par = r % 2
                sa.wait_ge(xst_done, t + 1)
                if not (isinstance(t, int) and t < 2):
                    sa.wait_ge(h_done, t - 1)
                nc.scalar.activation(xs_t[:, par], ps[:, par, 0:2 * P].rearrange("p (k t) -> p k t", k=2),
                                     ACT.Copy).then_inc(xst_ok, 1)

            def expert_y(t, r):
                sa.wait_ge(y_done, t + 1)
                if not (isinstance(t, int) and t < 4):
                    sa.wait_ge(ysc[r], (t // 4) * 16 if isinstance(t, int) else t4(t))
                nc.scalar.activation(y_out[:, r, :], ps[:, 5 + r % 2, 0:D], ACT.Copy,
                                     scale=xs_in[:, r, D + 1:D + 2]).then_inc(y_ok, 1)

            turn = [None]

            def t4(_):
                return turn[0] * 16

            expert_x(0, 0)
            expert_x(1, 1)
            expert(0, 0)
            for r in range(4):
                expert_x(r + 2, (r + 2) % 4)
                expert(r + 1, (r + 1) % 4)
                expert_y(r, r)
            with sa.Fori(1, MOE_LOOP) as i:
                turn[0] = i
                for r in range(4):
                    expert_x(i * 4 + r + 2, (r + 2) % 4)
                    expert(i * 4 + r + 1, (r + 1) % 4)
                    expert_y(i * 4 + r, r)
            for t in range(4 * MOE_LOOP, NT):
                if t + 2 < NT:
                    expert_x(t + 2, (t + 2) % 4)
                if t + 1 < NT:
                    expert(t + 1, (t + 1) % 4)
                expert_y(t, t % 4)

            with sa.Fori(1, NCH) as c:
                shared(c)

        @block.vector
        def _(ve):
            links = [0]

            def link(ins):
                links[0] += 1
                ins.then_inc(dve_link, 1)
                ve.wait_ge(dve_link, links[0])

            def relink():
                if links[0]:
                    ve.wait_ge(dve_link, links[0])
                    ve.sem_clear(dve_link)
                    links[0] = 0

            nc.vector.memset(ones_r[:, :], 1.0).then_inc(const_ok, 1)
            nc.vector.memset(ones_b[:, :], 1.0).then_inc(const_ok, 1)
            nc.vector.memset(cum[:, :, :], 0.0).then_inc(cum_ok, 1)
            def stats(b0, b1):
                for b in range(b0, b1):
                    nc.vector.bn_stats(st1[:, b, :], x_all[:, b, :]).then_inc(dve_link, 1)
                links[0] += b1 - b0
                ve.wait_ge(dve_link, links[0])
                for b in range(b0, b1):
                    nc.vector.bn_aggr(mv1[:, b, :], st1[:, b, :]).then_inc(dve_link, 1)
                links[0] += b1 - b0
                ve.wait_ge(dve_link, links[0])
                nc.vector.tensor_scalar(ve1[:, b0:b1], mv1[:, b0:b1, 1], EPS, None, ALU.add).then_inc(ln1_var, 1)

            ve.wait_ge(x_in0, 16)
            stats(0, 2)
            ve.wait_ge(small_in, 32)
            link(nc.vector.tensor_copy(mask_f[:, :], mask_u[:, :].bitcast(U8)))
            ve.wait_ge(rs1_ok, 1)
            link(nc.vector.tensor_tensor(rm1[:, 0:2], rs1[:, 0:2], mask_f[:, 0:2], ALU.mult))

            def norm1(g):
                b = g.n(2, 2)
                for j in range(2):
                    at = b + j
                    if isinstance(at, int):
                        src, mean, rstd = x_all[:, at, :], mv1[:, at, 0:1], rm1[:, at:at + 1]
                    else:
                        src = x_all[:, bass.ds(at, 1), :].rearrange("p a d -> p (a d)")
                        mean = mv1[:, bass.ds(at, 1), 0:1].rearrange("p a d -> p (a d)")
                        rstd = rm1[:, bass.ds(at, 1)]
                    nc.vector.tensor_scalar(xn[:, j, :], src, mean, rstd, ALU.subtract, ALU.mult).then_inc(xn_ok, 1)

            def maxima(g, j, h, d=0):
                ve.wait_ge(s_done, g.n(4, d, 2 * j + h + 1))
                nc.vector.reduce_max(mx[:, 8 * h:8 * h + 8], ps_s, AX_X).then_inc(max_ok, 1)

            def pieces(g, j, d=0):
                ve.wait_ge(max_ok, g.n(4, d, 2 * j + 2))
                if not (isinstance(g.i, int) and g.c + d == 0 and j == 0):
                    ve.wait_ge(maxt_done, g.n(2, d, j))
                link(nc.vector.tensor_scalar(mx_pc[:, 0, :], mx[:, :], -1.0, None, ALU.mult))
                link(nc.vector.scalar_tensor_tensor(mx_rest[:, :], mx[:, :], -1.0, mx_pc[:, 0, :],
                                                    ALU.mult, ALU.subtract))
                link(nc.vector.tensor_copy(mx_pc[:, 1, :], mx_rest[:, :]))
                nc.vector.tensor_tensor(mx_pc[:, 2, :], mx_rest[:, :], mx_pc[:, 1, :],
                                        ALU.subtract).then_inc(pieces_ok, 1)

            def attended(g, j):
                ve.wait_ge(pv_done, g.n(4, 0, 2 * j + 2))
                o = ps_o[:, 0:VW * HEADS].rearrange("p (h e) -> p h e", e=VW)
                link(nc.vector.reciprocal(rsum[:, :], o[:, :, HD]))
                link(nc.vector.tensor_scalar(rsg[:, :], rsum[:, :], tg[:, 0:1], None, ALU.mult))
                nc.vector.tensor_tensor(att[:, :].rearrange("p (h e) -> p h e", e=HD), o[:, :, 0:HD],
                                        rsg[:, :].unsqueeze(2).broadcast_to([P, HEADS, HD]),
                                        ALU.mult).then_inc(o_read, 1)
                ve.wait_ge(o_read, g.n(2, 0, j + 1))
                b = g.n(2, 0, j)
                xb = x_all[:, b, :] if isinstance(b, int) else x_all[:, bass.ds(b, 1), :].rearrange("p a d -> p (a d)")
                link(nc.vector.tensor_tensor(xb, xb, att[:, :], ALU.add))
                link(nc.vector.bn_stats(st2[:, :], xb))
                link(nc.vector.bn_aggr(mv2[:, j, :], st2[:, :]))
                nc.vector.tensor_scalar(ve2[:, j:j + 1], mv2[:, j, 1:2], EPS, None, ALU.add).then_inc(ln2_var, 1)

            def norm2(g, j, d=0):
                par = (g.c + d) % 2
                ve.wait_ge(rs2_ok, g.n(2, d, j + 1))
                if j == 0 and g.c + d >= 1:
                    ve.wait_ge(scat[par], g.turns(64, d - 2) + 16 * par)
                b = g.n(2, d, j)
                xb = x_all[:, b, :] if isinstance(b, int) else x_all[:, bass.ds(b, 1), :].rearrange("p a d -> p (a d)")
                nc.vector.tensor_scalar(row_s[:, par, 2 * j, 0:D], xb, mv2[:, j, 0:1], rs2[:, j:j + 1],
                                        ALU.subtract, ALU.mult).then_inc(xn2_ok, 1)

            def body(g, now, soon, later, past):
                pp = 1 - g.par
                if past:
                    norm2(g, 1, -1)
                if now:
                    maxima(g, 1, 0)
                if soon:
                    ve.wait_ge(k1_ok, g.n(1, 2))
                    if now:
                        ve.wait_ge(k3_ok, g.n(1, 1))
                    nc.vector.tensor_tensor(k_rest[:, :], ps[:, 6, :], k_pc[:, 0, :], ALU.subtract).then_inc(kr_ok, 1)
                if now:
                    maxima(g, 1, 1)
                    pieces(g, 1)
                if past:
                    ve.wait_ge(router_done, g.n(1))
                    nc.vector.tensor_copy(lg[:, :, :], ps_c[:, 0:2 * NV].rearrange("p (j e) -> p j e", j=2)[:, :, 0:8]
                                          ).then_inc(lg_read, 1)
                    ve.wait_ge(const_ok, 9)
                    ve.wait_ge(lg_read, g.n(1))
                    nc.vector.max(top[:, 0, :], lg[:, 0, :]).then_inc(dve_link, 1)
                    links[0] += 1
                    link(nc.vector.max(top[:, 1, :], lg[:, 1, :]))
                    nc.vector.tensor_tensor(dif[:, :, :], top[:, :, 1:2], top[:, :, 0:1],
                                            ALU.subtract).then_inc(dif_ok, 1)
                    nc.vector.max_index(topi[:, 0, :], top[:, 0, :], lg[:, 0, :]).then_inc(dve_link, 1)
                    links[0] += 1
                    link(nc.vector.max_index(topi[:, 1, :], top[:, 1, :], lg[:, 1, :]))
                    link(nc.vector.tensor_copy(idx_f[:, :].rearrange("p (j k) -> p j k", j=2), topi[:, :, 0:2]))
                    link(nc.vector.tensor_tensor(oh[:, :, :, :].rearrange("p j k e -> p (j k) e"),
                                                 e_f[:, :].unsqueeze(1).broadcast_to([P, 4, 8]),
                                                 idx_f[:, :].unsqueeze(2).broadcast_to([P, 4, 8]), ALU.is_equal))
                    ve.wait_ge(cum_ok, g.n(1))
                    link(nc.vector.tensor_tensor(cnt[:, :, :], oh[:, :, 0, :], oh[:, :, 1, :], ALU.add))
                    nc.vector.tensor_tensor(cum[:, 1, :], cum[:, 0, :], cnt[:, 0, :], ALU.add).then_inc(oh_ok, 1)
                if later:
                    if g.c == -1:
                        ve.wait_ge(rs1_ok, 2)
                        link(nc.vector.tensor_tensor(rm1[:, 2:4], rs1[:, 2:4], mask_f[:, 2:4], ALU.mult))
                    if g.c == 0:
                        ve.wait_ge(rs1_ok, 3)
                        link(nc.vector.tensor_tensor(rm1[:, 4:B], rs1[:, 4:B], mask_f[:, 4:B], ALU.mult))
                    if g.c >= -1:
                        ve.wait_ge(xnt_done, g.n(1, 2))
                    norm1(g)
                if past:
                    ve.wait_ge(ex_ok, g.n(1))
                    link(nc.vector.tensor_scalar(den[:, :, :], ex[:, :, :], 1.0, None, ALU.add))
                    link(nc.vector.reciprocal(sc1[:, :, :], den[:, :, :]))
                    rows = row_s[:, pp, :, :].rearrange("p (j k) c -> p j k c", j=2)
                    link(nc.vector.tensor_scalar(rows[:, :, 0, D + 1:D + 2], sc1[:, :, :], tg[:, 1:2], None, ALU.mult))
                    nc.vector.tensor_tensor(rows[:, :, 1, D + 1:D + 2], rows[:, :, 0, D + 1:D + 2], ex[:, :, :],
                                            ALU.mult).then_inc(dve_link, 1)
                    links[0] += 1
                    link(nc.vector.tensor_copy(row_s[:, pp, :, D], dest_f[:, :]))
                    link(nc.vector.tensor_scalar(dest_f[:, :], dest_f[:, :], float(-TG), None, ALU.add))
                if now:
                    attended(g, 0)
                if past:
                    ve.wait_ge(pos_done, g.n(1))
                    nc.vector.tensor_tensor(slot[:, :, :], ps_c[:, 192:208].rearrange("p (j e) -> p j e", j=2),
                                            er_f[:, :].unsqueeze(1).broadcast_to([P, 2, 8]), ALU.add
                                            ).then_inc(pos_read, 1)
                    ve.wait_ge(pos_read, g.n(1))
                    link(nc.vector.tensor_tensor(slot_p[:, :, :, :], oh[:, :, :, :],
                                                 slot[:, :, :].unsqueeze(2).broadcast_to([P, 2, 2, 8]), ALU.mult))
                    link(nc.vector.reduce_sum(slot_f[:, :], slot_p[:, :, :, :].rearrange("p j k e -> p (j k) e"), AX_X))
                    nc.vector.tensor_copy(slot_u[:, pp, :], slot_f[:, :]).then_inc(slots_ok, 1)
                    nc.vector.tensor_tensor(cum[:, 0, :], cum[:, 1, :], cnt[:, 1, :], ALU.add).then_inc(cum_ok, 1)
                if now:
                    norm2(g, 0)
                if g.c == -2:
                    nc.vector.memset(k_f[96:99, :], TWO_ONES).then_inc(kones_ok, 1)
                    ve.wait_ge(x_in1, 16)
                    stats(2, 4)
                if soon:
                    maxima(g, 0, 0, 1)
                if later:
                    ve.wait_ge(q1_ok, g.n(1, 3))
                    if g.c >= -1:
                        ve.wait_ge(q3_ok, g.n(1, 2))
                    nc.vector.tensor_tensor(q_rest[:, :], ps[:, 6, :], q_pc[:, 0, :], ALU.subtract).then_inc(qr_ok, 1)
                if soon:
                    maxima(g, 0, 1, 1)
                    pieces(g, 0, 1)
                if now:
                    attended(g, 1)
                if g.c == -2:
                    nc.vector.memset(v_s[:, :, :, :], 1.0).then_inc(v_ones_ok, 1)
                if g.c == -1:
                    ve.wait_ge(x_rest, 16)
                    stats(4, B)
                    ve.wait_ge(tanh_ok, 1)
                    ve.wait_ge(const_ok, 9)
                    nc.vector.tensor_copy(e_f[:, :], e_i[:, :]).then_inc(dve_link, 1)
                    nc.vector.tensor_copy(t_f[:, :], t_i[:, :]).then_inc(dve_link, 1)
                    links[0] += 2
                    link(nc.vector.tensor_copy(dest_f[:, :], dest_i[:, :]))
                    link(nc.vector.tensor_scalar(er_f[:, :], e_f[:, :], float(R), None, ALU.mult))
                relink()

            relink()
            attention_steps(ve, body)

            ve.wait_ge(total_done, 1)
            link(nc.vector.tensor_copy(c_f[:, :], ps_c[0:1, 224:232]))
            nc.vector.tensor_tensor(pad_f[:, :], er_f[0:1, :], c_f[:, :], ALU.add).then_inc(dve_link, 1)
            links[0] += 1
            link(nc.vector.tensor_scalar(c_up[:, :], c_f[:, :], float(P - 1), None, ALU.add))
            link(nc.vector.tensor_copy(pad_i[:, :], pad_f[:, :]))
            link(nc.vector.tensor_scalar(c_sh[:, :], c_up[:, :], 7, None, ALU.logical_shift_right))
            link(nc.vector.tensor_copy(nt_f[:, :], c_sh[:, :]))
            link(nc.vector.tensor_tensor(end_m[:, :, :], tri_f[:, :, :],
                                         nt_f[:, :].unsqueeze(1).broadcast_to([1, 8, 8]), ALU.mult))
            link(nc.vector.reduce_sum(end_f[:, :], end_m[:, :, :], AX_X))
            nc.vector.tensor_scalar(jump[:, :], nt_f[:, :], float(-P), float(R), ALU.mult, ALU.add
                                    ).then_inc(dve_link, 1)
            links[0] += 1
            link(nc.vector.tensor_tensor(past[:, :, :], t_f[:, :].unsqueeze(2).broadcast_to([1, NT, 8]),
                                         end_f[:, :].unsqueeze(1).broadcast_to([1, NT, 8]), ALU.is_ge))
            nc.vector.tensor_tensor(past_j[:, :, :], past[:, :, :],
                                    jump[:, :].unsqueeze(1).broadcast_to([1, NT, 8]), ALU.mult
                                    ).then_inc(dve_link, 1)
            links[0] += 1
            link(nc.vector.reduce_sum(eid_f[:, :], past[:, :, :], AX_X))
            link(nc.vector.reduce_sum(base_f[:, :], past_j[:, :, :], AX_X))
            link(nc.vector.scalar_tensor_tensor(base_g[:, :], t_f[:, :], float(P), base_f[:, :], ALU.mult, ALU.add))
            link(nc.vector.tensor_scalar(eid_i[:, :], eid_f[:, :], float(E - 1), None, ALU.min))
            nc.vector.tensor_scalar(base_i[:, :], base_g[:, :], float(NULL_ROW), None, ALU.min).then_inc(table_ok, 1)

            def shared(c):
                def times(j):
                    ve.wait_ge(sil_ok, c * NJ + j + 1)
                    if j == 0 and not isinstance(c, int):
                        ve.wait_ge(down_done, c * CH)
                    nc.vector.tensor_tensor(hid[:, j, :], ps[:, 2 + j % 2, :], sil_sh[:, j % 2], ALU.mult
                                            ).then_inc(hid_ok, 1)
                for j in range(NJ):
                    times(j)
                for t in range(CH):
                    ve.wait_ge(down_done, c * CH + t + 1)
                    at = c * CH + t
                    xb = x_all[:, at, :] if isinstance(at, int) else x_all[:, bass.ds(at, 1), :].rearrange(
                        "p a d -> p (a d)")
                    nc.vector.scalar_tensor_tensor(xb, ps[:, 4 + t, 0:D], tg[:, 1:2], xb, ALU.mult, ALU.add
                                                   ).then_inc(base_ok, 1)

            shared(0)

            def expert_dst(t, r):
                ve.wait_ge(tile_in[r], (t // 4 + 1) * 16 if isinstance(t, int) else turn[0] * 16 + turn[1])
                if not (isinstance(t, int) and t < 4):
                    ve.wait_ge(ysc[r], (t // 4) * 16 if isinstance(t, int) else turn[0] * 16 + turn[1] - 16)
                nc.vector.tensor_scalar(dst_u[:, r:r + 1], xs_in[:, r, D:D + 1], -1.0, float(2 * T),
                                        ALU.mult, ALU.add).then_inc(dst_ok, 1)

            turn = [None, 0]

            def expert_act(t, r):
                par = r % 2
                ve.wait_ge(silm_ok, t + 1)
                if not (isinstance(t, int) and t < 2):
                    ve.wait_ge(actt_done, t - 1)
                nc.vector.tensor_tensor(act[:, par], ps[:, 2 + par, FI:2 * FI], sil[:, par], ALU.mult
                                        ).then_inc(act_ok, 1)

            def expert_actt(t, r):
                par = r % 2
                ve.wait_ge(actt_done, t + 1)
                if not (isinstance(t, int) and t < 2):
                    ve.wait_ge(y_done, t - 1)
                nc.vector.tensor_copy(act_t[:, par], ps[:, 4, 0:2 * P].rearrange("p (k t) -> p k t", k=2)
                                      ).then_inc(actt_ok, 1)

            def step(t, r):
                expert_actt(t, r)
                if not isinstance(t, int) or t + 1 < NT:
                    expert_act(t + 1, (r + 1) % 4)
                    turn[1] = 16 if r < 3 else 32
                    expert_dst(t + 1, (r + 1) % 4)

            expert_act(0, 0)
            expert_dst(0, 0)
            for r in range(4):
                step(r, r)
            with ve.Fori(1, MOE_LOOP) as i:
                turn[0] = i
                for r in range(4):
                    step(i * 4 + r, r)
            for t in range(4 * MOE_LOOP, NT):
                step(t, t % 4)

            with ve.Fori(1, NCH) as c:
                shared(c)
            for c in range(NCH):
                ve.wait_ge(y_got[c % 2], 32 * (c // 2 + 1))
                xc = x_all[:, CH * c:CH * c + CH, :]
                ve.wait_ge(base_ok, CH * (c + 1))
                link(nc.vector.tensor_tensor(xc, xc, y_in[:, c % 2, 0], ALU.add))
                nc.vector.tensor_tensor(xc, xc, y_in[:, c % 2, 1], ALU.add).then_inc(fin_ok, 1)

        @block.tensor
        def _(pe):
            def body(g, now, soon, later, past):
                pn = 1 - g.par

                def scores(j, h, d=0):
                    par = (g.c + d) % 2
                    if not (isinstance(g.i, int) and g.c + d == 0 and j == 0 and h == 0):
                        pe.wait_ge(max_ok, g.n(4, d, 2 * j + h))
                    for n in range(8):
                        at = (slice(0, 96), par, 8 * h + n, slice(P * j, P * j + P))
                        last = nc.tensor.matmul(ps_s[:, n, :], q_st[at], k_st[at], start=True, stop=True)
                    last.then_inc(s_done, 1)

                def scores_t(j, h):
                    if h == 0:
                        pe.wait_ge(rows_in[j], g.n(16, 1))
                    if not (isinstance(g.i, int) and g.c == 0 and j == 0 and h == 0):
                        pe.wait_ge(probs_ok, g.n(4, 0, 2 * j + h))
                    for n in range(8):
                        at = (slice(0, 99), g.par, 8 * h + n, slice(P * j, P * j + P))
                        last = nc.tensor.matmul(ps_t[:, n, :], k_st[at], q_st[at], start=True, stop=True)
                    last.then_inc(st_done, 1)

                def values(j, h):
                    pe.wait_ge(probs_ok, g.n(4, 0, 2 * j + h + 1))
                    if h == 0 and not (isinstance(g.i, int) and g.c == 0 and j == 0):
                        pe.wait_ge(o_read, g.n(2, 0, j))
                    if h == 0 and j == 0:
                        pe.wait_ge(v_ok, g.n(1, 1))
                    for n in range(8):
                        c = VW * (8 * h + n)
                        last = nc.tensor.matmul(ps_o[:, c:c + NV], probs[:, 2 * j + h, n, :],
                                                v_s[:, g.par, j, c:c + NV], start=True, stop=True)
                    last.then_inc(pv_done, 1)

                def max_rows(j, d, bank_read):
                    ready, read = held(pe, g.n(2, d, j + 1)), held(pe, g.n(1))
                    pe.wait_ge(const_ok, 9)
                    if g.c == -1:
                        pe.wait_ge(tanh_ok, 1)
                    if past:
                        pe.wait_ge(bank_read, read)
                    pe.wait_ge(pieces_ok, ready)
                    nc.tensor.matmul(ps_m, mx_pc[:, :, :].rearrange("p c h -> p (c h)"), ident_b[:, :],
                                     is_transpose=True, start=True, stop=True).then_inc(maxt_done, 1)

                if now:
                    scores(1, 0)
                if past:
                    pe.wait_ge(xn2_ok, g.n(2))
                    if now:
                        pe.wait_ge(maxt_ok, g.n(2, 0, 1))
                    else:
                        pe.wait_ge(maxt_ok, g.n(2))
                        pe.wait_ge(pos_read, g.n(1, -1))
                    for k in range(2):
                        for j in range(2):
                            last = nc.tensor.matmul(ps_x[:, k, P * j:P * j + P],
                                                    row_s[:, pn, 2 * j, P * k:P * k + P], ident[:, :],
                                                    is_transpose=True, start=True, stop=True)
                    last.then_inc(x2t_done, 1)
                if now:
                    scores(1, 1)
                if past:
                    if g.c == 1 or not now:
                        pe.wait_ge(wr_in, 16)
                    pe.wait_ge(xt_ok, g.n(1))
                    for j in range(2):
                        for k in range(2):
                            last = nc.tensor.matmul(ps_c[:, NV * j:NV * j + NV], xt_grp[:, k, P * j:P * j + P],
                                                    wr_s[:, k, :], start=k == 0, stop=k == 1)
                    last.then_inc(router_done, 1)
                if now:
                    if g.c == 0:
                        pe.wait_ge(kones_ok, 1)
                    scores_t(0, 0)
                if soon:
                    if g.c == -1:
                        pe.wait_ge(wv_in, 16)
                    if now:
                        pe.wait_ge(v_ok, g.n(1, 1))
                    for j in range(2):
                        for k in range(2):
                            last = nc.tensor.matmul(ps[:, 5, D * j:D * j + D], ctx_s[:, pn, k, P * j:P * j + P],
                                                    wv_s[:, k, :], start=k == 0, stop=k == 1)
                    last.then_inc(v_done, 1)
                if now:
                    max_rows(1, 0, lg_read)
                    scores_t(0, 1)
                    values(0, 0)
                    values(0, 1)
                if later:
                    if g.c == -2:
                        pe.wait_ge(const_ok, 9)
                    pe.wait_ge(xn_ok, g.n(2, 3))
                    if g.c >= -1:
                        pe.wait_ge(kr_ok, g.n(1, 2))
                    for k in range(2):
                        for j in range(2):
                            last = nc.tensor.matmul(ps_b[:, k, P * j:P * j + P], xn[:, j, P * k:P * k + P],
                                                    ident[:, :], is_transpose=True, start=True, stop=True)
                    last.then_inc(xnt_done, 1)
                if now:
                    scores_t(1, 0)
                if past:
                    pe.wait_ge(oh_ok, g.n(1))
                    if now:
                        pe.wait_ge(maxt_ok, g.n(2, 1))
                    for j in range(2):
                        nc.tensor.matmul(ps_c[:, 192 + 8 * j:200 + 8 * j], before[:, :], cnt[:, j, :],
                                         start=True, stop=False)
                        last = nc.tensor.matmul(ps_c[:, 192 + 8 * j:200 + 8 * j], ones_b[:, :], cum[:, j, :],
                                                start=False, stop=True)
                    last.then_inc(pos_done, 1)
                if later:
                    if g.c == -2:
                        pe.wait_ge(wq_in, 16)
                    pe.wait_ge(xnt_ok, g.n(1, 3))
                    for c in range(2):
                        for k in range(2):
                            last = nc.tensor.matmul(ps_b[:, c, :], wq_s[:, k, c, :], xn_t[:, k, :],
                                                    start=k == 0, stop=k == 1)
                    last.then_inc(q_done, 1)
                if soon:
                    pe.wait_ge(qst[pn], g.turns(96, 1))
                    pe.wait_ge(kst[pn], g.turns(96, 1))
                    scores(0, 0, 1)
                if now:
                    scores_t(1, 1)
                    values(1, 0)
                if soon:
                    scores(0, 1, 1)
                if now:
                    values(1, 1)
                if soon:
                    max_rows(0, 1, pos_read)
                if later:
                    if g.c == -2:
                        pe.wait_ge(wk_in, 16)
                    pe.wait_ge(ctx_in[g.par], g.turns(16, 2))
                    pe.wait_ge(qr_ok, g.n(1, 3))
                    for c in range(2):
                        for k in range(2):
                            last = nc.tensor.matmul(ps_b[:, c, :], wk_s[:, k, c, :], ctx_s[:, g.par, k, :],
                                                    start=k == 0, stop=k == 1)
                    last.then_inc(k_done, 1)
                if g.c == -2:
                    pe.wait_ge(small_in, 32)
                    nc.tensor.matmul(ps_c[:, 0:2], ones_r[:, :], gate_r[:, :], start=True, stop=True
                                     ).then_inc(gates_done, 1)

            attention_steps(pe, body)

            pe.wait_ge(cum_ok, G + 1)
            nc.tensor.matmul(ps_c[:, 224:232], ones_b[:, :], cum[:, 0, :], start=True, stop=True
                             ).then_inc(total_done, 1)
            pe.wait_ge(ffn_in, 48)
            pe.wait_ge(xt_out, 16 * (G + 1))
            pe.wait_ge(table_ok, 1)

            def shared(c):
                at = c * (CH * P)
                xt = xt_all[:, :, 0:CH * P] if isinstance(c, int) else xt_all[:, :, bass.ds(at, CH * P)]

                def gate_up(j):
                    if j >= 2:
                        pe.wait_ge(hid_ok, c * NJ + j - 1)
                    elif not isinstance(c, int):
                        pe.wait_ge(hid_ok, c * NJ + j - 1)
                    for w, bank in ((gate_s, j % 2), (up_s, 2 + j % 2)):
                        for k in range(2):
                            last = nc.tensor.matmul(ps[:, bank, :], w[:, k, P * j:P * j + P], xt[:, k, :],
                                                    start=k == 0, stop=k == 1)
                    last.then_inc(gu_done, 1)

                def down(j):
                    pe.wait_ge(hid_ok, c * NJ + j + 1)
                    if j == 0 and not isinstance(c, int):
                        pe.wait_ge(base_ok, c * CH)
                    for t in range(CH):
                        last = nc.tensor.matmul(ps[:, 4 + t, 0:D], hid[:, j, P * t:P * t + P], down_s[:, j, :],
                                                start=j == 0, stop=j == NJ - 1)
                        if j == NJ - 1:
                            last.then_inc(down_done, 1)

                gate_up(0)
                for j in range(1, NJ):
                    gate_up(j)
                    down(j - 1)
                down(NJ - 1)

            shared(0)
            pe.wait_ge(base_ok, CH)
            pe.wait_ge(fc1_in, 16 * E)
            pe.wait_ge(fc2_in, 16 * E)

            turn = [None, 0]

            def expert_x(t, r):
                par = r % 2
                pe.wait_ge(tile_in[r], (t // 4 + 1) * 16 if isinstance(t, int) else turn[0] * 16 + turn[1])
                if not (isinstance(t, int) and t < 2):
                    pe.wait_ge(xst_ok, t - 1)
                for k in range(2):
                    last = nc.tensor.matmul(ps[:, par, P * k:P * k + P], xs_in[:, r, P * k:P * k + P], ident[:, :],
                                            is_transpose=True, start=True, stop=True)
                last.then_inc(xst_done, 1)

            def experts_of(t, n):
                at = eid_i[0:1, t:t + n] if isinstance(t, int) else eid_i[0:1, bass.ds(t, n)]
                _, values = nc.values_load_multi_w_load_instructions(
                    at, engines=[mybir.EngineType.PE], min_val=0, max_val=E - 1)
                return values

            def expert_h(t, r, e):
                par = r % 2
                pe.wait_ge(xst_ok, t + 1)
                if not (isinstance(t, int) and t < 2):
                    pe.wait_ge(act_ok, t - 1)
                for k in range(2):
                    w = fc1_s[:, bass.ds(e * 2 + k, 1), :].rearrange("p a n -> p (a n)")
                    last = nc.tensor.matmul(ps[:, 2 + par, :], xs_t[:, par, k, :], w, start=k == 0, stop=k == 1)
                last.then_inc(h_done, 1)

            def expert_at(t, r):
                par = r % 2
                pe.wait_ge(act_ok, t + 1)
                if not (isinstance(t, int) and t < 1):
                    pe.wait_ge(actt_ok, t)
                for k in range(2):
                    last = nc.tensor.matmul(ps[:, 4, P * k:P * k + P], act[:, par, P * k:P * k + P], ident[:, :],
                                            is_transpose=True, start=True, stop=True)
                last.then_inc(actt_done, 1)

            def expert_y(t, r, e):
                par = r % 2
                pe.wait_ge(actt_ok, t + 1)
                if not (isinstance(t, int) and t < 2):
                    pe.wait_ge(y_ok, t - 1)
                for k in range(2):
                    w = fc2_s[:, bass.ds(e * 2 + k, 1), :].rearrange("p a n -> p (a n)")
                    last = nc.tensor.matmul(ps[:, 5 + par, 0:D], act_t[:, par, k, :], w, start=k == 0, stop=k == 1)
                last.then_inc(y_done, 1)

            def step(t, r, e, e_next):
                if not isinstance(t, int) or t + 2 < NT:
                    turn[1] = 16 if r < 2 else 32
                    expert_x(t + 2, (r + 2) % 4)
                expert_at(t, r)
                if not isinstance(t, int) or t + 1 < NT:
                    expert_h(t + 1, (r + 1) % 4, e_next)
                expert_y(t, r, e)

            ids = experts_of(0, 5)
            expert_x(0, 0)
            expert_x(1, 1)
            expert_h(0, 0, ids[0])
            for r in range(4):
                step(r, r, ids[r], ids[r + 1])
            with pe.Fori(1, MOE_LOOP) as i:
                turn[0] = i
                ids = experts_of(i * 4, 5)
                for r in range(4):
                    step(i * 4 + r, r, ids[r], ids[r + 1])
            ids = list(experts_of(4 * MOE_LOOP, NT - 4 * MOE_LOOP)) + [None]
            for t in range(4 * MOE_LOOP, NT):
                step(t, t % 4, ids[t - 4 * MOE_LOOP], ids[t - 4 * MOE_LOOP + 1])

            pe.wait_ge(y_ok, NT)
            with pe.Fori(1, NCH) as c:
                shared(c)



def kernel(x, ctx_768, mask_BxS_bk0, g_xattn, g_ffn, L0_xattn_Wq, L0_xattn_Wkv, L0_ffn_w_router,
           L0_ffn_fc1_w, L0_ffn_fc2_w, L0_ffn_gate_w, L0_ffn_up_w, L0_ffn_down_w):
    import numpy as np
    import concourse.bacc as bacc
    from concourse.bass_utils import run_bass_kernel_spmd

    def tiles(w, p):
        w = np.asarray(w)
        w = w.reshape(*w.shape[:-2], w.shape[-2] // p, p, w.shape[-1])
        return np.moveaxis(w, -2, 0)

    x = np.asarray(x)
    ctx_768 = np.asarray(ctx_768)
    batch, seq, d = x.shape
    cy = ctx_768.shape[2]
    kc = cy // 2
    w_q, w_kv = np.asarray(L0_xattn_Wq), np.asarray(L0_xattn_Wkv)
    fc1, fc2 = tiles(L0_ffn_fc1_w, 128), tiles(L0_ffn_fc2_w, 128)
    arrays = {
        "x": x.reshape(batch * seq, d),
        "ctx_t": ctx_768.reshape(batch * seq, 2, kc).transpose(2, 1, 0),
        "mask": np.ascontiguousarray(np.asarray(mask_BxS_bk0).T).view(np.uint32),
        "gates": np.stack([np.asarray(g_xattn), np.asarray(g_ffn)], axis=1),
        "wq": w_q.reshape(8, 2, 16, 2, 128).transpose(4, 3, 1, 2, 0).reshape(128, 2, 2, 128),
        "wk": w_kv[:d].reshape(8, 2, 16, 2, kc).transpose(4, 3, 1, 2, 0).reshape(kc, 2, 2, 128),
        "wv": w_kv[d:].reshape(d, 2, kc).transpose(2, 1, 0),
        "w_router": tiles(L0_ffn_w_router, 128),
        "fc1": fc1.reshape(128, -1, fc1.shape[-1]),
        "fc2": fc2.reshape(128, -1, fc2.shape[-1]),
        "gate_w": tiles(L0_ffn_gate_w, 128),
        "up_w": tiles(L0_ffn_up_w, 128),
        "down_w": tiles(L0_ffn_down_w, 128),
    }
    arrays = {f"in_{n}": np.ascontiguousarray(a) for n, a in arrays.items()}
    nc = bacc.Bacc("TRN2", target_bir_lowering=False, num_devices=1)
    args = [nc.dram_tensor(n, a.shape, mybir.dt.from_np(a.dtype), kind="ExternalInput").ap()
            for n, a in arrays.items()]
    out = nc.dram_tensor("out", (batch * seq, d), F32, kind="ExternalOutput").ap()
    build_program(nc, *args, out)
    r = run_bass_kernel_spmd(nc, [arrays], core_ids=[0])
    return r.results[0]["out"].reshape(batch, seq, d)
```

```python
from contextlib import ExitStack

import numpy as np

import concourse.bass as bass
from concourse import mybir

ALU = mybir.AluOpType
ACT = mybir.ActivationFunctionType
F32 = mybir.dt.float32
F32R = mybir.dt.float32r
BF16 = mybir.dt.bfloat16
I32 = mybir.dt.int32
U32 = mybir.dt.uint32
U8 = mybir.dt.uint8
AX_X = mybir.AxisListType.X

P = 128
HEADS = 16
HD = 16
PIECES = 6
VW = HD + 1
NV = 96
Q_SLOTS = [(0, 0), (1, 1), (2, 2), (3, 0), (4, 1), (5, 0)]
K_SLOTS = [(0, 0), (1, 0), (2, 0), (3, 1), (4, 1), (5, 2)]
TURN = 8
CLAMPED = "the tables are clamped to this range on the chip"
HEAD = 5
EPS = 1e-5
TWO_ONES = float(np.array([0x3F803F80], np.uint32).view(np.float32)[0])


class Group:

    def __init__(self, i, c):
        self.i, self.c = i, c
        self.par = c % 2

    def n(self, k, d=0, plus=0):
        const = k * (self.c + d) + plus
        return const if isinstance(self.i, int) else self.i * (2 * k) + const

    def turns(self, k, d=0):
        const = k * ((self.c + d) // 2 + 1)
        return const if isinstance(self.i, int) else self.i * k + const


class Tile:

    def __init__(self, i, c):
        self.i, self.c = i, c

    def n(self, plus=0):
        return self.c + plus if isinstance(self.i, int) else self.i * TURN + (self.c + plus)

    def laps(self, d, more=0):
        const = 16 * ((self.c + d) // 4 + more)
        return const if isinstance(self.i, int) else self.i * (4 * TURN) + const

    def since(self, first):
        return not isinstance(self.i, int) or self.c >= first


def build_program(nc, x, ctx_t, mask, gates, wq, wk, wv, w_router, fc1, fc2, gate_w, up_w, down_w, out):
    T, D = x.shape
    B = T // P
    G = B // 2
    TG = 2 * P
    KC = ctx_t.shape[0]
    E = w_router.shape[2]
    FI = fc1.shape[2] // 2
    ISH = gate_w.shape[2]
    R = T + P
    NULL_ROW = E * R
    NT = (2 * T + E * (P - 1)) // P
    ROW = D + 2
    CH = 4
    NCH = B // CH
    NJ = ISH // P

    xs = nc.dram_tensor("dispatched", (NULL_ROW + P, ROW), F32, kind="Internal").ap()
    ys = nc.dram_tensor("expert_rows", (2 * T, D), F32, kind="Internal").ap()
    x_view = x.rearrange("(b p) d -> p b d", p=P)
    out_view = out.rearrange("(b p) d -> p b d", p=P)
    y_view = ys.rearrange("(k b p) d -> p k b d", k=2, p=P)

    with ExitStack() as es:
        start = {}

        def sb(name, shape, dt=F32):
            start[name] = nc.sbuf_base
            return es.enter_context(nc.sbuf_tensor(name, shape, dt))

        def over(name, place, shape, words=0):
            return nc.alloc_sbuf_tensor_at(name, shape, F32R, offset=start[place] + 4 * words)

        def sem(name):
            return es.enter_context(nc.semaphore(name))

        wq_s = sb("wq_s", [P, 2, 2, P])
        wk_s = sb("wk_s", [KC, 2, 2, P])
        wv_s = sb("wv_s", [KC, 2, D])
        wr_s = sb("wr_s", [P, 2, NV])
        fc1_s = sb("fc1_s", [P, 2 * E, 2 * FI])
        fc2_s = sb("fc2_s", [P, 2 * E, D])
        gate_s = sb("gate_s", [P, 2, ISH])
        up_s = sb("up_s", [P, 2, ISH])
        down_s = sb("down_s", [P, NJ, D])
        x_all = sb("x_all", [P, B, D])
        xt_all = sb("xt_all", [P, 2, T])
        ctx_s = sb("ctx_s", [KC, 2, 2, TG])
        work = sb("work", [P, 7 * TG * 2])
        xn = work[:, 0:2 * D].rearrange("p (j d) -> p j d", j=2)
        xn_t = work[:, 2 * D:4 * D].rearrange("p (k t) -> p k t", k=2)
        q_rest = work[:, 4 * D:6 * D]
        k_rest = work[:, 6 * D:8 * D]
        q_pc = work[:, 8 * D:11 * D].bitcast(BF16).rearrange("p (s t) -> p s t", s=3)
        k_pc = work[:, 11 * D:14 * D].bitcast(BF16).rearrange("p (s t) -> p s t", s=3)
        stacks = sb("stacks", [P, 2, 2, HEADS, TG], BF16)
        q_st, k_st = stacks[:, 0], stacks[:, 1]
        v_s = sb("v_s", [P, 2, 2, VW * (HEADS - 1) + NV + 1])
        probs = sb("probs", [P, 4, 8, P])
        row_s = sb("row_s", [P, 2, 4, ROW])
        xt_grp = sb("xt_grp", [P, 2, TG])
        att = sb("att", [P, D])
        hid_0 = sb("hid_0", [P, NJ, CH * P])
        sig_0 = sb("sig_0", [P, 2, CH * P])
        ident = sb("ident", [P, P])
        ident_b = sb("ident_b", [P, P], BF16)
        before = sb("before", [P, P], BF16)
        ones_b = sb("ones_b", [P, P], BF16)
        ones_r = sb("ones_r", [1, P])
        mask_u = sb("mask_u", [P, B // 4], U32)
        mask_f = sb("mask_f", [P, B])
        gate_r = sb("gate_r", [1, 2])
        tg = sb("tg", [P, 2])
        mhalf = sb("mhalf", [P, B])
        st1 = sb("st1", [P, B, 6])
        mv1 = sb("mv1", [P, B, 2])
        ve1 = sb("ve1", [P, B])
        rs1 = sb("rs1", [P, B])
        rm1 = sb("rm1", [P, B])
        st2 = sb("st2", [P, 6])
        mv2 = sb("mv2", [P, 2, 2])
        ve2 = sb("ve2", [P, 2])
        rs2 = sb("rs2", [P, 2])
        mx = sb("mx", [P, HEADS])
        mx_pc = sb("mx_pc", [P, 3, HEADS], BF16)
        mx_rest = sb("mx_rest", [P, HEADS])
        mx_t = sb("mx_t", [3 * HEADS, 2, P], BF16)
        rsum = sb("rsum", [P, HEADS])
        rsg = sb("rsg", [P, HEADS])
        lg = sb("lg", [P, 2, 8])
        top = sb("top", [P, 2, 8])
        topi = sb("topi", [P, 2, 8], U32)
        idx_f = sb("idx_f", [P, 4])
        dif = sb("dif", [P, 2, 1])
        ex = sb("ex", [P, 2, 1])
        den = sb("den", [P, 2, 1])
        sc1 = sb("sc1", [P, 2, 1])
        oh = sb("oh", [P, 2, 2, 8])
        cnt = sb("cnt", [P, 2, 8], BF16)
        cum = sb("cum", [P, 2, 8], BF16)
        slot = sb("slot", [P, 2, 8])
        slot_p = sb("slot_p", [P, 2, 2, 8])
        slot_f = sb("slot_f", [P, 4])
        slot_u = sb("slot_u", [P, 2, 4], U32)
        e_i = sb("e_i", [P, 8], I32)
        e_f = sb("e_f", [P, 8])
        er_f = sb("er_f", [P, 8])
        dest_i = sb("dest_i", [P, 4], I32)
        dest_f = sb("dest_f", [P, 4])
        t_i = sb("t_i", [1, NT], I32)
        t_f = sb("t_f", [1, NT])
        tri_f = sb("tri_f", [1, 8, 8])
        c_f = sb("c_f", [1, 8])
        c_up = sb("c_up", [1, 8], I32)
        c_sh = sb("c_sh", [1, 8], I32)
        nt_f = sb("nt_f", [1, 8])
        end_m = sb("end_m", [1, 8, 8])
        end_f = sb("end_f", [1, 8])
        jump = sb("jump", [1, 8])
        past = sb("past", [1, NT, 8])
        past_j = sb("past_j", [1, NT, 8])
        eid_f = sb("eid_f", [1, NT])
        base_f = sb("base_f", [1, NT])
        base_g = sb("base_g", [1, NT])
        eid_i = sb("eid_i", [1, NT], I32)
        base_i = sb("base_i", [1, NT], I32)
        pad_f = sb("pad_f", [1, 8])
        pad_i = sb("pad_i", [1, 8], I32)
        zrow = sb("zrow", [P, ROW])
        wt = sb("wt", [P, 4])

        st_f = stacks[:, :, :, :, :].rearrange("p s a h t -> p (s a h t)").bitcast(F32)
        q_f, k_f = st_f[:, 0:8192 // 2], st_f[:, 8192 // 2:8192]
        fc1_hi, fc1_lo = over("fc1_hi", "stacks", [P, 2 * E, 2 * FI]), over("fc1_lo", "fc1_s", [P, 2 * E, 2 * FI])
        gate_hi, gate_lo = over("gate_hi", "work", [P, 2, ISH]), over("gate_lo", "gate_s", [P, 2, ISH])
        up_hi, up_lo = over("up_hi", "work", [P, 2, ISH], 2 * ISH), over("up_lo", "up_s", [P, 2, ISH])
        down_hi, down_lo = over("down_hi", "work", [P, NJ, D], 4 * ISH), over("down_lo", "down_s", [P, NJ, D])
        xt_hi = over("xt_hi", "hid_0", [P, 4, CH * P])
        xt_lo = over("xt_lo", "xt_all", [P, 2, T])
        hid_hi = over("hid_hi", "stacks", [P, NJ, CH * P], 4096)
        hid_lo = over("hid_lo", "stacks", [P, NJ, CH * P], 4096 + NJ * CH * P)
        sil_sh = sig_0[:, :, :]
        y_in = [q_f[:, 0:8 * D].rearrange("p (k t d) -> p k t d", k=2, t=CH),
                q_f[:, 8 * D:16 * D].rearrange("p (k t d) -> p k t d", k=2, t=CH)]
        pf = probs[:, :, :, :].rearrange("p a h t -> p (a h t)")
        xs_in = pf[:, 0:4 * ROW].rearrange("p (r c) -> p r c", r=4)
        hid_1 = pf[:, 2048:4096].rearrange("p (j t) -> p j t", j=NJ)
        o0 = 4 * ROW
        xs_hi = over("xs_hi", "probs", [P, 2, 2, P], o0)
        xs_lo = over("xs_lo", "sig_0", [P, 2, 2, P])
        o0 += 4 * P
        sil = pf[:, o0:o0 + 2 * FI].rearrange("p (r c) -> p r c", r=2)
        o0 += 2 * FI
        act = pf[:, o0:o0 + 2 * FI].rearrange("p (r c) -> p r c", r=2)
        o0 += 2 * FI
        act_t = pf[:, o0:o0 + 4 * P].rearrange("p (r k t) -> p r k t", r=2, k=2)
        y_out = v_s[:, :, :, :].rearrange("p a b c -> p (a b c)")[:, 0:4 * D].rearrange("p (r c) -> p r c", r=4)
        dst_u = slot_u[:, 0, :]

        ps = es.enter_context(nc.psum_tensor("ps", [P, 8, 512], F32))
        ps_s = ps[:, 0:2, :].rearrange("p b (h t) -> p (b h) t", h=4)
        ps_t = ps[:, 2:4, :].rearrange("p b (h t) -> p (b h) t", h=4)
        ps_o = ps[:, 4, :]
        ps_a = ps[:, 5, :].rearrange("p (k t) -> p k t", k=2)
        ps_b = ps[:, 6, :].rearrange("p (c t) -> p c t", c=2)
        ps_c = ps[:, 7, :]
        ps_x = ps_c.rearrange("p (k t) -> p k t", k=2)
        ps_m = ps_c[0:3 * HEADS, 256:256 + P // 2].bitcast(BF16)

        sums_0 = [ps[:, 5 + t // 2, D * (t % 2):D * (t % 2) + D] for t in range(CH)]
        sums = [ps[:, 4 + t, 0:D] for t in range(CH)]

        names = """x_in0 x_in1 x_rest ctx_in0 ctx_in1 wq_in wk_in wv_in kones_ok small_in wr_in ffn_in fc1_in fc2_in
            const_ok tanh_ok gates_done zero_row_ok v_ones_ok wr_ok mask_ok
            ln1_var rs1_ok rm1_ok xn_ok xnt_done xnt_ok q_done k_done v_done q1_ok q2_ok q3_ok k1_ok k2_ok k3_ok
            qr_ok kr_ok qst0 qst1 kst0 kst1 v_ok s_done max_ok pieces_ok maxt_done maxt_ok rows_in0 rows_in1
            st_done probs_ok pv_done o_read ln2_var rs2_ok xn2_ok dup_ok x2t_done xt_ok xt_out router_done lg_read
            dif_ok ex_ok oh_ok cum_ok pos_done pos_read slots_ok scat0 scat1 table_ok pad_out
            dve_link pool_link act_link
            gu_done sil_ok hid_ok down_done base_ok
            tile_in0 tile_in1 tile_in2 tile_in3 xst_done xst_ok h_done silm_ok act_ok actt_done actt_ok y_done y_ok
            dst_ok ysc0 ysc1 ysc2 ysc3 y_in0 y_in1 y_added sig_ok out_done
            fhi_ok flo_ok high_ok low_ok xlo_ok prod_ok hhi_ok""".split()
        S = {n: sem(n) for n in names}
        x_in0, x_in1, x_rest = S["x_in0"], S["x_in1"], S["x_rest"]
        wq_in, wk_in, wv_in, kones_ok = S["wq_in"], S["wk_in"], S["wv_in"], S["kones_ok"]
        small_in, wr_in, ffn_in, fc1_in, fc2_in = S["small_in"], S["wr_in"], S["ffn_in"], S["fc1_in"], S["fc2_in"]
        ctx_in = [S["ctx_in0"], S["ctx_in1"]]
        const_ok, tanh_ok, gates_done, zero_row_ok = S["const_ok"], S["tanh_ok"], S["gates_done"], S["zero_row_ok"]
        v_ones_ok, wr_ok, mask_ok, ln1_var, rs1_ok, rm1_ok = (S["v_ones_ok"], S["wr_ok"], S["mask_ok"], S["ln1_var"],
                                                              S["rs1_ok"], S["rm1_ok"])
        xn_ok, xnt_done, xnt_ok, q_done, k_done, v_done = (S["xn_ok"], S["xnt_done"], S["xnt_ok"], S["q_done"],
                                                           S["k_done"], S["v_done"])
        q1_ok, q2_ok, q3_ok, k1_ok, k2_ok, k3_ok = (S["q1_ok"], S["q2_ok"], S["q3_ok"], S["k1_ok"], S["k2_ok"],
                                                    S["k3_ok"])
        qr_ok, kr_ok, v_ok, s_done, max_ok, pieces_ok = (S["qr_ok"], S["kr_ok"], S["v_ok"], S["s_done"], S["max_ok"],
                                                         S["pieces_ok"])
        qst, kst, rows_in = [S["qst0"], S["qst1"]], [S["kst0"], S["kst1"]], [S["rows_in0"], S["rows_in1"]]
        maxt_done, maxt_ok, st_done, probs_ok, pv_done = (S["maxt_done"], S["maxt_ok"], S["st_done"], S["probs_ok"],
                                                          S["pv_done"])
        o_read, ln2_var, rs2_ok, xn2_ok, dup_ok = S["o_read"], S["ln2_var"], S["rs2_ok"], S["xn2_ok"], S["dup_ok"]
        x2t_done, xt_ok, xt_out, router_done, lg_read = (S["x2t_done"], S["xt_ok"], S["xt_out"], S["router_done"],
                                                         S["lg_read"])
        dif_ok, ex_ok, oh_ok, pos_done, pos_read, slots_ok = (S["dif_ok"], S["ex_ok"], S["oh_ok"], S["pos_done"],
                                                              S["pos_read"], S["slots_ok"])
        scat = [S["scat0"], S["scat1"]]
        cum_ok = S["cum_ok"]
        table_ok, pad_out = S["table_ok"], S["pad_out"]
        dve_link, pool_link = S["dve_link"], S["pool_link"]
        gu_done, sil_ok, hid_ok, down_done, base_ok = (S["gu_done"], S["sil_ok"], S["hid_ok"], S["down_done"],
                                                       S["base_ok"])
        tile_in = [S[f"tile_in{r}"] for r in range(4)]
        ysc = [S[f"ysc{r}"] for r in range(4)]
        y_got = [S["y_in0"], S["y_in1"]]
        xst_done, xst_ok, h_done, silm_ok, act_ok = (S["xst_done"], S["xst_ok"], S["h_done"], S["silm_ok"],
                                                     S["act_ok"])
        actt_done, actt_ok, y_done, y_ok, dst_ok = (S["actt_done"], S["actt_ok"], S["y_done"], S["y_ok"],
                                                    S["dst_ok"])
        fhi_ok, flo_ok, high_ok, low_ok = S["fhi_ok"], S["flo_ok"], S["high_ok"], S["low_ok"]
        xlo_ok, prod_ok, hhi_ok = S["xlo_ok"], S["prod_ok"], S["hhi_ok"]
        y_added, sig_ok, out_done = S["y_added"], S["sig_ok"], S["out_done"]

        def held(eng, value):
            return value if isinstance(value, int) else eng.to_reg(value)

        def attention_steps(eng, body):
            def step(i, c):
                body(Group(i, c), now=0 <= c < G, soon=-1 <= c < G - 1, later=c < G - 2, past=c >= 1)

            step(0, -2)
            step(0, -1)
            step(0, 0)
            with eng.Fori(0, (G - 4) // 2) as i:
                step(i, 1)
                step(i, 2)
            for c in range(G - 3, G + 1):
                step(0, c)

        def expert_steps(eng, body, load=None):
            def run(i, c, n):
                values = load(i, c, n) if load else None
                for r in range(n):
                    body(Tile(i, c + r), *([values[r]] if load else []))

            turns = (NT - HEAD) // TURN
            run(0, 0, HEAD)
            with eng.Fori(0, turns) as i:
                run(i, HEAD, TURN)
            run(0, HEAD + TURN * turns, NT - HEAD - TURN * turns)

        block = es.enter_context(nc.Block())

        @block.sync
        def _(sp):
            sp.dma_start(x_all[:, 0:2, :], x_view[:, 0:2, :]).then_inc(x_in0, 16)
            sp.sem_inc(xt_out, 16)

            def load_k(g, par, count):
                if g.c >= 1:
                    old = held(sp, g.n(4))
                    sp.wait_ge(small_in, 32)
                    sp.wait_ge(st_done, old)
                for piece, ready in ((0, k1_ok), (1, k2_ok), (2, k3_ok)):
                    sp.wait_ge(ready, count)
                    for s, p in K_SLOTS:
                        if p == piece:
                            sp.dma_start(k_st[HD * s:HD * s + HD, par].rearrange("p h t -> p (h t)"),
                                         k_pc[:, p, :]).then_inc(kst[par], 16)

            def body(g, now, soon, later, past):
                pn = 1 - g.par
                if later:
                    if now:
                        sp.wait_ge(v_done, g.n(1, 1))
                    off = g.n(TG, 2)
                    src = ctx_t[:, :, off:off + TG] if isinstance(off, int) else ctx_t[:, :, bass.ds(off, TG)]
                    sp.dma_start(ctx_s[:, g.par], src).then_inc(ctx_in[g.par], 16)
                if g.c == -2:
                    sp.dma_start(mask_u[:, :], mask).then_inc(small_in, 16)
                    sp.dma_start(gate_r[:, :], gates).then_inc(small_in, 16)
                    sp.dma_start(x_all[:, 2:4, :], x_view[:, 2:4, :]).then_inc(x_in1, 16)
                    sp.dma_start(wv_s[:, :, :], wv).then_inc(wv_in, 16)
                    sp.wait_ge(wr_ok, 1)
                    sp.dma_start(wr_s[:, :, 0:E], w_router).then_inc(wr_in, 16)
                if g.c == -2:
                    load_k(g, 0, 1)
                if g.c >= 0 and soon:
                    load_k(g, pn, g.n(1, 2))
                if past:
                    sp.wait_ge(xt_ok, g.n(1))
                    off = g.n(TG, -1)
                    dst = xt_all[:, :, off:off + TG] if isinstance(off, int) else xt_all[:, :, bass.ds(off, TG)]
                    sp.dma_start(dst, xt_grp[:, :, :]).then_inc(xt_out, 16)
                if soon:
                    e2 = g.n(2, 1)
                    part = slice(e2, e2 + 2) if isinstance(e2, int) else bass.ds(e2, 2)
                    sp.dma_start(fc1_s[:, part, :], fc1[:, part, :]).then_inc(fc1_in, 16)
                    sp.dma_start(fc2_s[:, part, :], fc2[:, part, :]).then_inc(fc2_in, 16)
                if later:
                    if now:
                        old = held(sp, g.n(4, 1))
                        sp.wait_ge(small_in, 32)
                        sp.wait_ge(st_done, old)
                    for piece, ready in ((0, q1_ok), (1, q2_ok), (2, q3_ok)):
                        sp.wait_ge(ready, g.n(1, 3))
                        for s, p in Q_SLOTS:
                            if p == piece:
                                sp.dma_start(q_st[HD * s:HD * s + HD, g.par].rearrange("p h t -> p (h t)"),
                                             q_pc[:, p, :]).then_inc(qst[g.par], 16)
                if g.c == -2:
                    sp.dma_start(x_all[:, 4:B, :], x_view[:, 4:B, :]).then_inc(x_rest, 16)
                if g.c == G - 3:
                    sp.dma_start(gate_s[:, :, :], gate_w).then_inc(ffn_in, 16)
                    sp.dma_start(up_s[:, :, :], up_w).then_inc(ffn_in, 16)
                    sp.dma_start(down_s[:, :, :], down_w).then_inc(ffn_in, 16)

            attention_steps(sp, body)

            sp.wait_ge(zero_row_ok, 1)
            sp.wait_ge(table_ok, 1)
            pads = nc.values_load_multi_w_load_instructions(
                pad_i[0:1, :], engines=[mybir.EngineType.SP], min_val=0, max_val=NULL_ROW - P)[1]
            for e in range(E):
                sp.dma_start(xs[bass.ds(pads[e], P), :], zrow[:, :]).then_inc(pad_out, 16)
            first = nc.values_load_multi_w_load_instructions(
                base_i[0:1, 0:HEAD], engines=[mybir.EngineType.SP], min_val=0, max_val=NULL_ROW, skip_runtime_bounds_check_because=CLAMPED)[1]
            sp.wait_ge(scat[0], 64 * (G // 2))
            sp.wait_ge(scat[1], 64 * (G // 2) + 16)
            sp.wait_ge(pad_out, 16 * E)

            def first_rows(i, c, n):
                at = base_i[0:1, c:c + n] if isinstance(i, int) else base_i[0:1, bass.ds(i * TURN + c, n)]
                return nc.values_load_multi_w_load_instructions(
                    at, engines=[mybir.EngineType.SP], min_val=0, max_val=NULL_ROW, skip_runtime_bounds_check_because=CLAMPED)[1]

            def load_tile(t, row):
                r = t.c % 4
                if t.since(4):
                    sp.wait_ge(xst_done, t.n(-3))
                    sp.wait_ge(dst_ok, t.n(-3))
                sp.dma_start(xs_in[:, r, :], xs[bass.ds(row, P), :]).then_inc(tile_in[r], 16)

            expert_steps(sp, load_tile, lambda i, c, n: first if c == 0 else first_rows(i, c, n))

            for r in range(4):
                sp.wait_ge(ysc[r], 16 * len(range(r, NT, 4)))
            for c in range(NCH):
                if c >= 2:
                    sp.wait_ge(y_added, c - 1)
                sp.dma_start(y_in[c % 2][:, 0], y_view[:, 0, CH * c:CH * c + CH, :]).then_inc(y_got[c % 2], 16)
                sp.dma_start(y_in[c % 2][:, 1], y_view[:, 1, CH * c:CH * c + CH, :]).then_inc(y_got[c % 2], 16)
                if c < 2:
                    continue
                sp.wait_ge(y_added, c - 1)
                sp.dma_start(out_view[:, CH * (c - 2):CH * (c - 1), :],
                             x_all[:, CH * (c - 2):CH * (c - 1), :]).then_inc(out_done, 16)
            sp.wait_ge(y_added, NCH - 1)
            sp.dma_start(out_view[:, B - 2 * CH:B - CH, :], x_all[:, B - 2 * CH:B - CH, :]).then_inc(out_done, 16)
            for t in range(CH):
                sp.wait_ge(base_ok, B - CH + t + 1)
                sp.dma_start(out_view[:, B - CH + t, :], x_all[:, B - CH + t, :]).then_inc(out_done, 16)
            sp.wait_ge(out_done, 16 * (NCH - 1 + CH))

        @block.gpsimd
        def _(pool):
            nc.gpsimd.memset(wr_s[:, :, :], 0.0).then_inc(wr_ok, 1)
            nc.gpsimd.memset(ident[:, :], 0.0).then_inc(pool_link, 1)
            nc.gpsimd.memset(ident_b[:, :], 0.0).then_inc(pool_link, 1)
            nc.gpsimd.memset(before[:, :], 1.0).then_inc(pool_link, 1)
            nc.gpsimd.memset(tri_f[:, :, :], 1.0).then_inc(pool_link, 1)
            nc.gpsimd.memset(mhalf[:, :], -0.5).then_inc(pool_link, 1)
            pool.wait_ge(pool_link, 5)
            nc.gpsimd.affine_select(out=ident[:, :], in_=ident[:, :], compare_op=ALU.not_equal, fill=1.0,
                                    base=0, pattern=[[-1, P]], channel_multiplier=1).then_inc(const_ok, 1)
            nc.gpsimd.affine_select(out=ident_b[:, :], in_=ident_b[:, :], compare_op=ALU.not_equal, fill=1.0,
                                    base=0, pattern=[[-1, P]], channel_multiplier=1).then_inc(const_ok, 1)
            nc.gpsimd.affine_select(out=before[:, :], in_=before[:, :], compare_op=ALU.is_gt, fill=0.0,
                                    base=0, pattern=[[1, P]], channel_multiplier=-1).then_inc(const_ok, 1)
            nc.gpsimd.affine_select(out=tri_f[:, :, :], in_=tri_f[:, :, :], compare_op=ALU.is_ge, fill=0.0,
                                    base=0, pattern=[[1, 8], [-1, 8]], channel_multiplier=0).then_inc(const_ok, 1)
            nc.gpsimd.iota(e_i[:, :], pattern=[[1, 8]], base=0, channel_multiplier=0).then_inc(const_ok, 1)
            nc.gpsimd.iota(t_i[:, :], pattern=[[1, NT]], base=0, channel_multiplier=0).then_inc(const_ok, 1)
            nc.gpsimd.iota(dest_i[:, :], pattern=[[-P, 2], [-T, 2]], base=2 * T,
                           channel_multiplier=-1).then_inc(const_ok, 1)
            nc.gpsimd.memset(zrow[:, :], 0.0).then_inc(zero_row_ok, 1)
            pool.wait_ge(zero_row_ok, 1)
            nc.gpsimd.dma_start(xs[NULL_ROW:NULL_ROW + P, :], zrow[:, :]).then_inc(scat[1], 16)
            def low_of_fc1(e):
                w = fc1_s[:, 2 * e:2 * e + 2, :]
                pool.wait_ge(fhi_ok, e + 1)
                nc.gpsimd.tensor_tensor(fc1_lo[:, 2 * e:2 * e + 2, :], w, fc1_hi[:, 2 * e:2 * e + 2, :].bitcast(F32),
                                        ALU.subtract).then_inc(flo_ok, 1)

            def third_of_k(g, count):
                pool.wait_ge(k2_ok, count)
                if g.c >= 0:
                    pool.wait_ge(kst[g.par], g.turns(96))
                nc.gpsimd.tensor_tensor(k_pc[:, 2, :], k_rest[:, :], k_pc[:, 1, :], ALU.subtract).then_inc(k3_ok, 1)

            pool.wait_ge(ln1_var, 1)
            nc.gpsimd.tensor_tensor(rs1[:, 0:2], ve1[:, 0:2], mhalf[:, 0:2], ALU.pow).then_inc(rs1_ok, 1)
            def body(g, now, soon, later, past):
                pn = 1 - g.par
                if past:
                    pool.wait_ge(ln2_var, g.n(2))
                    nc.gpsimd.tensor_tensor(rs2[:, 1:2], ve2[:, 1:2], mhalf[:, 0:1], ALU.pow).then_inc(rs2_ok, 1)
                if g.c == -2:
                    third_of_k(g, 1)
                    pool.wait_ge(ln1_var, 2)
                    nc.gpsimd.tensor_tensor(rs1[:, 2:4], ve1[:, 2:4], mhalf[:, 2:4], ALU.pow).then_inc(rs1_ok, 1)
                if g.c >= 0 and soon:
                    third_of_k(g, g.n(1, 2))
                if g.c == G:
                    for e in range(3):
                        low_of_fc1(e)
                if now:
                    pool.wait_ge(ln2_var, g.n(2, 0, 1))
                    nc.gpsimd.tensor_tensor(rs2[:, 0:1], ve2[:, 0:1], mhalf[:, 0:1], ALU.pow).then_inc(rs2_ok, 1)
                if past:
                    places, rows = held(pool, g.n(1)), held(pool, g.n(2))
                    pool.wait_ge(pool_link, 5)
                    pool.wait_ge(slots_ok, places)
                    pool.wait_ge(dup_ok, rows)
                    for m in range(4):
                        nc.gpsimd.indirect_dma_start(
                            xs, bass.IndirectOffsetOnAxis(slot_u[:, pn, m:m + 1], 0), row_s[:, pn, m, :], None,
                            bounds_check=NULL_ROW + P - 1, oob_is_err=False).then_inc(scat[pn], 16)
                if later:
                    pool.wait_ge(q2_ok, g.n(1, 3))
                    if g.c >= -1:
                        pool.wait_ge(qst[pn], g.turns(96, 1))
                    nc.gpsimd.tensor_tensor(q_pc[:, 2, :], q_rest[:, :], q_pc[:, 1, :],
                                            ALU.subtract).then_inc(q3_ok, 1)
                if g.c == -1:
                    pool.wait_ge(ln1_var, 3)
                    nc.gpsimd.tensor_tensor(rs1[:, 4:B], ve1[:, 4:B], mhalf[:, 4:B], ALU.pow).then_inc(rs1_ok, 1)

            attention_steps(pool, body)
            for e in range(3, E):
                low_of_fc1(e)

            def low_half(low, w, high):
                nc.gpsimd.tensor_tensor(low, w, high.bitcast(F32), ALU.subtract).then_inc(low_ok, 1)

            def scatter(t):
                r = t.c % 4
                tiles = held(pool, t.n(1))
                pool.wait_ge(pool_link, 5)
                pool.wait_ge(y_ok, tiles)
                pool.wait_ge(dst_ok, tiles)
                nc.gpsimd.indirect_dma_start(
                    ys, bass.IndirectOffsetOnAxis(dst_u[:, r:r + 1], 0), y_out[:, r, :], None,
                    bounds_check=2 * T - 1, oob_is_err=False).then_inc(ysc[r], 16)
                if isinstance(t.i, int):
                    if 1 <= t.c <= 3:
                        pool.wait_ge(down_done, 2 * CH)
                        pool.wait_ge(high_ok, t.c)
                        low, w, high = ((gate_lo, gate_s, gate_hi), (up_lo, up_s, up_hi),
                                        (down_lo, down_s, down_hi))[t.c - 1]
                        low_half(low[:, :, :], w[:, :, :], high[:, :, :])
                    for c in range(2, NCH) if t.c == 4 else ():
                        pool.wait_ge(high_ok, c + 2)
                        tokens = slice(CH * P * c, CH * P * (c + 1))
                        low_half(xt_lo[:, :, tokens], xt_all[:, :, tokens], xt_hi[:, 2 * c - 4:2 * c - 2, :])

            expert_steps(pool, scatter)

        @block.scalar
        def _(sa):
            sa.dma_start(wk_s[:, :, :, :], wk).then_inc(wk_in, 16)
            sa.dma_start(wq_s[:, :, :, :], wq).then_inc(wq_in, 16)

            def first_of_k(g, count, bank):
                sa.wait_ge(k_done, count)
                if g.c >= 0:
                    sa.wait_ge(kst[g.par], g.turns(96))
                nc.scalar.activation(k_pc[:, 0, :], ps[:, bank, :], ACT.Copy).then_inc(k1_ok, 1)

            def second_of_k(count):
                sa.wait_ge(kr_ok, count)
                nc.scalar.activation(k_pc[:, 1, :], k_rest[:, :], ACT.Copy).then_inc(k2_ok, 1)

            def high_of_fc1(e):
                sa.wait_ge(fc1_in, 16 * E)
                nc.scalar.activation(fc1_hi[:, 2 * e:2 * e + 2, :], fc1_s[:, 2 * e:2 * e + 2, :],
                                     ACT.Copy).then_inc(fhi_ok, 1)

            def gate_tanh(j):
                sa.wait_ge(gu_done, j + 1)
                if j >= 2:
                    sa.wait_ge(hid_ok, j - 1)
                nc.scalar.activation(sig_0[:, j % 2], ps[:, 5, :], ACT.Tanh, scale=0.5).then_inc(sig_ok, 1)

            def body(g, now, soon, later, past):
                pn = 1 - g.par

                def exp(j, h):
                    sa.wait_ge(st_done, g.n(4, 0, 2 * j + h + 1))
                    if not (isinstance(g.i, int) and g.c == 0):
                        sa.wait_ge(pv_done, g.n(4, -1, 2 * j + h + 1))
                    nc.scalar.activation(probs[:, 2 * j + h], ps_t, ACT.Exp, scale=HD ** -0.5).then_inc(probs_ok, 1)

                def max_rows(j, d):
                    par = (g.par + d) % 2
                    count = held(sa, g.n(2, d, j + 1))
                    if not (isinstance(g.i, int) and g.c + d == 0):
                        taken = held(sa, g.n(16, d))
                        sa.wait_ge(small_in, 32)
                        sa.wait_ge(rows_in[j], taken)
                    sa.wait_ge(maxt_done, count)
                    nc.scalar.activation(mx_t[:, j, :], ps_m, ACT.Copy).then_inc(maxt_ok, 1)
                    sa.wait_ge(small_in, 32)
                    sa.wait_ge(maxt_ok, count)
                    sa.dma_start(q_st[6 * HD:6 * HD + 3, par, :, P * j:P * j + P],
                                 mx_t[:, j, :]).then_inc(rows_in[j], 16)

                if g.c == -2:
                    first_of_k(g, 1, 5)
                    second_of_k(1)
                if g.c >= 0 and soon:
                    first_of_k(g, g.n(1, 2), 6)
                if soon:
                    sa.wait_ge(v_done, g.n(1, 2))
                    if g.c >= 1:
                        sa.wait_ge(pv_done, g.n(4))
                    if g.c == -1:
                        sa.wait_ge(v_ones_ok, 1)
                    dst = v_s[:, pn, :, 0:VW * HEADS].rearrange("p j (h e) -> p j h e", e=VW)[:, :, :, 0:HD]
                    nc.scalar.activation(dst, ps[:, 5, :].rearrange("p (j h e) -> p j h e", j=2, h=HEADS),
                                         ACT.Copy).then_inc(v_ok, 1)
                if past:
                    sa.wait_ge(x2t_done, g.n(1))
                    sa.wait_ge(xt_out, g.n(16))
                    nc.scalar.activation(xt_grp[:, :, :], ps_x, ACT.Copy).then_inc(xt_ok, 1)
                if now:
                    exp(0, 0)
                if g.c >= 0 and soon:
                    second_of_k(g.n(1, 2))
                if past:
                    sa.wait_ge(xn2_ok, g.n(2))
                    nc.scalar.activation(row_s[:, pn, 3, 0:D], row_s[:, pn, 2, 0:D], ACT.Copy).then_inc(dup_ok, 1)
                if now:
                    exp(0, 1)
                    max_rows(1, 0)
                if past:
                    sa.wait_ge(dif_ok, g.n(1))
                    nc.scalar.activation(ex[:, :, :], dif[:, :, :], ACT.Exp).then_inc(ex_ok, 1)
                if g.c == G:
                    for e in range(4, E):
                        high_of_fc1(e)
                if later:
                    sa.wait_ge(xnt_done, g.n(1, 3))
                    if g.c >= -1:
                        sa.wait_ge(q_done, g.n(1, 2))
                    nc.scalar.activation(xn_t[:, :, :], ps_b, ACT.Copy).then_inc(xnt_ok, 1)
                if now:
                    exp(1, 0)
                    sa.wait_ge(xn2_ok, g.n(2, 0, 1))
                    nc.scalar.activation(row_s[:, g.par, 1, 0:D], row_s[:, g.par, 0, 0:D],
                                         ACT.Copy).then_inc(dup_ok, 1)
                if later:
                    sa.wait_ge(q_done, g.n(1, 3))
                    if g.c >= -1:
                        sa.wait_ge(qst[pn], g.turns(96, 1))
                    nc.scalar.activation(q_pc[:, 0, :], ps[:, 6, :], ACT.Copy).then_inc(q1_ok, 1)
                if g.c == G - 2:
                    gate_tanh(0)
                if g.c == G - 1:
                    gate_tanh(2)
                if now:
                    exp(1, 1)
                if later:
                    sa.wait_ge(qr_ok, g.n(1, 3))
                    nc.scalar.activation(q_pc[:, 1, :], q_rest[:, :], ACT.Copy).then_inc(q2_ok, 1)
                if g.c == -2:
                    sa.wait_ge(gates_done, 1)
                    nc.scalar.activation(tg[:, :], ps_c[:, 0:2], ACT.Tanh).then_inc(tanh_ok, 1)
                if soon:
                    max_rows(0, 1)
                if g.c == G - 2:
                    gate_tanh(1)
                if g.c == G - 1:
                    for e in range(4):
                        high_of_fc1(e)
                    gate_tanh(3)

            attention_steps(sa, body)

            def gate_silu(c, j):
                sa.wait_ge(gu_done, c * NJ + j + 1)
                sa.wait_ge(hid_ok, c * NJ + j - 1)
                nc.scalar.activation(sil_sh[:, j % 2], ps[:, j % 2, :], ACT.Silu).then_inc(sil_ok, 1)

            for j in range(NJ):
                gate_silu(1, j)

            def high_half(out, w):
                nc.scalar.activation(out, w, ACT.Copy).then_inc(high_ok, 1)

            def rows_in_halves(t, d):
                par = (t.c + d) % 2
                sa.wait_ge(xst_done, t.n(d + 1))
                if t.since(2 - d):
                    sa.wait_ge(h_done, t.n(d - 1))
                nc.scalar.activation(xs_hi[:, par],
                                     ps[:, par, 0:2 * P].rearrange("p (k t) -> p k t", k=2),
                                     ACT.Copy).then_inc(xst_ok, 1)

            def expert_silu(t, d):
                par = (t.c + d) % 2
                sa.wait_ge(h_done, t.n(d + 1))
                if t.since(2 - d):
                    sa.wait_ge(act_ok, t.n(d - 1))
                nc.scalar.activation(sil[:, par], ps[:, 2 + par, 0:FI], ACT.Silu).then_inc(silm_ok, 1)

            def expert_y(t, d):
                r = (t.c + d) % 4
                sa.wait_ge(y_done, t.n(d + 1))
                if t.since(4 - d):
                    sa.wait_ge(ysc[r], t.laps(d))
                nc.scalar.activation(y_out[:, r, :], ps[:, 5 + r % 2, 0:D], ACT.Copy,
                                     scale=wt[:, r:r + 1]).then_inc(y_ok, 1)

            def step(t):
                if t.c + 2 < NT:
                    rows_in_halves(t, 2)
                if t.c + 1 < NT:
                    expert_silu(t, 1)
                if t.since(1):
                    expert_y(t, -1)
                if isinstance(t.i, int):
                    if t.c < 3:
                        high_half((gate_hi, up_hi, down_hi)[t.c][:, :, :], (gate_s, up_s, down_s)[t.c][:, :, :])
                    elif t.c < 5:
                        if t.c == 3:
                            sa.wait_ge(xt_out, 16 * (G + 1))
                        high_half(xt_hi[:, 2 * t.c - 6:2 * t.c - 4, :],
                                  xt_all[:, :, CH * P * (t.c - 1):CH * P * t.c])

            rows_in_halves(Tile(0, 0), 0)
            rows_in_halves(Tile(0, 0), 1)
            expert_silu(Tile(0, 0), 0)
            expert_steps(sa, step)
            expert_y(Tile(0, NT), -1)

            with sa.Fori(2, NCH) as c:
                for j in range(NJ):
                    gate_silu(c, j)
                    sa.wait_ge(prod_ok, c * NJ + (j + 1 - 2 * NJ))
                    if j == 0:
                        sa.wait_ge(down_done, c * CH)
                    nc.scalar.activation(hid_hi[:, j, :], sil_sh[:, j % 2], ACT.Copy).then_inc(hhi_ok, 1)

        @block.vector
        def _(ve):
            links = [0]

            def link(ins):
                links[0] += 1
                ins.then_inc(dve_link, 1)
                ve.wait_ge(dve_link, links[0])

            def relink():
                if links[0]:
                    ve.wait_ge(dve_link, links[0])
                    ve.sem_clear(dve_link)
                    links[0] = 0

            nc.vector.memset(ones_r[:, :], 1.0).then_inc(const_ok, 1)
            nc.vector.memset(ones_b[:, :], 1.0).then_inc(const_ok, 1)
            nc.vector.memset(cum[:, :, :], 0.0).then_inc(cum_ok, 1)
            def stats(b0, b1):
                for b in range(b0, b1):
                    nc.vector.bn_stats(st1[:, b, :], x_all[:, b, :]).then_inc(dve_link, 1)
                links[0] += b1 - b0
                ve.wait_ge(dve_link, links[0])
                for b in range(b0, b1):
                    nc.vector.bn_aggr(mv1[:, b, :], st1[:, b, :]).then_inc(dve_link, 1)
                links[0] += b1 - b0
                ve.wait_ge(dve_link, links[0])
                nc.vector.tensor_scalar(ve1[:, b0:b1], mv1[:, b0:b1, 1], EPS, None, ALU.add).then_inc(ln1_var, 1)

            def first_norm():
                ve.wait_ge(x_in0, 16)
                stats(0, 2)
                ve.wait_ge(small_in, 32)
                link(nc.vector.tensor_copy(mask_f[:, :], mask_u[:, :].bitcast(U8)))
                ve.wait_ge(rs1_ok, 1)
                link(nc.vector.tensor_tensor(rm1[:, 0:2], rs1[:, 0:2], mask_f[:, 0:2], ALU.mult))

            def rest_of_k(g, count, bank):
                ve.wait_ge(k1_ok, count)
                if g.c >= 0:
                    ve.wait_ge(k3_ok, g.n(1, 1))
                nc.vector.tensor_tensor(k_rest[:, :], ps[:, bank, :], k_pc[:, 0, :], ALU.subtract).then_inc(kr_ok, 1)

            def gated(j):
                ve.wait_ge(sig_ok, j + 1)
                link(nc.vector.scalar_tensor_tensor(sig_0[:, j % 2], sig_0[:, j % 2], 1.0, ps[:, 5, :],
                                                    ALU.add, ALU.mult))
                nc.vector.scalar_tensor_tensor(hid_0[:, j, :], sig_0[:, j % 2], 0.5, ps[:, 6, :],
                                               ALU.mult, ALU.mult).then_inc(hid_ok, 1)

            def norm1(g):
                b = g.n(2, 2)
                for j in range(2):
                    at = b + j
                    if isinstance(at, int):
                        src, mean, rstd = x_all[:, at, :], mv1[:, at, 0:1], rm1[:, at:at + 1]
                    else:
                        src = x_all[:, bass.ds(at, 1), :].rearrange("p a d -> p (a d)")
                        mean = mv1[:, bass.ds(at, 1), 0:1].rearrange("p a d -> p (a d)")
                        rstd = rm1[:, bass.ds(at, 1)]
                    nc.vector.tensor_scalar(xn[:, j, :], src, mean, rstd, ALU.subtract, ALU.mult).then_inc(xn_ok, 1)

            def maxima(g, j, h, d=0):
                ve.wait_ge(s_done, g.n(4, d, 2 * j + h + 1))
                nc.vector.reduce_max(mx[:, 8 * h:8 * h + 8], ps_s, AX_X).then_inc(max_ok, 1)

            def pieces(g, j, d=0):
                ve.wait_ge(max_ok, g.n(4, d, 2 * j + 2))
                if not (isinstance(g.i, int) and g.c + d == 0 and j == 0):
                    ve.wait_ge(maxt_done, g.n(2, d, j))
                link(nc.vector.tensor_scalar(mx_pc[:, 0, :], mx[:, :], -1.0, None, ALU.mult))
                link(nc.vector.scalar_tensor_tensor(mx_rest[:, :], mx[:, :], -1.0, mx_pc[:, 0, :],
                                                    ALU.mult, ALU.subtract))
                link(nc.vector.tensor_copy(mx_pc[:, 1, :], mx_rest[:, :]))
                nc.vector.tensor_tensor(mx_pc[:, 2, :], mx_rest[:, :], mx_pc[:, 1, :],
                                        ALU.subtract).then_inc(pieces_ok, 1)

            def attended(g, j):
                ve.wait_ge(pv_done, g.n(4, 0, 2 * j + 2))
                o = ps_o[:, 0:VW * HEADS].rearrange("p (h e) -> p h e", e=VW)
                link(nc.vector.reciprocal(rsum[:, :], o[:, :, HD]))
                link(nc.vector.tensor_scalar(rsg[:, :], rsum[:, :], tg[:, 0:1], None, ALU.mult))
                nc.vector.tensor_tensor(att[:, :].rearrange("p (h e) -> p h e", e=HD), o[:, :, 0:HD],
                                        rsg[:, :].unsqueeze(2).broadcast_to([P, HEADS, HD]),
                                        ALU.mult).then_inc(o_read, 1)
                ve.wait_ge(o_read, g.n(2, 0, j + 1))
                b = g.n(2, 0, j)
                xb = x_all[:, b, :] if isinstance(b, int) else x_all[:, bass.ds(b, 1), :].rearrange("p a d -> p (a d)")
                link(nc.vector.tensor_tensor(xb, xb, att[:, :], ALU.add))
                link(nc.vector.bn_stats(st2[:, :], xb))
                link(nc.vector.bn_aggr(mv2[:, j, :], st2[:, :]))
                nc.vector.tensor_scalar(ve2[:, j:j + 1], mv2[:, j, 1:2], EPS, None, ALU.add).then_inc(ln2_var, 1)

            def norm2(g, j, d=0):
                par = (g.c + d) % 2
                ve.wait_ge(rs2_ok, g.n(2, d, j + 1))
                if j == 0 and g.c + d >= 1:
                    ve.wait_ge(scat[par], g.turns(64, d - 2) + 16 * par)
                b = g.n(2, d, j)
                xb = x_all[:, b, :] if isinstance(b, int) else x_all[:, bass.ds(b, 1), :].rearrange("p a d -> p (a d)")
                nc.vector.tensor_scalar(row_s[:, par, 2 * j, 0:D], xb, mv2[:, j, 0:1], rs2[:, j:j + 1],
                                        ALU.subtract, ALU.mult).then_inc(xn2_ok, 1)

            def body(g, now, soon, later, past):
                pp = 1 - g.par
                if now:
                    maxima(g, 1, 0)
                if past:
                    norm2(g, 1, -1)
                if g.c == G:
                    gated(3)
                if g.c == G - 1:
                    gated(1)
                if g.c == -2:
                    first_norm()
                if g.c >= 0 and soon:
                    rest_of_k(g, g.n(1, 2), 6)
                if later:
                    if g.c == -1:
                        ve.wait_ge(rs1_ok, 2)
                        link(nc.vector.tensor_tensor(rm1[:, 2:4], rs1[:, 2:4], mask_f[:, 2:4], ALU.mult))
                    if g.c == 0:
                        ve.wait_ge(rs1_ok, 3)
                        link(nc.vector.tensor_tensor(rm1[:, 4:B], rs1[:, 4:B], mask_f[:, 4:B], ALU.mult))
                    if g.c >= -1:
                        ve.wait_ge(xnt_done, g.n(1, 2))
                    norm1(g)
                if now:
                    maxima(g, 1, 1)
                    if not past:
                        pieces(g, 1)
                if past:
                    ve.wait_ge(router_done, g.n(1))
                    nc.vector.tensor_copy(lg[:, :, :], ps_c[:, 0:2 * NV].rearrange("p (j e) -> p j e", j=2)[:, :, 0:8]
                                          ).then_inc(lg_read, 1)
                    if now:
                        pieces(g, 1)
                    ve.wait_ge(const_ok, 9)
                    ve.wait_ge(lg_read, g.n(1))
                    nc.vector.max(top[:, 0, :], lg[:, 0, :]).then_inc(dve_link, 1)
                    links[0] += 1
                    link(nc.vector.max(top[:, 1, :], lg[:, 1, :]))
                    nc.vector.tensor_tensor(dif[:, :, :], top[:, :, 1:2], top[:, :, 0:1],
                                            ALU.subtract).then_inc(dif_ok, 1)
                    nc.vector.max_index(topi[:, 0, :], top[:, 0, :], lg[:, 0, :]).then_inc(dve_link, 1)
                    links[0] += 1
                    link(nc.vector.max_index(topi[:, 1, :], top[:, 1, :], lg[:, 1, :]))
                    link(nc.vector.tensor_copy(idx_f[:, :].rearrange("p (j k) -> p j k", j=2), topi[:, :, 0:2]))
                    link(nc.vector.tensor_tensor(oh[:, :, :, :].rearrange("p j k e -> p (j k) e"),
                                                 e_f[:, :].unsqueeze(1).broadcast_to([P, 4, 8]),
                                                 idx_f[:, :].unsqueeze(2).broadcast_to([P, 4, 8]), ALU.is_equal))
                    ve.wait_ge(cum_ok, g.n(1))
                    link(nc.vector.tensor_tensor(cnt[:, :, :], oh[:, :, 0, :], oh[:, :, 1, :], ALU.add))
                    nc.vector.tensor_tensor(cum[:, 1, :], cum[:, 0, :], cnt[:, 0, :], ALU.add).then_inc(oh_ok, 1)
                if past:
                    ve.wait_ge(ex_ok, g.n(1))
                    link(nc.vector.tensor_scalar(den[:, :, :], ex[:, :, :], 1.0, None, ALU.add))
                    link(nc.vector.reciprocal(sc1[:, :, :], den[:, :, :]))
                    rows = row_s[:, pp, :, :].rearrange("p (j k) c -> p j k c", j=2)
                    link(nc.vector.tensor_scalar(rows[:, :, 0, D + 1:D + 2], sc1[:, :, :], tg[:, 1:2], None, ALU.mult))
                    nc.vector.tensor_tensor(rows[:, :, 1, D + 1:D + 2], rows[:, :, 0, D + 1:D + 2], ex[:, :, :],
                                            ALU.mult).then_inc(dve_link, 1)
                    links[0] += 1
                    link(nc.vector.tensor_copy(row_s[:, pp, :, D], dest_f[:, :]))
                    link(nc.vector.tensor_scalar(dest_f[:, :], dest_f[:, :], float(-TG), None, ALU.add))
                if now:
                    attended(g, 0)
                if past:
                    ve.wait_ge(pos_done, g.n(1))
                    nc.vector.tensor_tensor(slot[:, :, :], ps_c[:, 192:208].rearrange("p (j e) -> p j e", j=2),
                                            er_f[:, :].unsqueeze(1).broadcast_to([P, 2, 8]), ALU.add
                                            ).then_inc(pos_read, 1)
                    ve.wait_ge(pos_read, g.n(1))
                    link(nc.vector.tensor_tensor(slot_p[:, :, :, :], oh[:, :, :, :],
                                                 slot[:, :, :].unsqueeze(2).broadcast_to([P, 2, 2, 8]), ALU.mult))
                    link(nc.vector.reduce_sum(slot_f[:, :], slot_p[:, :, :, :].rearrange("p j k e -> p (j k) e"), AX_X))
                    nc.vector.tensor_copy(slot_u[:, pp, :], slot_f[:, :]).then_inc(slots_ok, 1)
                    nc.vector.tensor_tensor(cum[:, 0, :], cum[:, 1, :], cnt[:, 1, :], ALU.add).then_inc(cum_ok, 1)
                if now:
                    norm2(g, 0)
                if g.c == -2:
                    rest_of_k(g, 1, 5)
                    nc.vector.memset(k_f[96:99, :], TWO_ONES).then_inc(kones_ok, 1)
                    ve.wait_ge(x_in1, 16)
                    stats(2, 4)
                if soon:
                    maxima(g, 0, 0, 1)
                if g.c == G - 2:
                    gated(0)
                if g.c == G - 1:
                    gated(2)
                if later:
                    ve.wait_ge(q1_ok, g.n(1, 3))
                    if g.c >= -1:
                        ve.wait_ge(q3_ok, g.n(1, 2))
                    nc.vector.tensor_tensor(q_rest[:, :], ps[:, 6, :], q_pc[:, 0, :], ALU.subtract).then_inc(qr_ok, 1)
                if soon:
                    maxima(g, 0, 1, 1)
                    pieces(g, 0, 1)
                if now:
                    attended(g, 1)
                if g.c == -2:
                    nc.vector.memset(v_s[:, :, :, :], 1.0).then_inc(v_ones_ok, 1)
                if g.c == -1:
                    ve.wait_ge(x_rest, 16)
                    stats(4, B)
                    ve.wait_ge(tanh_ok, 1)
                    ve.wait_ge(const_ok, 9)
                    nc.vector.tensor_copy(e_f[:, :], e_i[:, :]).then_inc(dve_link, 1)
                    nc.vector.tensor_copy(t_f[:, :], t_i[:, :]).then_inc(dve_link, 1)
                    links[0] += 2
                    link(nc.vector.tensor_copy(dest_f[:, :], dest_i[:, :]))
                    link(nc.vector.tensor_scalar(er_f[:, :], e_f[:, :], float(R), None, ALU.mult))
                relink()

            relink()
            attention_steps(ve, body)

            def sum_and_add(c, at, banks):
                for t in range(CH):
                    ve.wait_ge(down_done, c * CH + t + 1 if c >= 1 else (t | 1) + 1)
                    xb = x_all[:, at + t, :] if isinstance(at, int) else x_all[:, bass.ds(at + t, 1), :].rearrange(
                        "p a d -> p (a d)")
                    nc.vector.scalar_tensor_tensor(xb, banks[t], tg[:, 1:2], xb, ALU.mult, ALU.add
                                                   ).then_inc(base_ok, 1)

            def times(c, j):
                ve.wait_ge(sil_ok, j + 1)
                nc.vector.tensor_tensor(hid_1[:, j, :], ps[:, 2 + j % 2, :], sil_sh[:, j % 2], ALU.mult
                                        ).then_inc(hid_ok, 1)

            times(1, 0)
            ve.wait_ge(pos_done, G)
            link(nc.vector.tensor_copy(c_f[:, :], ps_c[0:1, 224:232]))
            nc.vector.tensor_tensor(pad_f[:, :], er_f[0:1, :], c_f[:, :], ALU.add).then_inc(dve_link, 1)
            links[0] += 1
            link(nc.vector.tensor_scalar(c_up[:, :], c_f[:, :], float(P - 1), None, ALU.add))
            link(nc.vector.tensor_copy(pad_i[:, :], pad_f[:, :]))
            link(nc.vector.tensor_scalar(c_sh[:, :], c_up[:, :], 7, None, ALU.logical_shift_right))
            link(nc.vector.tensor_copy(nt_f[:, :], c_sh[:, :]))
            link(nc.vector.tensor_tensor(end_m[:, :, :], tri_f[:, :, :],
                                         nt_f[:, :].unsqueeze(1).broadcast_to([1, 8, 8]), ALU.mult))
            link(nc.vector.reduce_sum(end_f[:, :], end_m[:, :, :], AX_X))
            nc.vector.tensor_scalar(jump[:, :], nt_f[:, :], float(-P), float(R), ALU.mult, ALU.add
                                    ).then_inc(dve_link, 1)
            links[0] += 1
            link(nc.vector.tensor_tensor(past[:, :, :], t_f[:, :].unsqueeze(2).broadcast_to([1, NT, 8]),
                                         end_f[:, :].unsqueeze(1).broadcast_to([1, NT, 8]), ALU.is_ge))
            nc.vector.tensor_tensor(past_j[:, :, :], past[:, :, :],
                                    jump[:, :].unsqueeze(1).broadcast_to([1, NT, 8]), ALU.mult
                                    ).then_inc(dve_link, 1)
            links[0] += 1
            link(nc.vector.reduce_sum(eid_f[:, :], past[:, :, :], AX_X))
            link(nc.vector.reduce_sum(base_f[:, :], past_j[:, :, :], AX_X))
            link(nc.vector.scalar_tensor_tensor(base_g[:, :], t_f[:, :], float(P), base_f[:, :], ALU.mult, ALU.add))
            link(nc.vector.tensor_scalar(eid_i[:, :], eid_f[:, :], float(E - 1), None, ALU.min))
            nc.vector.tensor_scalar(base_i[:, :], base_g[:, :], float(NULL_ROW), None, ALU.min).then_inc(table_ok, 1)

            sum_and_add(0, 0, sums_0)
            for j in range(1, NJ):
                times(1, j)
            def expert_rows(t, d):
                par = (t.c + d) % 2
                ve.wait_ge(xst_ok, t.n(d + 1))
                if t.since(2 - d):
                    ve.wait_ge(h_done, t.n(d - 1))
                nc.vector.tensor_tensor(xs_lo[:, par],
                                        ps[:, par, 0:2 * P].rearrange("p (k t) -> p k t", k=2), xs_hi[:, par].bitcast(F32),
                                        ALU.subtract).then_inc(xlo_ok, 1)

            def expert_dst(t, d):
                r = (t.c + d) % 4
                ve.wait_ge(tile_in[r], t.laps(d, 1))
                if t.since(4 - d):
                    ve.wait_ge(ysc[r], t.laps(d))
                nc.vector.tensor_copy(wt[:, r:r + 1], xs_in[:, r, D + 1:D + 2])
                nc.vector.tensor_scalar(dst_u[:, r:r + 1], xs_in[:, r, D:D + 1], -1.0, float(2 * T),
                                        ALU.mult, ALU.add).then_inc(dst_ok, 1)

            def expert_act(t, d):
                par = (t.c + d) % 2
                ve.wait_ge(silm_ok, t.n(d + 1))
                if t.since(2 - d):
                    ve.wait_ge(actt_done, t.n(d - 1))
                nc.vector.tensor_tensor(act[:, par], ps[:, 2 + par, FI:2 * FI], sil[:, par], ALU.mult
                                        ).then_inc(act_ok, 1)

            def expert_actt(t):
                par = t.c % 2
                ve.wait_ge(actt_done, t.n(1))
                if t.since(2):
                    ve.wait_ge(y_done, t.n(-1))
                nc.vector.tensor_copy(act_t[:, par], ps[:, 4, 0:2 * P].rearrange("p (k t) -> p k t", k=2)
                                      ).then_inc(actt_ok, 1)

            def step(t):
                if t.c + 2 < NT:
                    expert_rows(t, 2)
                if t.c + 1 < NT:
                    expert_act(t, 1)
                    expert_dst(t, 1)
                expert_actt(t)

            expert_dst(Tile(0, 0), 0)
            expert_rows(Tile(0, 0), 0)
            expert_rows(Tile(0, 0), 1)
            sum_and_add(1, CH, sums)
            expert_act(Tile(0, 0), 0)
            expert_steps(ve, step)

            def add_rows(c):
                ve.wait_ge(y_got[c % 2], 32 * (c // 2 + 1))
                if c < NCH - 1:
                    ve.wait_ge(base_ok, CH * (c + 1))
                xc = x_all[:, CH * c:CH * c + CH, :]
                link(nc.vector.tensor_tensor(xc, xc, y_in[c % 2][:, 0], ALU.add))
                nc.vector.tensor_tensor(xc, xc, y_in[c % 2][:, 1], ALU.add).then_inc(y_added, 1)

            def product(c, j):
                ve.wait_ge(sil_ok, (c - 1) * NJ + j + 1)
                nc.vector.tensor_tensor(sil_sh[:, j % 2], ps[:, 2 + j % 2, :], sil_sh[:, j % 2], ALU.mult
                                        ).then_inc(prod_ok, 1)

            for c in range(2, NCH):
                for j in range(NJ):
                    product(c, j)
                    ve.wait_ge(hhi_ok, (c - 2) * NJ + j + 1)
                    nc.vector.tensor_tensor(hid_lo[:, j, :], sil_sh[:, j % 2], hid_hi[:, j, :].bitcast(F32),
                                            ALU.subtract).then_inc(hid_ok, 1)
                    if j == 1:
                        add_rows(2 * c - 4)
                add_rows(2 * c - 3)
                if c == NCH - 1:
                    ve.wait_ge(y_added, NCH)
                sum_and_add(c, c * CH, sums)

        @block.tensor
        def _(pe):
            def gate_up_1(j):
                if j == 0:
                    pe.wait_ge(xt_out, 16 * 5)
                if j >= 2:
                    pe.wait_ge(hid_ok, NJ + j - 1)
                for w, bank in ((gate_s, j % 2), (up_s, 2 + j % 2)):
                    for k in range(2):
                        last = nc.tensor.matmul(ps[:, bank, :], w[:, k, P * j:P * j + P],
                                                xt_all[:, k, CH * P:2 * CH * P], start=k == 0, stop=k == 1)
                last.then_inc(gu_done, 1)

            def body(g, now, soon, later, past):
                pn = 1 - g.par

                def keys(bank, par, count):
                    for c in range(2):
                        for k in range(2):
                            last = nc.tensor.matmul(ps[:, bank, TG * c:TG * c + TG], wk_s[:, k, c, :],
                                                    ctx_s[:, par, k, :], start=k == 0, stop=k == 1)
                        if c == 0:
                            yield
                    last.then_inc(k_done, 1)
                    yield

                def keys_now(*at):
                    for _ in keys(*at):
                        pass

                def values_proj():
                    if g.c == -1:
                        pe.wait_ge(wv_in, 16)
                        pe.wait_ge(kr_ok, 1)
                    if now:
                        pe.wait_ge(v_ok, g.n(1, 1))
                    for j in range(2):
                        for k in range(2):
                            last = nc.tensor.matmul(ps[:, 5, D * j:D * j + D], ctx_s[:, pn, k, P * j:P * j + P],
                                                    wv_s[:, k, :], start=k == 0, stop=k == 1)
                    last.then_inc(v_done, 1)

                def gate_up_0(j):
                    if j == 0:
                        pe.wait_ge(ffn_in, 48)
                        pe.wait_ge(xt_out, 16 * 3)
                        pe.wait_ge(v_ok, G)
                        pe.wait_ge(kr_ok, G)
                    else:
                        pe.wait_ge(hid_ok, j)
                    for w, bank in ((gate_s, 5), (up_s, 6)):
                        for k in range(2):
                            last = nc.tensor.matmul(ps[:, bank, :], w[:, k, P * j:P * j + P], xt_all[:, k, 0:CH * P],
                                                    start=k == 0, stop=k == 1)
                    last.then_inc(gu_done, 1)

                def scores(j, h, d=0):
                    par = (g.c + d) % 2
                    if not (isinstance(g.i, int) and g.c + d == 0 and j == 0 and h == 0):
                        pe.wait_ge(max_ok, g.n(4, d, 2 * j + h))
                    for n in range(8):
                        at = (slice(0, 96), par, 8 * h + n, slice(P * j, P * j + P))
                        last = nc.tensor.matmul(ps_s[:, n, :], q_st[at], k_st[at], start=True, stop=True)
                    last.then_inc(s_done, 1)

                def scores_t(j, h):
                    if h == 0:
                        pe.wait_ge(rows_in[j], g.n(16, 1))
                    if not (isinstance(g.i, int) and g.c == 0 and j == 0 and h == 0):
                        pe.wait_ge(probs_ok, g.n(4, 0, 2 * j + h))
                    for n in range(8):
                        at = (slice(0, 99), g.par, 8 * h + n, slice(P * j, P * j + P))
                        last = nc.tensor.matmul(ps_t[:, n, :], k_st[at], q_st[at], start=True, stop=True)
                    last.then_inc(st_done, 1)

                def values(j, h):
                    pe.wait_ge(probs_ok, g.n(4, 0, 2 * j + h + 1))
                    if h == 0 and not (isinstance(g.i, int) and g.c == 0 and j == 0):
                        pe.wait_ge(o_read, g.n(2, 0, j))
                    if h == 0 and j == 0:
                        pe.wait_ge(v_ok, g.n(1, 1))
                    for n in range(8):
                        if h == 0 and j == 0 and n == 4:
                            max_rows(1, 0, lg_read)
                        c = VW * (8 * h + n)
                        last = nc.tensor.matmul(ps_o[:, c:c + NV], probs[:, 2 * j + h, n, :],
                                                v_s[:, g.par, j, c:c + NV], start=True, stop=True)
                    last.then_inc(pv_done, 1)

                def max_rows(j, d, bank_read):
                    ready, read = held(pe, g.n(2, d, j + 1)), held(pe, g.n(1))
                    pe.wait_ge(const_ok, 9)
                    if g.c == -1:
                        pe.wait_ge(tanh_ok, 1)
                    if past:
                        pe.wait_ge(bank_read, read)
                    pe.wait_ge(pieces_ok, ready)
                    nc.tensor.matmul(ps_m, mx_pc[:, :, :].rearrange("p c h -> p (c h)"), ident_b[:, :],
                                     is_transpose=True, start=True, stop=True).then_inc(maxt_done, 1)

                if g.c == -2:
                    pe.wait_ge(wk_in, 16)
                    pe.wait_ge(ctx_in[0], 16)
                    keys_now(5, 0, 1)
                if now:
                    scores(1, 0)
                if soon:
                    values_proj()
                if past:
                    pe.wait_ge(xn2_ok, g.n(2))
                    if now:
                        pe.wait_ge(maxt_ok, g.n(2, 0, 1))
                    else:
                        pe.wait_ge(maxt_ok, g.n(2))
                        pe.wait_ge(pos_read, g.n(1, -1))
                    for k in range(2):
                        for j in range(2):
                            last = nc.tensor.matmul(ps_x[:, k, P * j:P * j + P],
                                                    row_s[:, pn, 2 * j, P * k:P * k + P], ident[:, :],
                                                    is_transpose=True, start=True, stop=True)
                    last.then_inc(x2t_done, 1)
                if now:
                    if g.c == 0:
                        pe.wait_ge(kones_ok, 1)
                    scores_t(0, 0)
                    scores(1, 1)
                if past:
                    if g.c == 1 or not now:
                        pe.wait_ge(wr_in, 16)
                    pe.wait_ge(xt_ok, g.n(1))
                    for j in range(2):
                        for k in range(2):
                            last = nc.tensor.matmul(ps_c[:, NV * j:NV * j + NV], xt_grp[:, k, P * j:P * j + P],
                                                    wr_s[:, k, :], start=k == 0, stop=k == 1)
                    last.then_inc(router_done, 1)
                if now:
                    scores_t(0, 1)
                    values(0, 0)
                if later:
                    if g.c == -2:
                        pe.wait_ge(const_ok, 9)
                    pe.wait_ge(xn_ok, g.n(2, 3))
                    if g.c >= 0:
                        pe.wait_ge(kr_ok, g.n(1, 2))
                    if g.c == -1:
                        pe.wait_ge(qr_ok, 1)
                    for k in range(2):
                        for j in range(2):
                            last = nc.tensor.matmul(ps_b[:, k, P * j:P * j + P], xn[:, j, P * k:P * k + P],
                                                    ident[:, :], is_transpose=True, start=True, stop=True)
                    last.then_inc(xnt_done, 1)
                if now:
                    values(0, 1)
                    scores_t(1, 0)
                if g.c == G:
                    gate_up_1(0)
                if past:
                    pe.wait_ge(oh_ok, g.n(1))
                    if now:
                        pe.wait_ge(maxt_ok, g.n(2, 1))
                    for j in range(2):
                        nc.tensor.matmul(ps_c[:, 192 + 8 * j:200 + 8 * j], before[:, :], cnt[:, j, :],
                                         start=True, stop=False)
                        last = nc.tensor.matmul(ps_c[:, 192 + 8 * j:200 + 8 * j], ones_b[:, :], cum[:, j, :],
                                                start=False, stop=True)
                    if g.c == G:
                        nc.tensor.matmul(ps_c[:, 224:232], ones_b[:, :], cum[:, 1, :], start=True, stop=False)
                        last = nc.tensor.matmul(ps_c[:, 224:232], ones_b[:, :], cnt[:, 1, :], start=False, stop=True)
                    last.then_inc(pos_done, 1)
                if later:
                    if g.c == -2:
                        pe.wait_ge(wq_in, 16)
                    pe.wait_ge(xnt_ok, g.n(1, 3))
                    for c in range(2):
                        for k in range(2):
                            last = nc.tensor.matmul(ps_b[:, c, :], wq_s[:, k, c, :], xn_t[:, k, :],
                                                    start=k == 0, stop=k == 1)
                    last.then_inc(q_done, 1)
                if g.c == G - 2:
                    gate_up_0(0)
                if g.c == G - 1:
                    gate_up_0(2)
                if soon:
                    pe.wait_ge(qst[pn], g.turns(96, 1))
                    pe.wait_ge(kst[pn], g.turns(96, 1))
                    scores(0, 0, 1)
                if now:
                    scores_t(1, 1)
                    values(1, 0)
                if soon:
                    scores(0, 1, 1)
                if now:
                    values(1, 1)
                if g.c == G - 1:
                    gate_up_0(3)
                if later and g.c >= -1:
                    pe.wait_ge(ctx_in[g.par], g.turns(16, 2))
                    pe.wait_ge(qr_ok, g.n(1, 3))
                    second_half = keys(6, g.par, g.n(1, 3))
                    next(second_half)
                if soon:
                    max_rows(0, 1, pos_read)
                if later and g.c >= -1:
                    next(second_half)
                if g.c == G - 2:
                    gate_up_0(1)
                if g.c == -2:
                    pe.wait_ge(small_in, 32)
                    nc.tensor.matmul(ps_c[:, 0:2], ones_r[:, :], gate_r[:, :], start=True, stop=True
                                     ).then_inc(gates_done, 1)

            attention_steps(pe, body)

            for j in range(1, NJ):
                gate_up_1(j)
                if j == 1:
                    pe.wait_ge(hid_ok, NJ)
                    for t in range(CH):
                        for i in range(NJ):
                            last = nc.tensor.matmul(sums_0[t], hid_0[:, i, P * t:P * t + P], down_s[:, i, :],
                                                    start=i == 0, stop=i == NJ - 1)
                        last.then_inc(down_done, 1)
            def expert_x(t, d):
                r = (t.c + d) % 4
                pe.wait_ge(tile_in[r], t.laps(d, 1))
                if t.since(2 - d):
                    pe.wait_ge(xlo_ok, t.n(d - 1))
                for k in range(2):
                    last = nc.tensor.matmul(ps[:, r % 2, P * k:P * k + P], xs_in[:, r, P * k:P * k + P], ident[:, :],
                                            is_transpose=True, start=True, stop=True)
                last.then_inc(xst_done, 1)

            def experts_of(i, c, n):
                first = max(c - 1, 0)
                count = n + 2 if not isinstance(i, int) else min(c + n + 1, NT) - first
                at = eid_i[0:1, first:first + count] if isinstance(i, int) else eid_i[0:1, bass.ds(i * TURN + first, count)]
                e = list(nc.values_load_multi_w_load_instructions(
                    at, engines=[mybir.EngineType.PE], min_val=0, max_val=E - 1, skip_runtime_bounds_check_because=CLAMPED)[1])
                if c == 0:
                    e = [None] + e
                e.append(None)
                return [e[r:r + 3] for r in range(n)]

            pe.wait_ge(table_ok, 1)
            first_ids = experts_of(0, 0, HEAD)
            pe.wait_ge(base_ok, CH)
            for i in range(NJ):
                pe.wait_ge(hid_ok, NJ + i + 1)
                if i == NJ - 1:
                    expert_x(Tile(0, 0), 0)
                    expert_x(Tile(0, 0), 1)
                for t in range(CH):
                    last = nc.tensor.matmul(sums[t], hid_1[:, i, P * t:P * t + P], down_s[:, i, :],
                                            start=i == 0, stop=i == NJ - 1)
                    if i == NJ - 1:
                        last.then_inc(down_done, 1)

            def products(out, high, low, x_high, x_low, first, last):
                for n, (a, b) in enumerate(((high, x_high), (high, x_low), (low, x_high))):
                    ins = nc.tensor.matmul(out, a, b, start=first and n == 0,
                                           stop=last and n == 2)
                return ins

            def shared(c):
                def gate_up(j):
                    if j >= 2:
                        pe.wait_ge(prod_ok, c * NJ + (j - 1 - 2 * NJ))
                    for high, low, bank in ((gate_hi, gate_lo, j % 2), (up_hi, up_lo, 2 + j % 2)):
                        for k in range(2):
                            cols = slice(P * j, P * j + P)
                            x_high = xt_hi[:, bass.ds(c * 2 + (k - 4), 1), :].rearrange("p a t -> p (a t)")
                            last = products(ps[:, bank, :], high[:, k, cols], low[:, k, cols], x_high,
                                            xt_lo[:, k, bass.ds(c * (CH * P), CH * P)], k == 0, k == 1)
                    last.then_inc(gu_done, 1)

                def down(j):
                    pe.wait_ge(hid_ok, c * NJ + j + 1)
                    if j == 0:
                        pe.wait_ge(base_ok, c * CH)
                    for t in range(CH):
                        rows = slice(P * t, P * t + P)
                        last = products(sums[t], hid_hi[:, j, rows], hid_lo[:, j, rows], down_hi[:, j, :],
                                        down_lo[:, j, :], j == 0, j == NJ - 1)
                        if j == NJ - 1:
                            last.then_inc(down_done, 1)

                gate_up(0)
                gate_up(1)
                for j in range(NJ):
                    if j + 2 < NJ:
                        gate_up(j + 2)
                    down(j)

            pe.wait_ge(xt_out, 16 * (G + 1))
            pe.wait_ge(fc1_in, 16 * E)
            pe.wait_ge(fc2_in, 16 * E)

            pe.wait_ge(flo_ok, E)

            def expert_h(t, d, e):
                par = (t.c + d) % 2
                pe.wait_ge(xlo_ok, t.n(d + 1))
                if t.since(2 - d):
                    pe.wait_ge(act_ok, t.n(d - 1))
                for k in range(2):
                    w_high = fc1_hi[:, bass.ds(e * 2 + k, 1), :].rearrange("p a n -> p (a n)")
                    w_low = fc1_lo[:, bass.ds(e * 2 + k, 1), :].rearrange("p a n -> p (a n)")
                    last = products(ps[:, 2 + par, :], xs_hi[:, par, k, :], xs_lo[:, par, k, :], w_high, w_low,
                                    k == 0, k == 1)
                last.then_inc(h_done, 1)

            def expert_at(t, d):
                pe.wait_ge(act_ok, t.n(d + 1))
                if t.since(1 - d):
                    pe.wait_ge(actt_ok, t.n(d))
                for k in range(2):
                    last = nc.tensor.matmul(ps[:, 4, P * k:P * k + P], act[:, (t.c + d) % 2, P * k:P * k + P], ident[:, :],
                                            is_transpose=True, start=True, stop=True)
                last.then_inc(actt_done, 1)

            def expert_y(t, d, e):
                par = (t.c + d) % 2
                pe.wait_ge(actt_ok, t.n(d + 1))
                if t.since(2 - d):
                    pe.wait_ge(y_ok, t.n(d - 1))
                for k in range(2):
                    w = fc2_s[:, bass.ds(e * 2 + k, 1), :].rearrange("p a n -> p (a n)")
                    last = nc.tensor.matmul(ps[:, 5 + par, 0:D], act_t[:, par, k, :], w, start=k == 0, stop=k == 1)
                last.then_inc(y_done, 1)

            final = [None]

            def step(t, e):
                if t.c == 0:
                    expert_h(t, 0, e[1])
                    pe.wait_ge(base_ok, 2 * CH)
                else:
                    expert_at(t, -1)
                if t.c + 2 < NT:
                    expert_x(t, 2)
                if t.c + 1 < NT:
                    expert_h(t, 1, e[2])
                if t.since(1):
                    expert_y(t, -1, e[0])
                final[0] = e[1]

            expert_steps(pe, step, lambda i, c, n: first_ids if c == 0 else experts_of(i, c, n))
            expert_at(Tile(0, NT), -1)
            expert_y(Tile(0, NT), -1, final[0])

            pe.wait_ge(low_ok, 5)
            pe.wait_ge(y_ok, NT)
            with pe.Fori(2, NCH) as c:
                shared(c)


def kernel(x, ctx_768, mask_BxS_bk0, g_xattn, g_ffn, L0_xattn_Wq, L0_xattn_Wkv, L0_ffn_w_router,
           L0_ffn_fc1_w, L0_ffn_fc2_w, L0_ffn_gate_w, L0_ffn_up_w, L0_ffn_down_w):
    import numpy as np
    import concourse.bacc as bacc
    from concourse.bass_utils import run_bass_kernel_spmd

    def tiles(w, p):
        w = np.asarray(w)
        w = w.reshape(*w.shape[:-2], w.shape[-2] // p, p, w.shape[-1])
        return np.moveaxis(w, -2, 0)

    x = np.asarray(x)
    ctx_768 = np.asarray(ctx_768)
    batch, seq, d = x.shape
    cy = ctx_768.shape[2]
    kc = cy // 2
    w_q, w_kv = np.asarray(L0_xattn_Wq), np.asarray(L0_xattn_Wkv)
    fc1, fc2 = tiles(L0_ffn_fc1_w, 128), tiles(L0_ffn_fc2_w, 128)
    arrays = {
        "x": x.reshape(batch * seq, d),
        "ctx_t": ctx_768.reshape(batch * seq, 2, kc).transpose(2, 1, 0),
        "mask": np.ascontiguousarray(np.asarray(mask_BxS_bk0).T).view(np.uint32),
        "gates": np.stack([np.asarray(g_xattn), np.asarray(g_ffn)], axis=1),
        "wq": w_q.reshape(8, 2, 16, 2, 128).transpose(4, 3, 1, 2, 0).reshape(128, 2, 2, 128),
        "wk": w_kv[:d].reshape(8, 2, 16, 2, kc).transpose(4, 3, 1, 2, 0).reshape(kc, 2, 2, 128),
        "wv": w_kv[d:].reshape(d, 2, kc).transpose(2, 1, 0),
        "w_router": tiles(L0_ffn_w_router, 128),
        "fc1": fc1.reshape(128, -1, fc1.shape[-1]),
        "fc2": fc2.reshape(128, -1, fc2.shape[-1]),
        "gate_w": tiles(L0_ffn_gate_w, 128),
        "up_w": tiles(L0_ffn_up_w, 128),
        "down_w": tiles(L0_ffn_down_w, 128),
    }
    arrays = {f"in_{n}": np.ascontiguousarray(a) for n, a in arrays.items()}
    nc = bacc.Bacc("TRN2", target_bir_lowering=False, num_devices=1)
    args = [nc.dram_tensor(n, a.shape, mybir.dt.from_np(a.dtype), kind="ExternalInput").ap()
            for n, a in arrays.items()]
    out = nc.dram_tensor("out", (batch * seq, d), F32, kind="ExternalOutput").ap()
    build_program(nc, *args, out)
    r = run_bass_kernel_spmd(nc, [arrays], core_ids=[0])
    return r.results[0]["out"].reshape(batch, seq, d)
```
